# Optimizing a Trainium2 kernel written in Bass

```python
import numpy as np
import jax
import jax.numpy as jnp

def _softmax(x, axis=-1):
    return jax.nn.softmax(x, axis=axis)

def _gelu(x):
    return jax.nn.gelu(x, approximate=True)

def _silu(x):
    return jax.nn.silu(x)

def _sigmoid(x):
    return jax.nn.sigmoid(x)

def _layernorm(x, axis=-1, eps=1e-05):
    m = jnp.mean(x, axis=axis, keepdims=True)
    v = jnp.var(x, axis=axis, keepdims=True)
    return (x - m) / jnp.sqrt(v + eps)

def _scatter_add(tgt, idx, src, axis=0):
    return tgt.at[idx].add(src)

def _segment_sum(src, seg, n):
    return jax.ops.segment_sum(src, seg, n)
kernel_name = 'mk_gnn_preln_d2_gnn_r8_4eccff'

def setup_inputs(seed: int=0):
    np.random.seed(seed)
    _w = jnp.asarray

    def _rec_inputs():
        import jax
        import jax.numpy as jnp
        _gk = jax.random.key(seed)
        x = -0.0002117 + 1 * jax.random.normal(jax.random.fold_in(_gk, 1), (12500, 256), jnp.float32)
        src = jax.random.randint(jax.random.fold_in(_gk, 2), (200000,), 0, 12500, jnp.int32)
        dst = jnp.minimum((12500 * jax.random.uniform(jax.random.fold_in(_gk, 3), (200000,)) ** 2.0).astype(jnp.int32), 99999)
        _o = jnp.argsort(dst, stable=True)
        src = src[_o]
        dst = dst[_o]
        return (x, src, dst)
    x, src, dst = _rec_inputs()

    def _L0_gnn_setup():
        import jax, jax.numpy as jnp
        import numpy as np
        N_NODES = 12500
        N_EDGES = 200000
        D_IN = 256
        D_OUT = 256
        key = jax.random.key(seed)
        k1, k2, k3, k4, k5 = jax.random.split(key, 5)
        feat = jax.random.normal(k1, (N_NODES, D_IN), dtype=jnp.float32)
        lim = float(np.sqrt(6.0 / (D_IN + D_OUT)))
        W_neigh = jax.random.uniform(k2, (D_OUT, D_IN), minval=-lim, maxval=lim, dtype=jnp.float32)
        W_self = jax.random.uniform(k3, (D_OUT, D_IN), minval=-lim, maxval=lim, dtype=jnp.float32)
        b_self = jnp.zeros((D_OUT,), dtype=jnp.float32)
        src = jax.random.randint(k4, (N_EDGES,), 0, N_NODES, dtype=jnp.int32)
        dst = jax.random.randint(k5, (N_EDGES,), 0, N_NODES, dtype=jnp.int32)
        return {'feat': feat, 'W_neigh': W_neigh, 'W_self': W_self, 'b_self': b_self, 'src': src, 'dst': dst}
    _L0_gnn_all = _L0_gnn_setup()
    _L0_gnn_in = {k: v for k, v in _L0_gnn_all.items() if k in ('W_neigh', 'W_self', 'b_self')}
    del _L0_gnn_all

    def _L1_gnn_setup():
        import jax, jax.numpy as jnp
        import numpy as np
        N_NODES = 1250
        N_EDGES = 40000
        FEA = 256
        HID = 256
        HEADS = 4
        ODIM = HID // HEADS
        NEG_SLOPE = 0.2

        def _gat_layer(x, W, al, ar, b, src, dst):
            n = x.shape[0]
            z = (x @ W).reshape(n, HEADS, ODIM)
            el = jnp.sum(z * al, axis=-1)
            er = jnp.sum(z * ar, axis=-1)
            e = jax.nn.leaky_relu(el[src] + er[dst], negative_slope=NEG_SLOPE)
            e_max = jax.ops.segment_max(e, dst, num_segments=n)
            ex = jnp.exp(e - e_max[dst])
            denom = jax.ops.segment_sum(ex, dst, num_segments=n)
            alpha = ex / denom[dst]
            msg = z[src] * alpha[:, :, None]
            out = jax.ops.segment_sum(msg, dst, num_segments=n)
            out = out + x.reshape(n, HEADS, ODIM)
            out = out + b.reshape(HEADS, ODIM)
            out = jax.nn.elu(out)
            return out.reshape(n, HID)
        key = jax.random.key(seed)
        ks = jax.random.split(key, 12)
        inp = {'features': jax.random.normal(ks[0], (N_NODES, FEA), dtype=jnp.float32), 'src': jax.random.randint(ks[1], (N_EDGES,), 0, N_NODES, dtype=jnp.int32), 'dst': jax.random.randint(ks[2], (N_EDGES,), 0, N_NODES, dtype=jnp.int32), 'W0': jax.random.normal(ks[3], (FEA, HID), dtype=jnp.float32) * (1.0 / np.sqrt(FEA)), 'al0': jax.random.normal(ks[4], (HEADS, ODIM), dtype=jnp.float32) * 0.1, 'ar0': jax.random.normal(ks[5], (HEADS, ODIM), dtype=jnp.float32) * 0.1, 'b0': jnp.zeros((HID,), dtype=jnp.float32), 'W1': jax.random.normal(ks[6], (HID, HID), dtype=jnp.float32) * (1.0 / np.sqrt(HID)), 'al1': jax.random.normal(ks[7], (HEADS, ODIM), dtype=jnp.float32) * 0.1, 'ar1': jax.random.normal(ks[8], (HEADS, ODIM), dtype=jnp.float32) * 0.1, 'b1': jnp.zeros((HID,), dtype=jnp.float32)}
        return inp
    _L1_gnn_all = _L1_gnn_setup()
    _L1_gnn_in = {k: v for k, v in _L1_gnn_all.items() if k in ('W0', 'al0', 'ar0', 'b0', 'W1', 'al1', 'ar1', 'b1')}
    del _L1_gnn_all
    return {'x': x, 'src': src, 'dst': dst, 'L0_gnn_W_neigh': _L0_gnn_in['W_neigh'], 'L0_gnn_W_self': _L0_gnn_in['W_self'], 'L0_gnn_b_self': _L0_gnn_in['b_self'], 'L1_gnn_W0': _L1_gnn_in['W0'], 'L1_gnn_al0': _L1_gnn_in['al0'], 'L1_gnn_ar0': _L1_gnn_in['ar0'], 'L1_gnn_b0': _L1_gnn_in['b0'], 'L1_gnn_W1': _L1_gnn_in['W1'], 'L1_gnn_al1': _L1_gnn_in['al1'], 'L1_gnn_ar1': _L1_gnn_in['ar1'], 'L1_gnn_b1': _L1_gnn_in['b1']}

def reference(x, src, dst, L0_gnn_W_neigh, L0_gnn_W_self, L0_gnn_b_self, L1_gnn_W0, L1_gnn_al0, L1_gnn_ar0, L1_gnn_b0, L1_gnn_W1, L1_gnn_al1, L1_gnn_ar1, L1_gnn_b1):
    import jax
    import jax.numpy as jnp

    def _L0_gnn_ref(feat, W_neigh, W_self, b_self, src, dst):
        import jax, jax.numpy as jnp
        import numpy as np
        N_NODES = 12500
        N_EDGES = 200000
        D_IN = 256
        D_OUT = 256
        msgs = feat[src]
        neigh_sum = jax.ops.segment_sum(msgs, dst, num_segments=N_NODES)
        deg = jax.ops.segment_sum(jnp.ones((src.shape[0],), dtype=feat.dtype), dst, num_segments=N_NODES)
        h_neigh = neigh_sum / jnp.maximum(deg, 1.0)[:, None]
        h_neigh = h_neigh @ W_neigh.T
        h_self = feat @ W_self.T + b_self
        return h_self + h_neigh

    def _L1_gnn_ref(features, src, dst, W0, al0, ar0, b0, W1, al1, ar1, b1):
        import jax, jax.numpy as jnp
        import numpy as np
        N_NODES = 1250
        N_EDGES = 40000
        FEA = 256
        HID = 256
        HEADS = 4
        ODIM = HID // HEADS
        NEG_SLOPE = 0.2

        def _gat_layer(x, W, al, ar, b, src, dst):
            n = x.shape[0]
            z = (x @ W).reshape(n, HEADS, ODIM)
            el = jnp.sum(z * al, axis=-1)
            er = jnp.sum(z * ar, axis=-1)
            e = jax.nn.leaky_relu(el[src] + er[dst], negative_slope=NEG_SLOPE)
            e_max = jax.ops.segment_max(e, dst, num_segments=n)
            ex = jnp.exp(e - e_max[dst])
            denom = jax.ops.segment_sum(ex, dst, num_segments=n)
            alpha = ex / denom[dst]
            msg = z[src] * alpha[:, :, None]
            out = jax.ops.segment_sum(msg, dst, num_segments=n)
            out = out + x.reshape(n, HEADS, ODIM)
            out = out + b.reshape(HEADS, ODIM)
            out = jax.nn.elu(out)
            return out.reshape(n, HID)
        x = _gat_layer(features, W0, al0, ar0, b0, src, dst)
        x = _gat_layer(x, W1, al1, ar1, b1, src, dst)
        return x
    h = jnp.maximum(_layernorm(x, axis=-1), 0.0)
    x = x + _L0_gnn_ref(h, L0_gnn_W_neigh, L0_gnn_W_self, L0_gnn_b_self, src, dst)
    h = jnp.maximum(_layernorm(x, axis=-1), 0.0)
    x = x + _L1_gnn_ref(h, src, dst, L1_gnn_W0, L1_gnn_al0, L1_gnn_ar0, L1_gnn_b0, L1_gnn_W1, L1_gnn_al1, L1_gnn_ar1, L1_gnn_b1)
    return x

_drawn_inputs = setup_inputs


def setup_inputs(seed=0):
    import zlib

    import numpy as np

    out = dict(_drawn_inputs(seed))
    spreads = {'L0_gnn_b_self': (0.0, 0.1), 'L1_gnn_b0': (0.0, 0.1), 'L1_gnn_b1': (0.0, 0.1)}
    factors = {'L1_gnn_ar0': 6.761, 'L1_gnn_al1': 2.867, 'L1_gnn_ar1': 7.939}
    for name, (base, spread) in spreads.items():
        noise = np.random.default_rng([zlib.crc32(name.encode()), seed]).standard_normal(out[name].shape)
        drawn = base * np.exp(spread * noise) if base else spread * noise
        out[name] = jnp.asarray(drawn.astype(out[name].dtype))
    for name, factor in factors.items():
        out[name] = (out[name] * factor).astype(out[name].dtype)
    return out
```

```python
from contextlib import ExitStack

import concourse.bass as bass
from concourse import mybir

F32 = mybir.dt.float32
I32 = mybir.dt.int32
ACT = mybir.ActivationFunctionType
ALU = mybir.AluOpType
AX = mybir.AxisListType

P = 128
NODES, D, EDGES = 12500, 256, 200000
HEADS, HD = 4, 64
NT = -(-NODES // P)
NPAD = NT * P
LAST_ROWS = NODES - (NT - 1) * P
CT = 16
CE = CT * P
SLOTS = 3
NCH = -(-EDGES // (CE * SLOTS)) * SLOTS
ITER = NCH // SLOTS
EPAD = NCH * CE
QUADS, QT = 4, 4
QE = QT * P
ROWS = HEADS * CT
WIN = 2 * P
AW = HEADS * (HD + 1)
ROW = AW + 2 * HEADS
ACC_TILES = NT + 2
GROUP, HALF = 14, 7
NG = NT // GROUP
SB = 3
SLOPE = 0.2
LN_EPS = 1e-5
NEG = -1e30
PAD_NODE = NPAD - 1
NOWHERE = EPAD

assert NT == NG * GROUP and NCH <= P and PAD_NODE >= NODES


def gnn_kernel(nc, x, src, dst, w_neigh, w_self, b_self,
               w0, al0, ar0, b0, w1, al1, ar1, b1, out):
    ctx = ExitStack()
    with ctx:
        def sb(name, shape, dt=F32):
            return ctx.enter_context(nc.sbuf_tensor(name, shape, dt))

        def pb(name, shape):
            return ctx.enter_context(nc.psum_tensor(name, shape, F32))

        def sem(name):
            return ctx.enter_context(nc.semaphore(name))

        shared = {}

        def stage_sem(name):
            if name not in shared:
                shared[name] = sem(name)
            return shared[name]

        def clear_stage_sems():
            with nc.Block() as block:
                @block.sync
                def _(sp):
                    for handle in shared.values():
                        sp.sem_clear(handle)

        def dram(name, shape, dt=F32):
            return nc.dram_tensor(name, shape, dt, kind="Internal").ap()

        h0_tab = dram("h0_tab", (NPAD, D))
        z_tab = dram("z_tab", (NPAD, ROW))
        x1_tab = dram("x1_tab", (NPAD, D))
        hin_tab = dram("hin_tab", (NPAD, D))
        er_start = dram("er_start", (EPAD, HEADS))
        er_rows = dram("er_rows", (NCH, HEADS, CE))
        pen_rows = dram("pen_rows", (NCH, HEADS, CT, P + 2))
        same_tab = dram("same_tab", (NCH, CE))
        chain_tab = dram("chain_tab", (NCH, 2 * CT))
        base_tab = dram("base_tab", (NCH, QUADS), I32)

        acc = sb("acc", [P, ACC_TILES * AW])
        slots = sb("slots", [P, SLOTS, CT, ROW])
        onehot = sb("onehot", [P, SB, QT, WIN])
        src_t = sb("src_t", [P, NCH * CT], I32)
        negrel = sb("negrel", [P, NCH * CT])
        idx = sb("idx", [P, SLOTS, CT], I32)
        base_row = sb("base_row", [1, NCH * QUADS], I32)
        rounds_i = sb("rounds_i", [1, 1], I32)
        first_dst = sb("first_dst", [NCH, 1], I32)
        seg_pos = sb("seg_pos", [P, NT], I32)
        ident = sb("ident", [P, P])
        ones = sb("ones", [P, P])
        before = sb("before", [P, P])
        lanes = sb("lanes", [P, WIN])
        tile_mask = sb("tile_mask", [ROWS, CT])
        head_mask = sb("head_mask", [ROWS, HEADS])
        head_rows = sb("head_rows", [HEADS, ROWS])
        first_rows = sb("first_rows", [ROWS, HEADS])
        one_c = sb("one_c", [P, 1])
        eps_c = sb("eps_c", [P, 1])
        wsT = sb("wsT", [P, 2, D])
        wnT = sb("wnT", [P, 2, D])
        wz = [sb(f"wz{i}", [P, 2, D + 2 * HEADS]) for i in range(2)]
        attn = [sb(f"attn{i}", [P, 2, 2 * HEADS]) for i in range(2)]
        bias = [sb(f"bias{i}", [P, D]) for i in range(3)]
        pen = sb("pen", [ROWS, SLOTS, P + 2])
        er = sb("er", [ROWS, SLOTS, P])
        chain_pen = sb("chain_pen", [HEADS, SLOTS, 2 * CT])
        el_cols = sb("el_cols", [P, ROWS])
        scan_f = sb("scan_f", [ROWS, P])
        scan_b = sb("scan_b", [ROWS, P])
        ends = sb("ends", [ROWS, 2, CT])
        carry = sb("carry", [HEADS, 2 * CT + 4])
        scrap = sb("scrap", [ROWS, 2, CT])
        edge_in = sb("edge_in", [ROWS, 2])
        logit = sb("logit", [ROWS, 2, P])
        old = sb("old", [ROWS, 2])
        wexp = sb("wexp", [ROWS, P + 1])
        wrow = sb("wrow", [ROWS, P + 1])
        rm1 = sb("rm1", [1, HEADS])
        rescale = sb("rescale", [P, HEADS])
        mv = sb("mv", [P, NT, 2])
        stats = sb("stats", [P, GROUP, 6])
        mvg = sb("mvg", [P, GROUP, 2])
        rstd = sb("rstd", [P, NT])
        nbias = sb("nbias", [P, NT])
        deg_inv = sb("deg_inv", [P, NT])
        deg = sb("deg", [P, NT])
        er_stage = sb("er_stage", [P, GROUP, HEADS])
        pos_stage = sb("pos_stage", [P, GROUP], I32)
        er_init = sb("er_init", [NCH, ROW])

        flat = slots[:, :, :, :].rearrange("p a b c -> p (a b c)")
        H = HALF * D
        in_a = flat[:, 0:2 * H].rearrange("p (s t d) -> p s t d", s=2, t=HALF)
        in_b = flat[:, 2 * H:4 * H].rearrange("p (s t d) -> p s t d", s=2, t=HALF)
        z_out = flat[:, 4 * H:4 * H + 2 * HALF * ROW].rearrange("p (s t d) -> p s t d", s=2, t=HALF)
        hot = onehot[:, :, :, :].rearrange("p a b c -> p (a b c)")
        lhs = hot[:, 0:1024].rearrange("p (s c) -> p s c", s=2)
        tmp_a = hot[:, 1024:1536].rearrange("p (s c) -> p s c", s=2)
        tmp_b = hot[:, 1536:2048].rearrange("p (s c) -> p s c", s=2)
        accf = acc[:, :]

        def acc_cols(tile, lo, n):
            return accf[:, bass.ds(tile * AW + lo, n)]

        pair = [pb(f"pair{i}", [P, 2, 512]) for i in range(2)]
        ps_x = pb("ps_x", [P, 512])
        ps_w = pb("ps_w", [P, 512])
        ps_c = pb("ps_c", [P, 512])
        ps_d = pb("ps_d", [P, 512])

        pool_turn = sem("pool_turn")
        dve_turn = sem("dve_turn")
        pe_turn = sem("pe_turn")

        s_masks = sem("s_masks")
        s_wload = sem("s_wload")
        s_wzero = sem("s_wzero")
        raw = [in_a[:, i, :, :].rearrange("p t d -> p (t d)")[:, 0:2 * D]
               .rearrange("p (c d) -> p c d", c=2) for i in range(2)]
        wT = in_b[:, 0, :, :].rearrange("p t d -> p (t d)")[:, 0:2 * D].rearrange("p (c d) -> p c d", c=2)
        lane_i = in_b[:, 1, 0, :].bitcast(I32)
        with nc.Block() as block:
            @block.gpsimd
            def _(pool):
                pool.memset(ident[:, :], 0.0)
                pool.memset(before[:, :], 1.0)
                pool.memset(ones[:, :], 1.0)
                pool.memset(one_c[:, :], 1.0)
                pool.memset(eps_c[:, :], LN_EPS)
                pool.iota(lane_i, [[1, WIN]], base=0, channel_multiplier=0).then_inc(s_masks, 1)
                pool.wait_ge(s_masks, 1)
                pool.affine_select(out=ident[:, :], in_=ident[:, :], compare_op=ALU.not_equal, fill=1.0,
                                   base=0, pattern=[[-1, P]], channel_multiplier=1)
                pool.affine_select(out=before[:, :], in_=before[:, :], compare_op=ALU.is_gt, fill=0.0,
                                   base=0, pattern=[[1, P]], channel_multiplier=-1)
                pool.tensor_copy(lanes[:, :], lane_i)

            @block.vector
            def _(dve):
                nc.vector.memset(attn[0][:, :, :], 0.0).then_inc(s_wzero, 1)
                nc.vector.memset(attn[1][:, :, :], 0.0).then_inc(s_wzero, 1)

            @block.sync
            def _(sp):
                n = 0
                for w, to in ((w_self, raw[0]), (w_neigh, raw[1]),
                              (w0, wz[0][:, :, 0:D]), (w1, wz[1][:, :, 0:D])):
                    sp.dma_start(to, w.rearrange("(c p) d -> p c d", p=P)).then_inc(s_wload, 16)
                    n += 16
                for i, b in enumerate((b_self, b0, b1)):
                    sp.dma_start(bias[i][:, :], b.unsqueeze(0).broadcast_to([P, D])).then_inc(s_wload, 16)
                    n += 16
                sp.wait_ge(s_wzero, 2)
                with nc.allow_non_contiguous_dma(reason="columns of the attention vectors, once"):
                    for i, pairs in enumerate(((al0, ar0), (al1, ar1))):
                        for j, a in enumerate(pairs):
                            for h in range(HEADS):
                                lo = (h % 2) * HD
                                c = j * HEADS + h
                                sp.dma_start(attn[i][lo:lo + HD, h // 2, c:c + 1],
                                             a[h, :].unsqueeze(1)).then_inc(s_wload, 16)
                                n += 16
                sp.wait_ge(s_wload, n)

        s_mk = sem("s_mk")
        s_wt = sem("s_wt")
        s_wc = sem("s_wc")
        s_wv = sem("s_wv")
        jobs = [("T", raw[0], wsT), ("T", raw[1], wnT), ("Z", wz[0], 0), ("Z", wz[1], 1)]
        with nc.Block() as block:
            @block.vector
            def _(dve):
                sq = ident[0:ROWS, 0:ROWS]
                nc.vector.tensor_reduce(out=tile_mask[:, :], in_=sq.rearrange("p (h t) -> p t h", h=HEADS),
                                        axis=AX.X, op=ALU.add)
                nc.vector.tensor_reduce(out=head_mask[:, :], in_=sq.rearrange("p (h t) -> p h t", h=HEADS),
                                        axis=AX.X, op=ALU.add)
                nc.vector.tensor_copy(head_rows[:, :].rearrange("p (h t) -> p h t", h=HEADS),
                                      ident[0:HEADS, 0:HEADS].unsqueeze(2).broadcast_to([HEADS, HEADS, CT]))
                nc.vector.tensor_copy(first_rows[:, :],
                                      sq.rearrange("p (h t) -> p h t", h=HEADS)[:, :, 0])
                for n, (kind, _, to) in enumerate(jobs):
                    dve.wait_ge(s_wt, n + 1)
                    if n >= 3:
                        dve.wait_ge(s_wv, n - 2)
                    view = (to if kind == "T" else wT)[:, :, :]
                    nc.vector.tensor_copy(view.rearrange("p c d -> p (c d)"), ps_x[:, :]).then_inc(s_wc, 1)
                    if kind == "Z":
                        dve.wait_ge(s_wv, to + 1)
                        nc.vector.tensor_copy(wz[to][:, :, D:D + 2 * HEADS],
                                              ps_w[:, 0:16].rearrange("p (c a) -> p c a", c=2)).then_inc(s_mk, 1)

            @block.tensor
            def _(pe):
                for n, (kind, w, to) in enumerate(jobs):
                    if n:
                        pe.wait_ge(s_wc, n)
                    for a in range(2):
                        for b in range(2):
                            last = nc.tensor.transpose(ps_x[:, b * D + a * P:b * D + a * P + P],
                                                       w[:, a, b * P:b * P + P], ident[:, :])
                    last.then_inc(s_wt, 1)
                    if kind == "Z":
                        pe.wait_ge(s_wc, n + 1)
                        if to:
                            pe.wait_ge(s_mk, to)
                        for a in range(2):
                            for b in range(2):
                                last = nc.tensor.matmul(ps_w[:, a * 8:a * 8 + 8], wT[:, b, a * P:a * P + P],
                                                        attn[to][:, b, :], start=(b == 0), stop=(b == 1))
                        last.then_inc(s_wv, 1)

        cols = [0]

        def edge_buf(n, dt=F32):
            v = accf[0:NCH, cols[0]:cols[0] + n]
            cols[0] += n
            return v if dt is F32 else v.bitcast(dt)

        d_i = edge_buf(CE + 2, I32)
        s_i = edge_buf(CE, I32)
        d_f = edge_buf(CE + 2)
        s_f = edge_buf(CE)
        start_f = edge_buf(CE + 1)
        pen_f = edge_buf(CE + 1)
        same_f = edge_buf(CE)
        ch_f = edge_buf(2 * CT)
        b_first = edge_buf(QUADS, I32)
        b_last = edge_buf(QUADS, I32)
        span_i = edge_buf(QUADS, I32)
        span_f = edge_buf(QUADS)
        span_m = edge_buf(1)
        whole, rest = EDGES // CE, EDGES % CE
        s_pad = sem("s_pad")
        s_eload = sem("s_eload")
        s_ev = sem("s_ev")
        s_estore = sem("s_estore")
        zero_view = accf[:, 16384:16384 + CE * HEADS * NCH // P]
        with nc.Block() as block:
            @block.vector
            def _(dve):
                nc.vector.memset(d_i, PAD_NODE).then_inc(s_pad, 1)
                nc.vector.memset(s_i, 0).then_inc(s_pad, 1)
                nc.vector.memset(zero_view, 0.0).then_inc(s_pad, 1)
                dve.wait_ge(s_pad, 1)
                nc.vector.memset(d_i[0:1, 0:1], -1).then_inc(s_pad, 1)

            @block.sync
            def _(sp):
                sp.wait_ge(s_pad, 4)
                rows = bass.AP(tensor=dst.tensor, offset=CE - 1, ap=[[CE, whole - 1], [1, CE + 2]])
                sp.dma_start(d_i[1:whole, :], rows).then_inc(s_eload, 16)
                sp.dma_start(d_i[0:1, 1:CE + 2], dst[0:CE + 1].unsqueeze(0)).then_inc(s_eload, 16)
                sp.dma_start(d_i[whole:whole + 1, 0:rest + 1],
                             dst[whole * CE - 1:EDGES].unsqueeze(0)).then_inc(s_eload, 16)
                sp.dma_start(s_i[0:whole, :], src[0:whole * CE].rearrange("(c e) -> c e", e=CE)).then_inc(s_eload, 16)
                sp.dma_start(s_i[whole:whole + 1, 0:rest], src[whole * CE:EDGES].unsqueeze(0)).then_inc(s_eload, 16)
                sp.dma_start(er_start.rearrange("(p e) h -> p (e h)", p=P), zero_view).then_inc(s_eload, 16)
                sp.wait_ge(s_eload, 96)

        with nc.Block() as block:
            @block.vector
            def _(dve):
                V = nc.vector
                step = [0]

                def then(ins):
                    step[0] += 1
                    ins.then_inc(s_ev, 1)
                    dve.wait_ge(s_ev, step[0])

                V.tensor_copy(s_f, s_i)
                V.tensor_single_scalar(b_first, d_i[:, 1:1 + CE:QE], 7, op=ALU.logical_shift_right)
                V.tensor_single_scalar(b_last, d_i[:, QE:CE + 1:QE], 7, op=ALU.logical_shift_right)
                V.tensor_copy(first_dst[:, :], d_i[:, 1:2])
                then(V.tensor_copy(d_f, d_i))
                then(V.tensor_tensor(start_f, d_f[:, 0:CE + 1], d_f[:, 1:CE + 2], ALU.not_equal))
                V.tensor_scalar(pen_f, start_f, NEG, None, ALU.mult)
                V.tensor_scalar(same_f, start_f[:, 0:CE], -1.0, 1.0, ALU.mult, ALU.add)
                V.tensor_tensor(ch_f[:, 0:CT], d_f[:, P:CE + 1:P], d_f[:, 0:CE:P], ALU.not_equal)
                then(V.tensor_tensor(ch_f[:, CT:2 * CT], d_f[:, 1:CE + 1:P], d_f[:, P + 1:CE + 2:P], ALU.not_equal))
                V.tensor_scalar(ch_f, ch_f, NEG, None, ALU.mult)
                then(V.tensor_tensor(span_i, b_last, b_first, ALU.subtract))
                then(V.tensor_copy(span_f, span_i))
                V.tensor_reduce(out=span_m, in_=span_f, axis=AX.X, op=ALU.max)

        s_e2 = sem("s_e2")
        s_eT = sem("s_eT")
        s_sT = sem("s_sT")
        s_dT = sem("s_dT")
        s_sp = sem("s_sp")
        with nc.Block() as block:
            @block.sync
            def _(sp):
                pv = pen_f[:, 0:CE].rearrange("c (t p) -> c t p", p=P)
                n = 0
                for h in range(HEADS):
                    sp.dma_start(pen_rows[:, h, :, 0:P], pv).then_inc(s_estore, 16)
                    with nc.allow_non_contiguous_dma(reason="a column per tile, once"):
                        for col in (P, P + 1):
                            sp.dma_start(pen_rows[:, h, :, col:col + 1],
                                         pen_f[:, P:CE + 1:P].unsqueeze(2)).then_inc(s_estore, 16)
                    n += 48
                sp.dma_start(same_tab, same_f).then_inc(s_estore, 16)
                sp.dma_start(chain_tab, ch_f).then_inc(s_estore, 16)
                sp.dma_start(base_tab, b_first).then_inc(s_estore, 16)
                sp.wait_ge(s_estore, n + 48)
                row = base_tab.rearrange("c q -> (c q)").unsqueeze(0)
                sp.dma_start(base_row[:, :], row).then_inc(s_e2, 16)
                sp.dma_start(in_a[:, 0, 0:2, :].rearrange("p t d -> p (t d)")[:, 0:NCH * QUADS].bitcast(I32),
                             row.broadcast_to([P, NCH * QUADS])).then_inc(s_e2, 16)
                sp.wait_ge(s_e2, 32)

            @block.tensor
            def _(pe):
                banks = [pair[0], pair[1]]
                for j in range(2 * CT):
                    t = j // 2
                    buf = (s_f, d_f)[j % 2]
                    lo = t * P + (j % 2)
                    if j >= 2:
                        pe.wait_ge((s_sT, s_dT)[j % 2], j // 2)
                    nc.tensor.transpose(banks[j % 2][:, 0, 0:NCH], buf[:, lo:lo + P],
                                        ident[0:NCH, 0:NCH]).then_inc(s_eT, 1)
                nc.tensor.transpose(ps_x[0:1, 0:NCH], span_m, ident[0:NCH, 0:NCH]).then_inc(s_eT, 1)

            @block.vector
            def _(dve):
                V = nc.vector
                for j in range(2 * CT):
                    dve.wait_ge(s_eT, j + 1)
                    to, done = ((src_t, s_sT), (negrel, s_dT))[j % 2]
                    V.tensor_copy(to[:, :].rearrange("p (c t) -> p c t", t=CT)[:, :, j // 2],
                                  pair[j % 2][:, 0, 0:NCH]).then_inc(done, 1)
                dve.wait_ge(s_eT, 2 * CT + 1)
                V.tensor_reduce(out=old[0:1, 0:1], in_=ps_x[0:1, 0:NCH], axis=AX.X, op=ALU.max).then_inc(s_sp, 1)
                dve.wait_ge(s_sp, 1)
                V.tensor_copy(rounds_i[:, :], old[0:1, 0:1]).then_inc(s_sp, 1)
                dve.wait_ge(s_sp, 2)
                V.tensor_single_scalar(rounds_i[:, :], rounds_i[:, :], 1, op=ALU.logical_shift_right).then_inc(s_sp, 1)
                dve.wait_ge(s_sp, 3)
                V.tensor_copy(old[0:1, 0:1], rounds_i[:, :]).then_inc(s_sp, 1)
                dve.wait_ge(s_sp, 4)
                V.tensor_scalar(rounds_i[:, :], old[0:1, 0:1], 1.0, None, ALU.add).then_inc(s_sp, 1)
                base_b = in_a[:, 0, 0:2, :].rearrange("p t d -> p (t d)")[:, 0:NCH * QUADS]
                base_f = in_a[:, 1, 0:2, :].rearrange("p t d -> p (t d)")[:, 0:NCH * QUADS]
                dve.wait_ge(s_e2, 32)
                V.tensor_copy(base_f, base_b.bitcast(I32)).then_inc(s_sp, 1)
                dve.wait_ge(s_sp, 6)
                V.tensor_scalar(base_f, base_f, float(P), None, ALU.mult).then_inc(s_sp, 1)
                dve.wait_ge(s_sp, 7)
                dve.wait_ge(s_dT, CT)
                rel = negrel[:, :].rearrange("p (q t) -> p q t", t=QT)
                V.tensor_tensor(rel, base_f.unsqueeze(2).broadcast_to([P, NCH * QUADS, QT]), rel,
                                ALU.subtract).then_inc(s_sp, 1)

        def half_load(sp, tab, buf, g, half, done, rows_limit):
            if rows_limit:
                full = (NT - HALF) * P
                n = (HALF - 1) * P
                sp.dma_start(buf[:, half, 0:HALF - 1, :],
                             tab[full:full + n, :].rearrange("(t p) d -> p t d", p=P)).then_inc(done, 16)
                sp.dma_start(buf[0:LAST_ROWS, half, HALF - 1, :], tab[full + n:NODES, :]).then_inc(done, 16)
            else:
                v = tab[bass.ds((g * 2 + half) * HALF * P, HALF * P), :]
                sp.dma_start(buf[:, half, :, :], v.rearrange("(t p) d -> p t d", p=P)).then_inc(done, 16)

        def store_rows(tab, g, half):
            return tab[bass.ds((g * 2 + half) * HALF * P, HALF * P), :].rearrange("(t p) d -> p t d", p=P)

        s_x = [sem(f"s_xload{i}") for i in range(2)]
        s_xz = sem("s_xz")
        s_h0 = [sem(f"s_h0out{i}") for i in range(2)]
        s_bn = sem("s_bn")
        s_agg = sem("s_agg")
        s_std = sem("s_std")
        s_rs = sem("s_rs")
        s_relu = sem("s_relu")
        with nc.Block() as block:
            @block.gpsimd
            def _(pool):
                pool.memset(in_a[:, :, :, :], 0.0).then_inc(s_xz, 1)

            @block.sync
            def _(sp):
                sp.wait_ge(s_xz, 1)

                def load(g, half, last=False):
                    half_load(sp, x, in_a, g, half, s_x[half], last)

                def store(g, half):
                    sp.wait_ge(s_relu, g * GROUP + half * HALF + HALF)
                    sp.dma_start(store_rows(h0_tab, g, half), in_b[:, half, :, :]).then_inc(s_h0[half], 16)

                load(0, 0)
                load(0, 1)
                with sp.Fori(0, NG - 2) as g:
                    for half in range(2):
                        store(g, half)
                        load(g + 1, half)
                store(NG - 2, 0)
                load(NG - 1, 0)
                store(NG - 2, 1)
                load(NG - 1, 1, last=True)
                store(NG - 1, 0)
                store(NG - 1, 1)
                sp.wait_ge(s_h0[0], 16 * NG)
                sp.wait_ge(s_h0[1], 16 * NG)

            @block.vector
            def _(dve):
                V = nc.vector

                def half_stats(g, half, last=False):
                    t0 = half * HALF
                    dve.wait_ge(s_x[half], 16 * g + 16 + (16 if last else 0))
                    for j in range(HALF):
                        V.bn_stats(stats[:, t0 + j, :], in_a[:, half, j, :]).then_inc(s_bn, 1)
                    dve.wait_ge(s_bn, g * GROUP + t0 + HALF)
                    dve.sem_inc(dve_turn, 1)
                    for j in range(HALF):
                        V.bn_aggr(mvg[:, t0 + j, :], stats[:, t0 + j, :]).then_inc(s_agg, 1)
                    dve.wait_ge(s_std, g * 2 + half + 1)
                    V.reciprocal(rstd[:, t0:t0 + HALF], rstd[:, t0:t0 + HALF]).then_inc(s_rs, 1)
                    dve.wait_ge(s_rs, g * 4 + half * 2 + 1)
                    V.scalar_tensor_tensor(out=nbias[:, t0:t0 + HALF], in0=mvg[:, t0:t0 + HALF, 0], scalar=-1.0,
                                           in1=rstd[:, t0:t0 + HALF], op0=ALU.mult, op1=ALU.mult).then_inc(s_rs, 1)

                half_stats(0, 0)
                half_stats(0, 1)
                with dve.Fori(1, NG - 1) as g:
                    for half in range(2):
                        half_stats(g, half)
                half_stats(NG - 1, 0)
                half_stats(NG - 1, 1, last=True)

            @block.scalar
            def _(act):
                def half_relu(g, half, wait_store):
                    t0 = half * HALF
                    act.wait_ge(s_agg, g * GROUP + t0 + HALF)
                    nc.scalar.activation(rstd[:, t0:t0 + HALF], mvg[:, t0:t0 + HALF, 1], ACT.Sqrt,
                                         bias=eps_c[:, 0:1]).then_inc(s_std, 1)
                    act.wait_ge(s_rs, g * 4 + half * 2 + 2)
                    if wait_store:
                        act.wait_ge(s_h0[half], 16 * g)
                    for j in range(HALF):
                        nc.scalar.activation(in_b[:, half, j, :], in_a[:, half, j, :], ACT.Relu,
                                             bias=nbias[:, t0 + j:t0 + j + 1],
                                             scale=rstd[:, t0 + j:t0 + j + 1]).then_inc(s_relu, 1)

                for half in range(2):
                    half_relu(0, half, False)
                with act.Fori(1, NG) as g:
                    for half in range(2):
                        half_relu(g, half, True)

        rounds = nc.values_load(rounds_i[0:1, 0:1], min_val=1, max_val=NT)

        def aggregate(name, table, gat):
            width = ROW if gat else D
            cols_in = AW if gat else D + 1
            s = {}

            def sm(n, count=None):
                s[n] = (stage_sem(f"agg_{n}") if count is None else
                        [stage_sem(f"agg_{n}{i}") for i in range(count)])

            for n in ("onehot", "sums", "added", "wz0", "base"):
                sm(n)
            sm("idx", SLOTS)
            s["rows"] = [sem(f"{name}_rows{i}") for i in range(SLOTS)]
            if gat:
                sm("tables", SLOTS)
                for n in ("el_cols", "el_rows", "fwd_local", "bwd_local", "tile_last", "tile_first", "tile_ends",
                          "carry_old", "carry_fwd", "carry_bwd", "carry_rows", "in_left", "in_right",
                          "fwd", "bwd", "seg_max", "e", "e_max", "leaky", "old_e", "old_leaky", "old_arg",
                          "arg", "weights", "w_cols", "r_row", "rm1", "r_cols", "rescale", "rescaled",
                          "scaled"):
                    sm(n)

            with nc.Block() as block:
                @block.vector
                def _(dve):
                    nc.vector.memset(accf, 0.0)
                    if not gat:
                        nc.vector.memset(slots[:, :, :, D:D + 1], 1.0)

                @block.gpsimd
                def _(pool):
                    pool.memset(carry[:, :], NEG)

            def body(fn, first, steady, last):
                for k in range(SLOTS):
                    first(k)
                return fn

            with nc.Fori(0, rounds) as rnd:
                with nc.Block() as block:
                    @block.sync
                    def _(sp):
                        turn0 = sp.snap(rnd * ITER)
                        n0 = sp.snap(rnd * NCH)

                        def load(g, k, peeled):
                            n = SLOTS * g + k
                            if not peeled:
                                sp.wait_ge(s["sums"], QUADS * (n0 + n) - QUADS * SLOTS + 1)
                            sp.dma_start(idx[:, k, :], src_t[:, bass.ds(n * CT, CT)]).then_inc(s["idx"][k], 16)
                            if gat:
                                if not peeled:
                                    sp.wait_ge(s["weights"], n0 + n - (SLOTS - 1))
                                sp.dma_start(pen[:, k, :], pen_rows[bass.ds(n, 1), :, :, :]
                                             .rearrange("c h t p -> (c h t) p")).then_inc(s["tables"][k], 16)
                                sp.dma_start(er[:, k, :], er_rows[bass.ds(n, 1), :, :]
                                             .rearrange("c h (t p) -> (c h t) p", p=P)).then_inc(s["tables"][k], 16)
                                sp.dma_start(chain_pen[:, k, :], chain_tab[bass.ds(n, 1), :]
                                             .broadcast_to([HEADS, 2 * CT])).then_inc(s["tables"][k], 16)

                        for k in range(SLOTS):
                            load(0, k, True)
                        with sp.Fori(1, ITER) as g:
                            for k in range(SLOTS):
                                load(g, k, False)

                    @block.gpsimd
                    def _(pool):
                        turn0 = pool.snap(rnd * ITER)
                        n0 = pool.snap(rnd * NCH)

                        def gather(g, k, peeled):
                            n = SLOTS * g + k
                            pool.wait_ge(s["idx"][k], 16 * (turn0 + g) + 16)
                            pool.sem_inc(pool_turn, 1)
                            for q in range(QUADS):
                                if not peeled:
                                    pool.wait_ge(s["sums"], QUADS * (n0 + n) - QUADS * SLOTS + q + 1)
                                    pool.sem_inc(pool_turn, 1)
                                for t in range(q * QT, q * QT + QT):
                                    pool.indirect_dma_start(
                                        slots[:, k, t, 0:width], None, table,
                                        bass.IndirectOffsetOnAxis(ap=idx[:, k, t:t + 1], axis=0),
                                    ).then_inc(s["rows"][k], 16)

                        for k in range(SLOTS):
                            gather(0, k, True)
                        with pool.Fori(1, ITER) as g:
                            for k in range(SLOTS):
                                gather(g, k, False)

                    @block.scalar
                    def _(act):
                        turn0 = act.snap(rnd * ITER)
                        n0 = act.snap(rnd * NCH)

                        def one_hot(g, k, q, free):
                            n = SLOTS * g + k
                            b = (QUADS * k + q) % SB
                            if free is None or free >= SB:
                                act.wait_ge(s["sums"], QUADS * (n0 + n) + q - SB + 1)
                            for t in range(QT):
                                col = n * CT + q * QT + t
                                nc.scalar.activation(onehot[:, b, t, :], lanes[:, :], ACT.Abs,
                                                     bias=negrel[:, bass.ds(col, 1)]).then_inc(s["wz0"], 1)
                            act.wait_ge(s["wz0"], CT * (n0 + n) + q * QT + QT)
                            nc.scalar.activation(onehot[:, b, :, :], onehot[:, b, :, :], ACT.Relu,
                                                 bias=one_c[:, 0:1], scale=-1.0).then_inc(s["onehot"], 1)

                        def pack_el(g, k, n):
                            act.wait_ge(s["rows"][k], 16 * CT * (turn0 + g) + 16 * CT)
                            nc.scalar.activation(el_cols[:, :].rearrange("p (h t) -> p h t", h=HEADS),
                                                 slots[:, k, :, AW:AW + HEADS].rearrange("p t h -> p h t"),
                                                 ACT.Copy).then_inc(s["el_cols"], 1)

                        def weigh(n):
                            act.wait_ge(s["arg"], n + 1)
                            act.wait_ge(s["old_arg"], n + 1)
                            nc.scalar.activation(wrow[:, :], wexp[:, :], ACT.Exp).then_inc(s["weights"], 1)

                        def chunk(g, k, nth=None, more=True):
                            n = SLOTS * g + k
                            g1, k1 = (g, k + 1) if k + 1 < SLOTS else (g + 1, 0)
                            free = (lambda i: None) if nth is None else (lambda i: nth * QUADS + i)
                            if more and gat:
                                pack_el(g1, k1, n0 + n + 1)
                            one_hot(g, k, 3, free(3))
                            if more:
                                one_hot(g1, k1, 0, free(4))
                                if gat:
                                    weigh(n0 + n + 1)
                                one_hot(g1, k1, 1, free(5))
                                one_hot(g1, k1, 2, free(6))

                        for q in range(3):
                            one_hot(0, 0, q, q)
                        if gat:
                            pack_el(0, 0, n0)
                            weigh(n0)
                        for k in range(SLOTS):
                            chunk(0, k, nth=k)
                        with act.Fori(1, ITER - 1) as g:
                            for k in range(SLOTS):
                                chunk(g, k)
                        for k in range(SLOTS):
                            chunk(ITER - 1, k, more=(k + 1 < SLOTS))

                    @block.tensor
                    def _(pe):
                        T = nc.tensor
                        turn0 = pe.snap(rnd * ITER)
                        n0 = pe.snap(rnd * NCH)

                        def quad(g, k, q, nth):
                            n = SLOTS * g + k
                            qn = QUADS * (n0 + n) + q
                            b = (QUADS * k + q) % SB
                            pe.wait_ge(s["onehot"], qn + 1)
                            if gat:
                                pe.wait_ge(s["scaled"], qn + 1)
                            else:
                                pe.wait_ge(s["rows"][k], 16 * CT * (turn0 + g) + 16 * CT)
                            if nth is None or nth * QUADS + q >= 2:
                                pe.wait_ge(s["added"], qn - 1)
                            for w in range(2):
                                for t in range(QT):
                                    last = T.matmul(pair[q % 2][:, w, 0:cols_in],
                                                    onehot[:, b, t, w * P:w * P + P],
                                                    slots[:, k, q * QT + t, 0:cols_in],
                                                    start=(t == 0), stop=(t == QT - 1))
                            last.then_inc(s["sums"], 1)

                        def el_rows(n):
                            pe.wait_ge(s["el_cols"], n + 1)
                            pe.sem_inc(pe_turn, 1)
                            T.transpose(ps_x[0:ROWS, 0:P], el_cols[:, :], ident[:, :]).then_inc(s["el_rows"], 1)

                        def tile_ends(n):
                            pe.wait_ge(s["tile_last"], n + 1)
                            pe.wait_ge(s["tile_first"], n + 1)
                            pe.sem_inc(pe_turn, 1)
                            T.matmul(ps_c[0:HEADS, 0:2 * CT], head_mask[:, :],
                                     ends[:, :, :].rearrange("p a t -> p (a t)"),
                                     start=True, stop=True).then_inc(s["tile_ends"], 1)

                        def carry_rows(n):
                            pe.wait_ge(s["carry_fwd"], n + 1)
                            pe.wait_ge(s["carry_bwd"], n + 1)
                            T.matmul(ps_c[0:ROWS, 64:64 + 2 * CT], head_rows[:, :],
                                     carry[:, :].rearrange("p (a t) -> p a t", a=2)[:, :, 0:CT],
                                     start=True, stop=True).then_inc(s["carry_rows"], 1)

                        def w_cols(n):
                            pe.wait_ge(s["weights"], n + 1)
                            pe.sem_inc(pe_turn, 1)
                            T.transpose(ps_w[:, 0:ROWS], wrow[:, 0:P], ident[0:ROWS, 0:ROWS]).then_inc(s["w_cols"], 1)
                            T.matmul(ps_c[0:1, 128:128 + HEADS], wrow[:, P:P + 1], first_rows[:, :],
                                     start=True, stop=True).then_inc(s["r_row"], 1)

                        def r_cols(k, n):
                            pe.wait_ge(s["rm1"], n + 1)
                            pe.wait_ge(s["onehot"], QUADS * n + 1)
                            T.matmul(ps_d[:, 0:HEADS], onehot[0:1, (QUADS * k) % SB, 0, 0:P], rm1[:, :],
                                     start=True, stop=True).then_inc(s["r_cols"], 1)

                        def chunk(g, k, nth=None, more=True):
                            n = n0 + SLOTS * g + k
                            g1, k1 = (g, k + 1) if k + 1 < SLOTS else (g + 1, 0)
                            more = more and gat
                            if more:
                                el_rows(n + 1)
                            quad(g, k, 0, nth)
                            if more:
                                tile_ends(n + 1)
                            quad(g, k, 1, nth)
                            if more:
                                carry_rows(n + 1)
                            quad(g, k, 2, nth)
                            if more:
                                w_cols(n + 1)
                            quad(g, k, 3, nth)
                            if more:
                                r_cols(k1, n + 1)

                        if gat:
                            el_rows(n0)
                            tile_ends(n0)
                            carry_rows(n0)
                            w_cols(n0)
                            r_cols(0, n0)
                        for k in range(SLOTS):
                            chunk(0, k, nth=k)
                        with pe.Fori(1, ITER - 1) as g:
                            for k in range(SLOTS):
                                chunk(g, k)
                        for k in range(SLOTS):
                            chunk(ITER - 1, k, more=(k + 1 < SLOTS))

                    @block.vector
                    def _(dve):
                        V = nc.vector
                        turn0 = dve.snap(rnd * ITER)
                        n0 = dve.snap(rnd * NCH)

                        def add(g, k, q, first):
                            qn = QUADS * (n0 + SLOTS * g + k) + q
                            base = dve.value_load(base_row[0:1, bass.ds(QUADS * (SLOTS * g + k) + q, 1)],
                                                  min_val=0, max_val=NT)
                            dve.wait_ge(s["sums"], qn + 1)
                            if not (first and k == 0 and q == 0):
                                dve.wait_ge(s["added"], qn)
                            if gat and q == 0:
                                dve.wait_ge(s["rescaled"], n0 + SLOTS * g + k + 1)
                            to = accf[:, bass.ds(base * AW, 2 * AW)].rearrange("p (w c) -> p w c", w=2)[:, :, 0:cols_in]
                            V.tensor_tensor(to, to, pair[q % 2][:, :, 0:cols_in], ALU.add).then_inc(s["added"], 1)

                        def scans(k, left, right, out_f, out_b, done_f, done_b):
                            V.tensor_tensor_scan(out_f[:, :], pen[:, k, 0:P], ps_x[0:ROWS, 0:P], left,
                                                 ALU.add, ALU.max).then_inc(s[done_f], 1)
                            V.tensor_tensor_scan(out_b[:, P - 1::-1], pen[:, k, P:0:-1], ps_x[0:ROWS, P - 1::-1], right,
                                                 ALU.add, ALU.max).then_inc(s[done_b], 1)

                        def local_maxima(g, k, n):
                            dve.wait_ge(s["el_rows"], n + 1)
                            dve.wait_ge(s["tables"][k], 48 * (turn0 + g) + 48)
                            scans(k, NEG, NEG, scan_f, scan_b, "fwd_local", "bwd_local")
                            dve.wait_ge(s["fwd_local"], n + 1)
                            V.tensor_scalar(ends[:, 0, :], tile_mask[:, :], scan_f[:, P - 1:P], None,
                                            ALU.mult).then_inc(s["tile_last"], 1)
                            dve.wait_ge(s["bwd_local"], n + 1)
                            V.tensor_scalar(ends[:, 1, :], tile_mask[:, :], scan_b[:, 0:1], None,
                                            ALU.mult).then_inc(s["tile_first"], 1)

                        def carries(k, n, peeled=False):
                            dve.wait_ge(s["tile_ends"], n + 1)
                            if not peeled:
                                dve.wait_ge(s["carry_fwd"], n)
                            V.tensor_copy(carry[:, 0:1], carry[:, CT:CT + 1]).then_inc(s["carry_old"], 1)
                            V.tensor_tensor_scan(carry[:, 2 * CT:CT:-1], chain_pen[:, k, 2 * CT - 1:CT - 1:-1],
                                                 ps_c[0:HEADS, 2 * CT - 1:CT - 1:-1], NEG,
                                                 ALU.add, ALU.max).then_inc(s["carry_bwd"], 1)
                            dve.wait_ge(s["carry_old"], n + 1)
                            V.tensor_tensor_scan(carry[:, 1:CT + 1], chain_pen[:, k, 0:CT], ps_c[0:HEADS, 0:CT],
                                                 carry[:, 0:1], ALU.add, ALU.max).then_inc(s["carry_fwd"], 1)

                        def exponents(k, n):
                            dve.wait_ge(s["carry_rows"], n + 1)
                            for side, done in ((0, "in_left"), (1, "in_right")):
                                V.tensor_tensor_reduce(out=scrap[:, side, :], in0=ps_c[0:ROWS, 64 + side * CT:64 + side * CT + CT],
                                                       in1=tile_mask[:, :], scale=1.0, scalar=0.0, op0=ALU.mult,
                                                       op1=ALU.add, accum_out=edge_in[:, side:side + 1]).then_inc(s[done], 1)
                            V.tensor_tensor(logit[:, 0, :], er[:, k, :], ps_x[0:ROWS, 0:P], ALU.add).then_inc(s["e"], 1)
                            dve.wait_ge(s["in_left"], n + 1)
                            dve.wait_ge(s["in_right"], n + 1)
                            scans(k, edge_in[:, 0:1], edge_in[:, 1:2], scan_f, scan_b, "fwd", "bwd")
                            V.tensor_tensor(old[:, 0:1], edge_in[:, 0:1], er[:, k, 0:1], ALU.add).then_inc(s["old_e"], 1)
                            dve.wait_ge(s["fwd"], n + 1)
                            dve.wait_ge(s["bwd"], n + 1)
                            V.tensor_tensor(scan_f[:, :], scan_f[:, :], scan_b[:, :], ALU.max).then_inc(s["seg_max"], 1)
                            dve.wait_ge(s["old_e"], n + 1)
                            V.scalar_tensor_tensor(out=old[:, 1:2], in0=old[:, 0:1], scalar=SLOPE, in1=old[:, 0:1],
                                                   op0=ALU.mult, op1=ALU.max).then_inc(s["old_leaky"], 1)
                            dve.wait_ge(s["seg_max"], n + 1)
                            V.tensor_tensor(logit[:, 1, :], scan_f[:, :], er[:, k, :], ALU.add).then_inc(s["e_max"], 1)
                            dve.wait_ge(s["e"], n + 1)
                            dve.wait_ge(s["e_max"], n + 1)
                            V.scalar_tensor_tensor(out=logit[:, :, :], in0=logit[:, :, :], scalar=SLOPE, in1=logit[:, :, :],
                                                   op0=ALU.mult, op1=ALU.max).then_inc(s["leaky"], 1)
                            dve.wait_ge(s["leaky"], n + 1)
                            V.tensor_tensor(wexp[:, 0:P], logit[:, 0, :], logit[:, 1, :], ALU.subtract).then_inc(s["arg"], 1)
                            dve.wait_ge(s["old_leaky"], n + 1)
                            V.tensor_scalar(wexp[:, P:P + 1], old[:, 1:2], logit[:, 1, 0:1], 0.0,
                                            ALU.subtract, ALU.min).then_inc(s["old_arg"], 1)

                        def scale(k, q, n):
                            dve.wait_ge(s["w_cols"], n + 1)
                            v = slots[:, k, q * QT:(q + 1) * QT, 0:AW].rearrange("p t (h d) -> p t h d", h=HEADS)
                            w = ps_w[:, 0:ROWS].rearrange("p (h t) -> p t h", h=HEADS)[:, q * QT:(q + 1) * QT, :]
                            V.tensor_tensor(v, v, w.unsqueeze(3).broadcast_to([P, QT, HEADS, HD + 1]),
                                            ALU.mult).then_inc(s["scaled"], 1)

                        def r_minus_1(n):
                            dve.wait_ge(s["r_row"], n + 1)
                            V.tensor_scalar(rm1[:, :], ps_c[0:1, 128:128 + HEADS], 1.0, None,
                                            ALU.subtract).then_inc(s["rm1"], 1)

                        def rescale_acc(g, k, n, peeled=False):
                            base = dve.value_load(base_row[0:1, bass.ds(QUADS * (SLOTS * g + k), 1)],
                                                  min_val=0, max_val=NT)
                            dve.wait_ge(s["r_cols"], n + 1)
                            V.tensor_scalar(rescale[:, :], ps_d[:, 0:HEADS], 1.0, None, ALU.add).then_inc(s["rescale"], 1)
                            dve.wait_ge(s["rescale"], n + 1)
                            if not peeled:
                                dve.wait_ge(s["added"], QUADS * n)
                            v = accf[:, bass.ds(base * AW, AW)].rearrange("p (h d) -> p h d", h=HEADS)
                            V.tensor_tensor(v, v, rescale[:, :].unsqueeze(2).broadcast_to([P, HEADS, HD + 1]),
                                            ALU.mult).then_inc(s["rescaled"], 1)

                        def chunk(g, k, more=True, first=False):
                            n = n0 + SLOTS * g + k
                            g1, k1 = (g, k + 1) if k + 1 < SLOTS else (g + 1, 0)
                            more = more and gat
                            if more:
                                local_maxima(g1, k1, n + 1)
                            add(g, k, 0, first)
                            if more:
                                carries(k1, n + 1)
                            add(g, k, 1, first)
                            if more:
                                exponents(k1, n + 1)
                            add(g, k, 2, first)
                            if more:
                                scale(k1, 0, n + 1)
                                scale(k1, 1, n + 1)
                                r_minus_1(n + 1)
                                scale(k1, 2, n + 1)
                                scale(k1, 3, n + 1)
                            add(g, k, 3, first)
                            if more:
                                rescale_acc(g1, k1, n + 1)

                        if gat:
                            local_maxima(0, 0, n0)
                            carries(0, n0, peeled=True)
                            exponents(0, n0)
                            for q in range(QUADS):
                                scale(0, q, n0)
                            r_minus_1(n0)
                            rescale_acc(0, 0, n0, peeled=True)
                        for k in range(SLOTS):
                            chunk(0, k, first=True)
                        with dve.Fori(1, ITER - 1) as g:
                            for k in range(SLOTS):
                                chunk(g, k)
                        for k in range(SLOTS):
                            chunk(ITER - 1, k, more=(k + 1 < SLOTS))

                with nc.Block() as block:
                    @block.vector
                    def _(dve):
                        V = nc.vector
                        b0_ = s["base"]
                        row_f = in_a[0:1, 0, 0:2, :].rearrange("p t d -> p (t d)")[:, 0:NCH * QUADS]
                        V.tensor_scalar(lanes[:, :], lanes[:, :], float(WIN), None, ALU.add)
                        V.tensor_copy(row_f, base_row[:, :]).then_inc(b0_, 1)
                        dve.wait_ge(b0_, 3 * rnd + 1)
                        V.tensor_scalar(row_f, row_f, 2.0, float(NT), ALU.add, ALU.min).then_inc(b0_, 1)
                        dve.wait_ge(b0_, 3 * rnd + 2)
                        V.tensor_copy(base_row[:, :], row_f).then_inc(b0_, 1)

                    @block.gpsimd
                    def _(pool):
                        pool.memset(carry[:, :], NEG)

            clear_stage_sems()
            s_back = sem(f"{name}_back")
            with nc.Block() as block:
                @block.gpsimd
                def _(pool):
                    pool.iota(lane_i, [[1, WIN]], base=0, channel_multiplier=0).then_inc(s_back, 1)
                    pool.wait_ge(s_back, 1)
                    pool.tensor_copy(lanes[:, :], lane_i)

                @block.sync
                def _(sp):
                    sp.dma_start(base_row[:, :], base_tab.rearrange("c q -> (c q)").unsqueeze(0)).then_inc(s_back_d, 16)
                    sp.wait_ge(s_back_d, 16 * back_count[0])

        s_back_d = sem("s_back_d")
        back_count = [1]

        aggregate("sage", h0_tab, False)

        s_deg = sem("s_deg")
        s_cum = sem("s_cum")
        pos_f = tmp_a[:, 0, 0:NT]
        tot_f = tmp_b[:, 0, 0:NT]
        cum_f = tmp_b[:, 1, 0:NT]
        zer_f = tmp_a[:, 1, 0:NT]
        with nc.Block() as block:
            @block.vector
            def _(dve):
                V = nc.vector
                n = [0]

                def then(ins):
                    n[0] += 1
                    ins.then_inc(s_deg, 1)
                    dve.wait_ge(s_deg, n[0])

                V.memset(zer_f, 0.0)
                then(V.tensor_copy(deg[:, :], accf.rearrange("p (t c) -> p t c", c=AW)[:, 0:NT, D]))
                then(V.tensor_scalar(deg_inv[:, :], deg[:, :], 1.0, None, ALU.max))
                then(V.reciprocal(deg_inv[:, :], deg_inv[:, :]))
                dve.wait_ge(s_cum, 2)
                then(V.tensor_copy(tot_f, ps_w[:, 0:NT]))
                then(V.tensor_tensor_scan(cum_f, zer_f, tot_f, 0.0, ALU.add, ALU.add))
                then(V.tensor_tensor(cum_f, cum_f, tot_f, ALU.subtract))
                then(V.tensor_tensor(pos_f, cum_f, ps_x[:, 0:NT], ALU.add))
                then(V.tensor_scalar(tot_f, deg[:, :], 0.0, float(NOWHERE), ALU.is_equal, ALU.mult))
                then(V.tensor_tensor(pos_f, pos_f, tot_f, ALU.max))
                then(V.tensor_copy(seg_pos[:, :], pos_f))

            @block.tensor
            def _(pe):
                pe.wait_ge(s_deg, 1)
                nc.tensor.matmul(ps_x[:, 0:NT], before[:, :], deg[:, :], start=True, stop=True).then_inc(s_cum, 1)
                nc.tensor.matmul(ps_w[:, 0:NT], ones[:, :], deg[:, :], start=True, stop=True).then_inc(s_cum, 1)

        s_in = [sem(f"s_in{i}") for i in range(2)]
        s_mean = sem("s_mean")
        s_tr = sem("s_tr")
        s_cp = sem("s_cp")
        s_mm = sem("s_mm")
        s_xb = sem("s_xb")
        s_x1 = sem("s_x1")
        s_st = sem("s_st")
        s_ag = sem("s_ag")
        s_mv = sem("s_mv")
        s_x1o = [sem(f"s_x1o{i}") for i in range(2)]

        def tile_of(v, g, j):
            return v * 0 + g * GROUP + j

        with nc.Block() as block:
            @block.sync
            def _(sp):
                def load(g, half, last=False, peeled=False):
                    if not peeled:
                        sp.wait_ge(s_x1o[half], 16 * g)
                    half_load(sp, x, in_a, g, half, s_in[half], last)
                    half_load(sp, h0_tab, in_b, g, half, s_in[half], False)

                def store(g, half):
                    sp.wait_ge(s_x1, g * GROUP + half * HALF + HALF)
                    sp.wait_ge(s_st, g * GROUP + half * HALF + HALF)
                    sp.dma_start(store_rows(x1_tab, g, half), in_a[:, half, :, :]).then_inc(s_x1o[half], 16)

                load(0, 0, peeled=True)
                load(0, 1, peeled=True)
                with sp.Fori(0, NG - 2) as g:
                    for half in range(2):
                        store(g, half)
                        load(g + 1, half)
                store(NG - 2, 0)
                load(NG - 1, 0)
                store(NG - 2, 1)
                load(NG - 1, 1, last=True)
                store(NG - 1, 0)
                store(NG - 1, 1)
                sp.wait_ge(s_x1o[0], 16 * NG)
                sp.wait_ge(s_x1o[1], 16 * NG)

            @block.vector
            def _(dve):
                V = nc.vector

                def mean(g, j, first):
                    if not (first and j < 2):
                        dve.wait_ge(s_tr, g * GROUP + j - 1)
                    V.tensor_scalar(tmp_b[:, j % 2, :], acc_cols(g * GROUP + j, 0, D), deg_inv[:, bass.ds(g * GROUP + j, 1)], None, ALU.mult).then_inc(s_mean, 1)

                def finish(g, j, first):
                    t = g * GROUP + j
                    v = in_a[:, j // HALF, j % HALF, :]
                    dve.wait_ge(s_mm, t + 1)
                    V.tensor_tensor(tmp_a[:, j % 2, :], ps_w[:, 0:D] if j % 2 else ps_d[:, 0:D],
                                    v, ALU.add).then_inc(s_xb, 1)
                    dve.wait_ge(s_xb, t + 1)
                    V.tensor_tensor(v, tmp_a[:, j % 2, :], bias[0][:, :], ALU.add).then_inc(s_x1, 1)
                    dve.wait_ge(s_x1, t + 1)
                    V.bn_stats(stats[:, j, :], v).then_inc(s_st, 1)

                def aggregate_stats(g):
                    dve.wait_ge(s_st, g * GROUP + GROUP)
                    dve.sem_inc(dve_turn, 1)
                    for j in range(GROUP):
                        V.bn_aggr(mvg[:, j, :], stats[:, j, :]).then_inc(s_ag, 1)
                    dve.wait_ge(s_ag, g * GROUP + GROUP)
                    V.tensor_copy(mv[:, bass.ds(g * GROUP, GROUP), :], mvg[:, :, :]).then_inc(s_mv, 1)

                mean(0, 0, True)
                mean(0, 1, True)

                def group(g, first, last=False):
                    for j in range(GROUP):
                        if j == 0 or j == HALF:
                            dve.wait_ge(s_in[j // HALF], 32 * g + 32 + (16 if last and j else 0))
                        finish(g, j, first)
                        if not (last and j >= GROUP - 2):
                            mean(*((g, j + 2) if j + 2 < GROUP else (g + 1, j + 2 - GROUP)), False)
                    aggregate_stats(g)
                    dve.wait_ge(s_mv, g + 1)

                group(0, True)
                with dve.Fori(1, NG - 1) as g:
                    group(g, False)
                group(NG - 1, False, last=True)

            @block.tensor
            def _(pe):
                T = nc.tensor

                def transposes(g, j, first, last):
                    t = g * GROUP + j
                    if j == 0 or j == HALF:
                        pe.wait_ge(s_in[j // HALF], 32 * g + 32 + (16 if last and j else 0))
                    pe.wait_ge(s_mean, t + 1)
                    if not (first and j < 2):
                        pe.wait_ge(s_cp, t - 1)
                    to = pair[j % 2][:, 0, :]
                    for c in range(2):
                        T.transpose(to[:, c * P:c * P + P], tmp_b[:, j % 2, c * P:c * P + P], ident[:, :])
                    for c in range(2):
                        last_ = T.transpose(to[:, (2 + c) * P:(3 + c) * P],
                                            in_b[:, j // HALF, j % HALF, c * P:c * P + P], ident[:, :])
                    last_.then_inc(s_tr, 1)

                def products(g, j, first):
                    t = g * GROUP + j
                    pe.wait_ge(s_cp, t + 1)
                    if not (first and j < 2):
                        pe.wait_ge(s_xb, t - 1)
                    to = ps_w if j % 2 else ps_d
                    for c in range(4):
                        last = T.matmul(to[:, 0:D], lhs[:, j % 2, c * P:c * P + P],
                                        (wnT if c < 2 else wsT)[:, c % 2, :], start=(c == 0), stop=(c == 3))
                    last.then_inc(s_mm, 1)

                def group(g, first, last=False):
                    for j in range(GROUP):
                        nxt = (g, j + 1) if j + 1 < GROUP else (g + 1, 0)
                        if not (last and j == GROUP - 1):
                            transposes(*nxt, first and j + 1 < GROUP, last)
                        products(g, j, first)

                transposes(0, 0, True, False)
                group(0, True)
                with pe.Fori(1, NG - 1) as g:
                    group(g, False)
                group(NG - 1, False, last=True)

            @block.scalar
            def _(act):
                def copies(g, first):
                    for j in range(GROUP):
                        t = g * GROUP + j
                        act.wait_ge(s_tr, t + 1)
                        if not (first and j < 2):
                            act.wait_ge(s_mm, t - 1)
                        nc.scalar.activation(lhs[:, j % 2, :], pair[j % 2][:, 0, :], ACT.Copy).then_inc(s_cp, 1)

                copies(0, True)
                with act.Fori(1, NG) as g:
                    copies(g, False)

        s_sq = sem("s_sq")
        with nc.Block() as block:
            @block.scalar
            def _(act):
                nc.scalar.activation(rstd[:, :], mv[:, :, 1], ACT.Sqrt, bias=eps_c[:, 0:1]).then_inc(s_sq, 1)

            @block.vector
            def _(dve):
                dve.wait_ge(s_sq, 1)
                nc.vector.reciprocal(rstd[:, :], rstd[:, :]).then_inc(s_sq, 1)
                dve.wait_ge(s_sq, 2)
                nc.vector.scalar_tensor_tensor(out=nbias[:, :], in0=mv[:, :, 0], scalar=-1.0, in1=rstd[:, :],
                                               op0=ALU.mult, op1=ALU.mult)
                nc.vector.memset(z_out, 1.0)

        def gat_output(dve, act, s, b, g, j, first, to):
            pass

        def node_stage(name, norm, layer, final):
            s = {n: stage_sem(f"node_{n}") for n in
                 ("h", "tr", "cp", "mm", "z", "zel", "zer", "den", "rec", "div", "res", "bias", "neg", "exp",
                  "elu", "pos")}
            s["scat"] = sem(f"{name}_scat")
            s_load = [stage_sem(f"node_load{i}") for i in range(2)]
            s_hout = [stage_sem(f"node_hout{i}") for i in range(2)]
            s_zout = [stage_sem(f"node_zout{i}") for i in range(2)]
            z_w = None if final else wz[layer]
            with nc.Block() as block:
                @block.sync
                def _(sp):
                    def load(g, half):
                        half_load(sp, x1_tab if norm else hin_tab, in_a, g, half, s_load[half], False)
                        if final:
                            half_load(sp, x1_tab, in_b, g, half, s_load[half], False)

                    def store(g, half, last=False):
                        sp.wait_ge(s["h"], g * GROUP + half * HALF + HALF)
                        v = accf[:, bass.ds((g * 2 + half) * HALF * AW, HALF * AW)]
                        v = v.rearrange("p (t c) -> p t c", c=AW)[:, :, 0:D]
                        if not final:
                            sp.dma_start(store_rows(hin_tab, g, half), in_b[:, half, :, :]).then_inc(s_hout[half], 16)
                            sp.wait_ge(s["zel"], g * GROUP + half * HALF + HALF)
                            sp.wait_ge(s["z"], g * GROUP + half * HALF + HALF)
                            sp.dma_start(store_rows(z_tab, g, half), z_out[:, half, :, :]).then_inc(s_zout[half], 16)
                        elif not last:
                            sp.dma_start(store_rows(out, g, half), v).then_inc(s_hout[half], 16)
                        else:
                            full, n = (NT - HALF) * P, (HALF - 1) * P
                            sp.dma_start(out[full:full + n, :].rearrange("(t p) d -> p t d", p=P),
                                         v[:, 0:HALF - 1, :]).then_inc(s_hout[half], 16)
                            sp.dma_start(out[full + n:NODES, :], v[0:LAST_ROWS, HALF - 1, :]).then_inc(s_hout[half], 16)

                    load(0, 0)
                    load(0, 1)
                    with sp.Fori(0, NG - 1) as g:
                        for half in range(2):
                            store(g, half)
                            load(g + 1, half)
                    store(NG - 1, 0)
                    store(NG - 1, 1, last=True)
                    sp.wait_ge(s_hout[0], 16 * NG)
                    sp.wait_ge(s_hout[1], 16 * NG + (16 if final else 0))
                    if not final:
                        sp.wait_ge(s_zout[0], 16 * NG)
                        sp.wait_ge(s_zout[1], 16 * NG)

                @block.scalar
                def _(act):
                    def tile(g, j, first):
                        t = g * GROUP + j
                        if norm:
                            if not first and j % HALF == 0:
                                act.wait_ge(s_hout[j // HALF], 16 * g)
                            if j % HALF == 0:
                                act.wait_ge(s_load[j // HALF], 16 * (g + 1))
                            nc.scalar.activation(in_b[:, j // HALF, j % HALF, :],
                                                 in_a[:, j // HALF, j % HALF, :], ACT.Relu, bias=nbias[:, bass.ds(t, 1)],
                                                 scale=rstd[:, bass.ds(t, 1)]).then_inc(s["h"], 1)
                        else:
                            act.wait_ge(s["neg"], t + 1)
                            nc.scalar.activation(tmp_b[:, j % 2, :], tmp_b[:, j % 2, :], ACT.Exp).then_inc(s["exp"], 1)

                    def z_copy(g, j, first):
                        t = g * GROUP + j
                        act.wait_ge(s["mm"], t + 1)
                        if not first:
                            act.wait_ge(s_zout[j // HALF], 16 * g)
                        zp = ps_w if j % 2 else ps_d
                        to = z_out[:, j // HALF, j % HALF, 0:AW].rearrange("p (h d) -> p h d", h=HEADS)[:, :, 0:HD]
                        nc.scalar.activation(to, zp[:, 0:D].rearrange("p (h d) -> p h d", h=HEADS),
                                             ACT.Copy).then_inc(s["z"], 1)

                    def group(g, first, last=False):
                        for j in range(GROUP):
                            if not (last and j >= GROUP - ahead):
                                tile(*((g, j + ahead) if j + ahead < GROUP else (g + 1, j + ahead - GROUP)),
                                     first and j + ahead < GROUP)
                            if not final:
                                z_copy(g, j, first)

                    ahead = 2 if norm else 1
                    for j in range(ahead):
                        tile(0, j, True)
                    group(0, True)
                    with act.Fori(1, NG - 1) as g:
                        group(g, False)
                    group(NG - 1, False, last=True)

                @block.vector
                def _(dve):
                    V = nc.vector

                    def activated(g, j, first):
                        t = g * GROUP + j
                        v = acc_cols(t, 0, AW).rearrange("p (h d) -> p h d", h=HEADS)
                        if j == 0 or j == HALF:
                            dve.wait_ge(s_load[j // HALF], (32 if final else 16) * (g + 1))
                        V.tensor_scalar(rescale[:, :], v[:, :, HD], 1e-30, None, ALU.max).then_inc(s["den"], 1)
                        dve.wait_ge(s["den"], t + 1)
                        V.reciprocal(rescale[:, :], rescale[:, :]).then_inc(s["rec"], 1)
                        dve.wait_ge(s["rec"], t + 1)
                        a = tmp_a[:, j % 2, :]
                        V.tensor_tensor(a.rearrange("p (h d) -> p h d", h=HEADS), v[:, :, 0:HD],
                                        rescale[:, :].unsqueeze(2).broadcast_to([P, HEADS, HD]),
                                        ALU.mult).then_inc(s["div"], 1)
                        dve.wait_ge(s["div"], t + 1)
                        V.tensor_tensor(a, a, in_a[:, j // HALF, j % HALF, :], ALU.add).then_inc(s["res"], 1)
                        dve.wait_ge(s["res"], t + 1)
                        V.tensor_tensor(a, a, bias[layer if not final else 2][:, :], ALU.add).then_inc(s["bias"], 1)
                        dve.wait_ge(s["bias"], t + 1)
                        V.tensor_scalar(tmp_b[:, j % 2, :], a, 0.0, None, ALU.min).then_inc(s["neg"], 1)

                    def elu(g, j, first):
                        t = g * GROUP + j
                        dve.wait_ge(s["exp"], t + 1)
                        if not final and not first and j % HALF == 0:
                            dve.wait_ge(s_hout[j // HALF], 16 * g)
                        to = acc_cols(t, 0, D) if final else in_b[:, j // HALF, j % HALF, :]
                        e = V.scalar_tensor_tensor(out=tmp_a[:, j % 2, :] if final else to, in0=tmp_b[:, j % 2, :],
                                                   scalar=-1.0, in1=tmp_a[:, j % 2, :], op0=ALU.add, op1=ALU.max)
                        if final:
                            e.then_inc(s["elu"], 1)
                            dve.wait_ge(s["elu"], t + 1)
                            V.tensor_tensor(to, tmp_a[:, j % 2, :], in_b[:, j // HALF, j % HALF, :],
                                            ALU.add).then_inc(s["h"], 1)
                        else:
                            e.then_inc(s["h"], 1)

                    def lhs_copy(g, j, first):
                        t = g * GROUP + j
                        dve.wait_ge(s["tr"], t + 1)
                        if not (first and j < 2):
                            dve.wait_ge(s["mm"], t - 1)
                        V.tensor_copy(lhs[:, j % 2, 0:D], pair[j % 2][:, 0, 0:D]).then_inc(s["cp"], 1)

                    def tails(g, j, first):
                        t = g * GROUP + j
                        dve.wait_ge(s["mm"], t + 1)
                        dve.wait_ge(s["z"], t + 1)
                        if not first:
                            dve.wait_ge(s_zout[j // HALF], 16 * g)
                            if j == 0:
                                dve.wait_ge(s["scat"], 16 * GROUP * g)
                        zp = ps_w if j % 2 else ps_d
                        V.tensor_copy(z_out[:, j // HALF, j % HALF, AW:ROW], zp[:, D:D + 2 * HEADS]).then_inc(s["zel"], 1)
                        V.tensor_copy(er_stage[:, j, :], zp[:, D + HEADS:D + 2 * HEADS]).then_inc(s["zer"], 1)

                    def group(g, first, last=False):
                        for j in range(GROUP):
                            if not norm:
                                if not (last and j >= GROUP - 1):
                                    activated(*((g, j + 1) if j + 1 < GROUP else (g + 1, 0)),
                                              first and j + 1 < GROUP)
                                elu(g, j, first)
                            if not final:
                                lhs_copy(g, j, first)
                                tails(g, j, first)
                        if not final:
                            V.tensor_copy(pos_stage[:, :], seg_pos[:, bass.ds(g * GROUP, GROUP)]).then_inc(s["pos"], 1)

                    if not norm:
                        activated(0, 0, True)
                    group(0, True)
                    with dve.Fori(1, NG - 1) as g:
                        group(g, False)
                    group(NG - 1, False, last=True)

                if not final:
                    @block.tensor
                    def _(pe):
                        T = nc.tensor

                        def transposes(g, j, first):
                            t = g * GROUP + j
                            pe.wait_ge(s["h"], t + 1)
                            if not (first and j < 2):
                                pe.wait_ge(s["cp"], t - 1)
                            for c in range(2):
                                last = T.transpose(pair[j % 2][:, 0, c * P:c * P + P],
                                                   in_b[:, j // HALF, j % HALF, c * P:c * P + P], ident[:, :])
                            last.then_inc(s["tr"], 1)

                        def products(g, j, first):
                            t = g * GROUP + j
                            pe.wait_ge(s["cp"], t + 1)
                            if not (first and j < 2):
                                pe.wait_ge(s["zer"], t - 1)
                            zp = ps_w if j % 2 else ps_d
                            for c in range(2):
                                last = T.matmul(zp[:, 0:D + 2 * HEADS], lhs[:, j % 2, c * P:c * P + P], z_w[:, c, :],
                                                start=(c == 0), stop=(c == 1))
                            last.then_inc(s["mm"], 1)

                        def group(g, first, last=False):
                            for j in range(GROUP):
                                transposes(g, j, first)
                                products(g, j, first)

                        group(0, True)
                        with pe.Fori(1, NG) as g:
                            group(g, False)

                    @block.gpsimd
                    def _(pool):
                        def scatter(g):
                            pool.wait_ge(s["pos"], g + 1)
                            pool.wait_ge(s["zer"], g * GROUP + GROUP)
                            pool.sem_inc(pool_turn, 1)
                            for j in range(GROUP):
                                pool.indirect_dma_start(
                                    er_start, bass.IndirectOffsetOnAxis(ap=pos_stage[:, j:j + 1], axis=0),
                                    er_stage[:, j, :], None, bounds_check=EPAD - 1,
                                    oob_is_err=False).then_inc(s["scat"], 16)

                        with pool.Fori(0, NG) as g:
                            scatter(g)
                        pool.wait_ge(s["scat"], 16 * NT)

            clear_stage_sems()

        val = accf[0:NCH, 0:CE * HEADS]
        same = accf[0:NCH, CE * HEADS:CE * HEADS + CE]
        filled = accf[0:NCH, CE * HEADS + CE:CE * HEADS + 5 * CE].rearrange("c (h e) -> c h e", h=HEADS)

        def spread_er(name):
            s_l = sem(f"{name}_load")
            s_g = sem(f"{name}_first")
            s_f = sem(f"{name}_filled")
            s_o = sem(f"{name}_out")
            with nc.Block() as block:
                @block.sync
                def _(sp):
                    sp.dma_start(val, er_start.rearrange("(c e) h -> c (e h)", e=CE)).then_inc(s_l, 16)
                    sp.dma_start(same, same_tab).then_inc(s_l, 16)
                    for h in range(HEADS):
                        sp.wait_ge(s_f, h + 1)
                        sp.dma_start(er_rows[:, h, :], filled[:, h, :]).then_inc(s_o, 16)
                    sp.wait_ge(s_o, 16 * HEADS)

                @block.gpsimd
                def _(pool):
                    pool.indirect_dma_start(er_init[:, :], None, z_tab,
                                            bass.IndirectOffsetOnAxis(ap=first_dst[:, 0:1], axis=0)).then_inc(s_g, 16)

                @block.vector
                def _(dve):
                    dve.wait_ge(s_l, 32)
                    dve.wait_ge(s_g, 16)
                    for h in range(HEADS):
                        nc.vector.tensor_tensor_scan(filled[:, h, :], same, val[:, h:CE * HEADS:HEADS],
                                                     er_init[:, AW + HEADS + h:AW + HEADS + h + 1],
                                                     ALU.mult, ALU.add).then_inc(s_f, 1)

        back_count[0] = 2
        node_stage("norm", True, 0, False)
        spread_er("fill0")
        aggregate("gat0", z_tab, True)
        s_ones = sem("s_ones")
        with nc.Block() as block:
            @block.vector
            def _(dve):
                nc.vector.memset(z_out, 1.0).then_inc(s_ones, 1)

        back_count[0] = 3
        node_stage("mid", False, 1, False)
        spread_er("fill1")
        aggregate("gat1", z_tab, True)
        node_stage("last", False, 1, True)


_INS = ["x", "src", "dst", "L0_gnn_W_neigh", "L0_gnn_W_self", "L0_gnn_b_self",
        "L1_gnn_W0", "L1_gnn_al0", "L1_gnn_ar0", "L1_gnn_b0",
        "L1_gnn_W1", "L1_gnn_al1", "L1_gnn_ar1", "L1_gnn_b1"]


def kernel(**inputs):
    import numpy as np
    import concourse.bacc as bacc
    from concourse.bass_utils import run_bass_kernel_spmd

    nc = bacc.Bacc("TRN2", target_bir_lowering=False, num_devices=1)
    arrays, args = {}, []
    for name in _INS:
        a = np.ascontiguousarray(inputs[name])
        arrays[f"in_{name}"] = a
        args.append(nc.dram_tensor(f"in_{name}", a.shape, mybir.dt.from_np(a.dtype), kind="ExternalInput").ap())
    args.append(nc.dram_tensor("out", (NODES, D), F32, kind="ExternalOutput").ap())
    gnn_kernel(nc, *args)
    r = run_bass_kernel_spmd(nc, [arrays], core_ids=[0])
    return r.results[0]["out"]
```

```python
from contextlib import ExitStack

import concourse.bass as bass
from concourse import mybir

F32 = mybir.dt.float32
I32 = mybir.dt.int32
ACT = mybir.ActivationFunctionType
ALU = mybir.AluOpType
AX = mybir.AxisListType

P = 128
NODES, D, EDGES = 12500, 256, 200000
HEADS, HD = 4, 64
NT = -(-NODES // P)
NPAD = NT * P
LAST_ROWS = NODES - (NT - 1) * P
CT = 16
CE = CT * P
SLOTS = 3
NCH = -(-EDGES // CE)
ITER = NCH // SLOTS
TAIL = NCH % SLOTS
USES = [ITER + (k < TAIL) for k in range(SLOTS)]
EPAD = NCH * CE
QUADS, QT = 4, 4
QE = QT * P
ROWS = HEADS * CT
WIN = 2 * P
AW = HEADS * (HD + 1)
ROW = AW + 2 * HEADS
ACC_TILES = NT + 2
GROUP, HALF = 14, 7
NG = NT // GROUP
SB = 3
SLOPE = 0.2
LN_EPS = 1e-5
NEG = -1e30
PAD_NODE = NPAD - 1
NOWHERE = EPAD

assert TAIL and NT == NG * GROUP and NCH == EDGES // CE + 1 <= P and EDGES % QE and PAD_NODE >= NODES


def gnn_kernel(nc, x, src, dst, w_neigh, w_self, b_self,
               w0, al0, ar0, b0, w1, al1, ar1, b1, out):
    ctx = ExitStack()
    with ctx:
        def sb(name, shape, dt=F32):
            return ctx.enter_context(nc.sbuf_tensor(name, shape, dt))

        def pb(name, shape):
            return ctx.enter_context(nc.psum_tensor(name, shape, F32))

        def sem(name):
            return ctx.enter_context(nc.semaphore(name))

        shared = {}

        def stage_sem(name):
            if name not in shared:
                shared[name] = sem(name)
            return shared[name]

        def clear_stage_sems():
            with nc.Block() as block:
                @block.sync
                def _(sp):
                    for handle in shared.values():
                        sp.sem_clear(handle)

        def dram(name, shape, dt=F32):
            return nc.dram_tensor(name, shape, dt, kind="Internal").ap()

        h0_tab = dram("h0_tab", (NPAD, D))
        z_tab = dram("z_tab", (NPAD, ROW))
        x1_tab = dram("x1_tab", (NPAD, D))
        hin_tab = dram("hin_tab", (NPAD, D))
        er_start = dram("er_start", (EPAD, HEADS))
        er_rows = dram("er_rows", (NCH, HEADS, CE))
        pen_rows = dram("pen_rows", (NCH, HEADS, CT, P + 2))
        same_tab = dram("same_tab", (NCH, CE))
        chain_tab = dram("chain_tab", (NCH, 2 * CT))
        base_tab = dram("base_tab", (NCH, QUADS), I32)

        acc = sb("acc", [P, ACC_TILES * AW])
        slots = sb("slots", [P, SLOTS, CT, ROW])
        onehot = sb("onehot", [P, SB, QT, WIN])
        src_t = sb("src_t", [P, NCH * CT], I32)
        negrel = sb("negrel", [P, NCH * CT])
        idx = sb("idx", [P, SLOTS, CT], I32)
        base_row = sb("base_row", [1, NCH * QUADS], I32)
        rounds_i = sb("rounds_i", [1, 1], I32)
        first_dst = sb("first_dst", [NCH, 1], I32)
        seg_pos = sb("seg_pos", [P, NT], I32)
        ident = sb("ident", [P, P])
        ones = sb("ones", [P, P])
        before = sb("before", [P, P])
        lanes = sb("lanes", [P, WIN])
        tile_mask = sb("tile_mask", [ROWS, CT])
        head_mask = sb("head_mask", [ROWS, HEADS])
        head_rows = sb("head_rows", [HEADS, ROWS])
        first_rows = sb("first_rows", [ROWS, HEADS])
        one_c = sb("one_c", [P, 1])
        eps_c = sb("eps_c", [P, 1])
        wsT = sb("wsT", [P, 2, D])
        wnT = sb("wnT", [P, 2, D])
        wz = [sb(f"wz{i}", [P, 2, D + 2 * HEADS]) for i in range(2)]
        attn = [sb(f"attn{i}", [P, 2, 2 * HEADS]) for i in range(2)]
        bias = [sb(f"bias{i}", [P, D]) for i in range(3)]
        pen = sb("pen", [ROWS, SLOTS, P + 2])
        er = sb("er", [ROWS, SLOTS, P])
        chain_pen = sb("chain_pen", [HEADS, SLOTS, 2 * CT])
        el_cols = sb("el_cols", [P, ROWS])
        scan_f = sb("scan_f", [ROWS, P])
        scan_b = sb("scan_b", [ROWS, P])
        ends = sb("ends", [ROWS, 2, CT])
        carry = sb("carry", [HEADS, 2 * CT + 4])
        scrap = sb("scrap", [ROWS, 2, CT])
        edge_in = sb("edge_in", [ROWS, 2])
        logit = sb("logit", [ROWS, 2, P])
        old = sb("old", [ROWS, 2])
        wexp = sb("wexp", [ROWS, P + 1])
        wrow = sb("wrow", [ROWS, P + 1])
        rm1 = sb("rm1", [1, HEADS])
        rescale = sb("rescale", [P, HEADS])
        mv = sb("mv", [P, NT, 2])
        stats = sb("stats", [P, GROUP, 6])
        mvg = sb("mvg", [P, GROUP, 2])
        rstd = sb("rstd", [P, NT])
        nbias = sb("nbias", [P, NT])
        deg_inv = sb("deg_inv", [P, NT])
        deg = sb("deg", [P, NT])
        w_inv = sb("w_inv", [P, NT * HEADS])
        er_stage = sb("er_stage", [P, GROUP, HEADS])
        pos_stage = sb("pos_stage", [P, GROUP], I32)
        er_init = sb("er_init", [NCH, ROW])

        flat = slots[:, :, :, :].rearrange("p a b c -> p (a b c)")
        H = HALF * D
        in_a = flat[:, 0:2 * H].rearrange("p (s t d) -> p s t d", s=2, t=HALF)
        in_b = flat[:, 2 * H:4 * H].rearrange("p (s t d) -> p s t d", s=2, t=HALF)
        z_out = flat[:, 4 * H:4 * H + 2 * HALF * ROW].rearrange("p (s t d) -> p s t d", s=2, t=HALF)
        hot = onehot[:, :, :, :].rearrange("p a b c -> p (a b c)")
        lhs = hot[:, 0:1024].rearrange("p (s c) -> p s c", s=2)
        tmp_a = hot[:, 1024:1536].rearrange("p (s c) -> p s c", s=2)
        tmp_b = hot[:, 1536:2048].rearrange("p (s c) -> p s c", s=2)
        accf = acc[:, :]

        def loop(eng, start, end):
            return nc.Fori(start, end, engines=bass.OrderedEngineSet([eng.engine]), hint_back_edge=True)

        def acc_cols(tile, lo, n):
            return accf[:, bass.ds(tile * AW + lo, n)]

        pair = [pb(f"pair{i}", [P, 2, 512]) for i in range(2)]
        ps_x = pb("ps_x", [P, 512])
        ps_w = pb("ps_w", [P, 512])
        ps_c = pb("ps_c", [P, 512])
        ps_d = pb("ps_d", [P, 512])

        pool_turn = sem("pool_turn")
        dve_turn = sem("dve_turn")
        pe_turn = sem("pe_turn")

        s_masks = sem("s_masks")
        s_wload = sem("s_wload")
        s_wzero = sem("s_wzero")
        raw = [in_a[:, i, :, :].rearrange("p t d -> p (t d)")[:, 0:2 * D]
               .rearrange("p (c d) -> p c d", c=2) for i in range(2)]
        wT = in_b[:, 0, :, :].rearrange("p t d -> p (t d)")[:, 0:2 * D].rearrange("p (c d) -> p c d", c=2)
        lane_i = in_b[:, 1, 0, :].bitcast(I32)
        with nc.Block() as block:
            @block.gpsimd
            def _(pool):
                pool.memset(ident[:, :], 0.0)
                pool.memset(before[:, :], 1.0)
                pool.memset(ones[:, :], 1.0)
                pool.memset(one_c[:, :], 1.0)
                pool.memset(eps_c[:, :], LN_EPS)
                pool.iota(lane_i, [[1, WIN]], base=0, channel_multiplier=0).then_inc(s_masks, 1)
                pool.wait_ge(s_masks, 1)
                pool.affine_select(out=ident[:, :], in_=ident[:, :], compare_op=ALU.not_equal, fill=1.0,
                                   base=0, pattern=[[-1, P]], channel_multiplier=1)
                pool.affine_select(out=before[:, :], in_=before[:, :], compare_op=ALU.is_gt, fill=0.0,
                                   base=0, pattern=[[1, P]], channel_multiplier=-1)
                pool.tensor_copy(lanes[:, :], lane_i)

            @block.vector
            def _(dve):
                nc.vector.memset(attn[0][:, :, :], 0.0).then_inc(s_wzero, 1)
                nc.vector.memset(attn[1][:, :, :], 0.0).then_inc(s_wzero, 1)

            @block.sync
            def _(sp):
                n = 0
                for w, to in ((w_self, raw[0]), (w_neigh, raw[1]),
                              (w0, wz[0][:, :, 0:D]), (w1, wz[1][:, :, 0:D])):
                    sp.dma_start(to, w.rearrange("(c p) d -> p c d", p=P)).then_inc(s_wload, 16)
                    n += 16
                for i, b in enumerate((b_self, b0, b1)):
                    sp.dma_start(bias[i][:, :], b.unsqueeze(0).broadcast_to([P, D])).then_inc(s_wload, 16)
                    n += 16
                sp.wait_ge(s_wzero, 2)
                with nc.allow_non_contiguous_dma(reason="columns of the attention vectors, once"):
                    for i, pairs in enumerate(((al0, ar0), (al1, ar1))):
                        for j, a in enumerate(pairs):
                            for h in range(HEADS):
                                lo = (h % 2) * HD
                                c = j * HEADS + h
                                sp.dma_start(attn[i][lo:lo + HD, h // 2, c:c + 1],
                                             a[h, :].unsqueeze(1)).then_inc(s_wload, 16)
                                n += 16
                sp.wait_ge(s_wload, n)

        s_mk = sem("s_mk")
        s_wt = sem("s_wt")
        s_wc = sem("s_wc")
        s_wv = sem("s_wv")
        jobs = [("T", raw[0], wsT), ("T", raw[1], wnT), ("Z", wz[0], 0), ("Z", wz[1], 1)]
        with nc.Block() as block:
            @block.vector
            def _(dve):
                sq = ident[0:ROWS, 0:ROWS]
                nc.vector.tensor_reduce(out=tile_mask[:, :], in_=sq.rearrange("p (h t) -> p t h", h=HEADS),
                                        axis=AX.X, op=ALU.add)
                nc.vector.tensor_reduce(out=head_mask[:, :], in_=sq.rearrange("p (h t) -> p h t", h=HEADS),
                                        axis=AX.X, op=ALU.add)
                nc.vector.tensor_copy(head_rows[:, :].rearrange("p (h t) -> p h t", h=HEADS),
                                      ident[0:HEADS, 0:HEADS].unsqueeze(2).broadcast_to([HEADS, HEADS, CT]))
                nc.vector.tensor_copy(first_rows[:, :],
                                      sq.rearrange("p (h t) -> p h t", h=HEADS)[:, :, 0])
                for n, (kind, _, to) in enumerate(jobs):
                    dve.wait_ge(s_wt, n + 1)
                    if n >= 3:
                        dve.wait_ge(s_wv, n - 2)
                    view = (to if kind == "T" else wT)[:, :, :]
                    nc.vector.tensor_copy(view.rearrange("p c d -> p (c d)"), ps_x[:, :]).then_inc(s_wc, 1)
                    if kind == "Z":
                        dve.wait_ge(s_wv, to + 1)
                        nc.vector.tensor_copy(wz[to][:, :, D:D + 2 * HEADS],
                                              ps_w[:, 0:16].rearrange("p (c a) -> p c a", c=2)).then_inc(s_mk, 1)

            @block.tensor
            def _(pe):
                for n, (kind, w, to) in enumerate(jobs):
                    if n:
                        pe.wait_ge(s_wc, n)
                    for a in range(2):
                        for b in range(2):
                            last = nc.tensor.transpose(ps_x[:, b * D + a * P:b * D + a * P + P],
                                                       w[:, a, b * P:b * P + P], ident[:, :])
                    last.then_inc(s_wt, 1)
                    if kind == "Z":
                        pe.wait_ge(s_wc, n + 1)
                        if to:
                            pe.wait_ge(s_mk, to)
                        for a in range(2):
                            for b in range(2):
                                last = nc.tensor.matmul(ps_w[:, a * 8:a * 8 + 8], wT[:, b, a * P:a * P + P],
                                                        attn[to][:, b, :], start=(b == 0), stop=(b == 1))
                        last.then_inc(s_wv, 1)

        cols = [0]

        def edge_buf(n, dt=F32):
            v = accf[0:NCH, cols[0]:cols[0] + n]
            cols[0] += n
            return v if dt is F32 else v.bitcast(dt)

        d_i = edge_buf(CE + 2, I32)
        s_i = edge_buf(CE, I32)
        d_f = edge_buf(CE + 2)
        s_f = edge_buf(CE)
        start_f = edge_buf(CE + 1)
        pen_f = edge_buf(CE + 1)
        same_f = edge_buf(CE)
        ch_f = edge_buf(2 * CT)
        b_first = edge_buf(QUADS, I32)
        b_last = edge_buf(QUADS, I32)
        span_i = edge_buf(QUADS, I32)
        span_f = edge_buf(QUADS)
        span_m = edge_buf(1)
        d_last = edge_buf(QUADS, I32)
        whole, rest = EDGES // CE, EDGES % CE
        s_pad = sem("s_pad")
        s_eload = sem("s_eload")
        s_ev = sem("s_ev")
        s_estore = sem("s_estore")
        zero_view = accf[:, 16384:16384 + EPAD * HEADS // P]
        with nc.Block() as block:
            @block.vector
            def _(dve):
                nc.vector.memset(d_i, PAD_NODE).then_inc(s_pad, 1)
                nc.vector.memset(d_last, PAD_NODE).then_inc(s_pad, 1)
                nc.vector.memset(s_i, 0).then_inc(s_pad, 1)
                nc.vector.memset(zero_view, 0.0).then_inc(s_pad, 1)
                dve.wait_ge(s_pad, 1)
                nc.vector.memset(d_i[0:1, 0:1], -1).then_inc(s_pad, 1)

            @block.sync
            def _(sp):
                sp.wait_ge(s_pad, 5)
                rows = bass.AP(tensor=dst.tensor, offset=CE - 1, ap=[[CE, whole - 1], [1, CE + 2]])
                sp.dma_start(d_i[1:whole, :], rows).then_inc(s_eload, 16)
                sp.dma_start(d_i[0:1, 1:CE + 2], dst[0:CE + 1].unsqueeze(0)).then_inc(s_eload, 16)
                sp.dma_start(d_i[whole:whole + 1, 0:rest + 1],
                             dst[whole * CE - 1:EDGES].unsqueeze(0)).then_inc(s_eload, 16)
                sp.dma_start(s_i[0:whole, :], src[0:whole * CE].rearrange("(c e) -> c e", e=CE)).then_inc(s_eload, 16)
                sp.dma_start(s_i[whole:whole + 1, 0:rest], src[whole * CE:EDGES].unsqueeze(0)).then_inc(s_eload, 16)
                sp.dma_start(er_start.rearrange("(p e) h -> p (e h)", p=P), zero_view).then_inc(s_eload, 16)
                with nc.allow_non_contiguous_dma(reason="an edge per quad, once"):
                    sp.dma_start(d_last[0:whole, :], bass.AP(tensor=dst.tensor, offset=QE - 1,
                                                             ap=[[CE, whole], [QE, QUADS]])).then_inc(s_eload, 16)
                    sp.dma_start(d_last[whole:whole + 1, 0:rest // QE],
                                 bass.AP(tensor=dst.tensor, offset=whole * CE + QE - 1,
                                         ap=[[CE, 1], [QE, rest // QE]])).then_inc(s_eload, 16)
                sp.dma_start(d_last[whole:whole + 1, rest // QE:rest // QE + 1],
                             dst[EDGES - 1:EDGES].unsqueeze(0)).then_inc(s_eload, 16)
                sp.wait_ge(s_eload, 144)

        with nc.Block() as block:
            @block.vector
            def _(dve):
                V = nc.vector
                step = [0]

                def then(ins):
                    step[0] += 1
                    ins.then_inc(s_ev, 1)
                    dve.wait_ge(s_ev, step[0])

                V.tensor_copy(s_f, s_i)
                V.tensor_single_scalar(b_first, d_i[:, 1:1 + CE:QE], 7, op=ALU.logical_shift_right)
                V.tensor_single_scalar(b_last, d_last, 7, op=ALU.logical_shift_right)
                V.tensor_copy(first_dst[:, :], d_i[:, 1:2])
                then(V.tensor_copy(d_f, d_i))
                then(V.tensor_tensor(start_f, d_f[:, 0:CE + 1], d_f[:, 1:CE + 2], ALU.not_equal))
                V.tensor_scalar(pen_f, start_f, NEG, None, ALU.mult)
                V.tensor_scalar(same_f, start_f[:, 0:CE], -1.0, 1.0, ALU.mult, ALU.add)
                V.tensor_tensor(ch_f[:, 0:CT], d_f[:, P:CE + 1:P], d_f[:, 0:CE:P], ALU.not_equal)
                then(V.tensor_tensor(ch_f[:, CT:2 * CT], d_f[:, 1:CE + 1:P], d_f[:, P + 1:CE + 2:P], ALU.not_equal))
                V.tensor_scalar(ch_f, ch_f, NEG, None, ALU.mult)
                then(V.tensor_tensor(span_i, b_last, b_first, ALU.subtract))
                then(V.tensor_copy(span_f, span_i))
                V.tensor_reduce(out=span_m, in_=span_f, axis=AX.X, op=ALU.max)

        s_e2 = sem("s_e2")
        s_eT = sem("s_eT")
        s_sT = sem("s_sT")
        s_dT = sem("s_dT")
        s_sp = sem("s_sp")
        with nc.Block() as block:
            @block.sync
            def _(sp):
                pv = pen_f[:, 0:CE].rearrange("c (t p) -> c t p", p=P)
                n = 0
                for h in range(HEADS):
                    sp.dma_start(pen_rows[:, h, :, 0:P], pv).then_inc(s_estore, 16)
                    with nc.allow_non_contiguous_dma(reason="a column per tile, once"):
                        for col in (P, P + 1):
                            sp.dma_start(pen_rows[:, h, :, col:col + 1],
                                         pen_f[:, P:CE + 1:P].unsqueeze(2)).then_inc(s_estore, 16)
                    n += 48
                sp.dma_start(same_tab, same_f).then_inc(s_estore, 16)
                sp.dma_start(chain_tab, ch_f).then_inc(s_estore, 16)
                sp.dma_start(base_tab, b_first).then_inc(s_estore, 16)
                sp.wait_ge(s_estore, n + 48)
                row = base_tab.rearrange("c q -> (c q)").unsqueeze(0)
                sp.dma_start(base_row[:, :], row).then_inc(s_e2, 16)
                sp.dma_start(in_a[:, 0, 0:2, :].rearrange("p t d -> p (t d)")[:, 0:NCH * QUADS].bitcast(I32),
                             row.broadcast_to([P, NCH * QUADS])).then_inc(s_e2, 16)
                sp.wait_ge(s_e2, 32)

            @block.tensor
            def _(pe):
                banks = [pair[0], pair[1]]
                for j in range(2 * CT):
                    t = j // 2
                    buf = (s_f, d_f)[j % 2]
                    lo = t * P + (j % 2)
                    if j >= 2:
                        pe.wait_ge((s_sT, s_dT)[j % 2], j // 2)
                    nc.tensor.transpose(banks[j % 2][:, 0, 0:NCH], buf[:, lo:lo + P],
                                        ident[0:NCH, 0:NCH]).then_inc(s_eT, 1)
                nc.tensor.transpose(ps_x[0:1, 0:NCH], span_m, ident[0:NCH, 0:NCH]).then_inc(s_eT, 1)

            @block.vector
            def _(dve):
                V = nc.vector
                for j in range(2 * CT):
                    dve.wait_ge(s_eT, j + 1)
                    to, done = ((src_t, s_sT), (negrel, s_dT))[j % 2]
                    V.tensor_copy(to[:, :].rearrange("p (c t) -> p c t", t=CT)[:, :, j // 2],
                                  pair[j % 2][:, 0, 0:NCH]).then_inc(done, 1)
                dve.wait_ge(s_eT, 2 * CT + 1)
                V.tensor_reduce(out=old[0:1, 0:1], in_=ps_x[0:1, 0:NCH], axis=AX.X, op=ALU.max).then_inc(s_sp, 1)
                dve.wait_ge(s_sp, 1)
                V.tensor_copy(rounds_i[:, :], old[0:1, 0:1]).then_inc(s_sp, 1)
                dve.wait_ge(s_sp, 2)
                V.tensor_single_scalar(rounds_i[:, :], rounds_i[:, :], 1, op=ALU.logical_shift_right).then_inc(s_sp, 1)
                dve.wait_ge(s_sp, 3)
                V.tensor_copy(old[0:1, 0:1], rounds_i[:, :]).then_inc(s_sp, 1)
                dve.wait_ge(s_sp, 4)
                V.tensor_scalar(rounds_i[:, :], old[0:1, 0:1], 1.0, None, ALU.add).then_inc(s_sp, 1)
                base_b = in_a[:, 0, 0:2, :].rearrange("p t d -> p (t d)")[:, 0:NCH * QUADS]
                base_f = in_a[:, 1, 0:2, :].rearrange("p t d -> p (t d)")[:, 0:NCH * QUADS]
                dve.wait_ge(s_e2, 32)
                V.tensor_copy(base_f, base_b.bitcast(I32)).then_inc(s_sp, 1)
                dve.wait_ge(s_sp, 6)
                V.tensor_scalar(base_f, base_f, float(P), None, ALU.mult).then_inc(s_sp, 1)
                dve.wait_ge(s_sp, 7)
                dve.wait_ge(s_dT, CT)
                rel = negrel[:, :].rearrange("p (q t) -> p q t", t=QT)
                V.tensor_tensor(rel, base_f.unsqueeze(2).broadcast_to([P, NCH * QUADS, QT]), rel,
                                ALU.subtract).then_inc(s_sp, 1)

        def half_load(sp, tab, buf, g, half, done, rows_limit):
            if rows_limit:
                full = (NT - HALF) * P
                n = (HALF - 1) * P
                sp.dma_start(buf[:, half, 0:HALF - 1, :],
                             tab[full:full + n, :].rearrange("(t p) d -> p t d", p=P)).then_inc(done, 16)
                sp.dma_start(buf[0:LAST_ROWS, half, HALF - 1, :], tab[full + n:NODES, :]).then_inc(done, 16)
            else:
                v = tab[bass.ds((g * 2 + half) * HALF * P, HALF * P), :]
                sp.dma_start(buf[:, half, :, :], v.rearrange("(t p) d -> p t d", p=P)).then_inc(done, 16)

        def store_rows(tab, g, half):
            return tab[bass.ds((g * 2 + half) * HALF * P, HALF * P), :].rearrange("(t p) d -> p t d", p=P)

        s_x = [sem(f"s_xload{i}") for i in range(2)]
        s_xz = sem("s_xz")
        s_h0 = [sem(f"s_h0out{i}") for i in range(2)]
        s_bn = sem("s_bn")
        s_agg = sem("s_agg")
        s_std = sem("s_std")
        s_rs = sem("s_rs")
        s_relu = sem("s_relu")
        with nc.Block() as block:
            @block.gpsimd
            def _(pool):
                pool.memset(in_a[:, :, :, :], 0.0).then_inc(s_xz, 1)

            @block.sync
            def _(sp):
                sp.wait_ge(s_xz, 1)

                def load(g, half, last=False):
                    half_load(sp, x, in_a, g, half, s_x[half], last)

                def store(g, half):
                    sp.wait_ge(s_relu, g * GROUP + half * HALF + HALF)
                    sp.dma_start(store_rows(h0_tab, g, half), in_b[:, half, :, :]).then_inc(s_h0[half], 16)

                load(0, 0)
                load(0, 1)
                with loop(sp, 0, NG - 2) as g:
                    for half in range(2):
                        store(g, half)
                        load(g + 1, half)
                store(NG - 2, 0)
                load(NG - 1, 0)
                store(NG - 2, 1)
                load(NG - 1, 1, last=True)
                store(NG - 1, 0)
                store(NG - 1, 1)
                sp.wait_ge(s_h0[0], 16 * NG)
                sp.wait_ge(s_h0[1], 16 * NG)

            @block.vector
            def _(dve):
                V = nc.vector

                def half_stats(g, half, last=False):
                    t0 = half * HALF
                    dve.wait_ge(s_x[half], 16 * g + 16 + (16 if last else 0))
                    for j in range(HALF):
                        V.bn_stats(stats[:, t0 + j, :], in_a[:, half, j, :]).then_inc(s_bn, 1)
                    dve.wait_ge(s_bn, g * GROUP + t0 + HALF)
                    dve.sem_inc(dve_turn, 1)
                    for j in range(HALF):
                        V.bn_aggr(mvg[:, t0 + j, :], stats[:, t0 + j, :]).then_inc(s_agg, 1)
                    dve.wait_ge(s_std, g * 2 + half + 1)
                    V.reciprocal(rstd[:, t0:t0 + HALF], rstd[:, t0:t0 + HALF]).then_inc(s_rs, 1)
                    dve.wait_ge(s_rs, g * 4 + half * 2 + 1)
                    V.scalar_tensor_tensor(out=nbias[:, t0:t0 + HALF], in0=mvg[:, t0:t0 + HALF, 0], scalar=-1.0,
                                           in1=rstd[:, t0:t0 + HALF], op0=ALU.mult, op1=ALU.mult).then_inc(s_rs, 1)

                half_stats(0, 0)
                half_stats(0, 1)
                with loop(dve, 1, NG - 1) as g:
                    for half in range(2):
                        half_stats(g, half)
                half_stats(NG - 1, 0)
                half_stats(NG - 1, 1, last=True)

            @block.scalar
            def _(act):
                def half_relu(g, half, wait_store):
                    t0 = half * HALF
                    act.wait_ge(s_agg, g * GROUP + t0 + HALF)
                    nc.scalar.activation(rstd[:, t0:t0 + HALF], mvg[:, t0:t0 + HALF, 1], ACT.Sqrt,
                                         bias=eps_c[:, 0:1]).then_inc(s_std, 1)
                    act.wait_ge(s_rs, g * 4 + half * 2 + 2)
                    if wait_store:
                        act.wait_ge(s_h0[half], 16 * g)
                    for j in range(HALF):
                        nc.scalar.activation(in_b[:, half, j, :], in_a[:, half, j, :], ACT.Relu,
                                             bias=nbias[:, t0 + j:t0 + j + 1],
                                             scale=rstd[:, t0 + j:t0 + j + 1]).then_inc(s_relu, 1)

                for half in range(2):
                    half_relu(0, half, False)
                with loop(act, 1, NG) as g:
                    for half in range(2):
                        half_relu(g, half, True)

        rounds = nc.values_load(rounds_i[0:1, 0:1], min_val=1, max_val=NT)

        def aggregate(name, table, gat):
            width = ROW if gat else D
            cols_in = AW if gat else D + 1
            s = {}

            def sm(n, count=None):
                s[n] = (stage_sem(f"agg_{n}") if count is None else
                        [stage_sem(f"agg_{n}{i}") for i in range(count)])

            for n in ("onehot", "sums", "added", "wz0", "base"):
                sm(n)
            sm("idx", SLOTS)
            s["rows"] = [sem(f"{name}_rows{i}") for i in range(SLOTS)]
            if gat:
                sm("tables", SLOTS)
                for n in ("el_cols", "el_rows", "fwd_local", "bwd_local", "tile_last", "tile_first", "tile_ends",
                          "carry_old", "carry_fwd", "carry_bwd", "carry_rows", "in_left", "in_right",
                          "fwd", "bwd", "seg_max", "e", "e_max", "leaky", "old_e", "old_leaky", "old_arg",
                          "arg", "weights", "w_cols", "r_row", "rm1", "r_cols", "rescale", "rescaled",
                          "scaled"):
                    sm(n)

            with nc.Block() as block:
                @block.vector
                def _(dve):
                    if not gat:
                        nc.vector.memset(accf, 0.0)
                        nc.vector.memset(slots[:, :, :, D:D + 1], 1.0)

                @block.gpsimd
                def _(pool):
                    pool.memset(carry[:, :], NEG)

            with nc.Fori(0, rounds) as rnd:
                with nc.Block() as block:
                    @block.sync
                    def _(sp):
                        n0 = sp.snap(rnd * NCH)

                        def load(g, k, peeled):
                            n = SLOTS * g + k
                            if not peeled:
                                sp.wait_ge(s["sums"], QUADS * (n0 + n) - QUADS * SLOTS + 1)
                            sp.dma_start(idx[:, k, :], src_t[:, bass.ds(n * CT, CT)]).then_inc(s["idx"][k], 16)
                            if gat:
                                if not peeled:
                                    sp.wait_ge(s["weights"], n0 + n - (SLOTS - 1))
                                sp.dma_start(pen[:, k, :], pen_rows[bass.ds(n, 1), :, :, :]
                                             .rearrange("c h t p -> (c h t) p")).then_inc(s["tables"][k], 16)
                                sp.dma_start(er[:, k, :], er_rows[bass.ds(n, 1), :, :]
                                             .rearrange("c h (t p) -> (c h t) p", p=P)).then_inc(s["tables"][k], 16)
                                sp.dma_start(chain_pen[:, k, :], chain_tab[bass.ds(n, 1), :]
                                             .broadcast_to([HEADS, 2 * CT])).then_inc(s["tables"][k], 16)

                        for k in range(SLOTS):
                            load(0, k, True)
                        with loop(sp, 1, ITER) as g:
                            for k in range(SLOTS):
                                load(g, k, False)
                        for k in range(TAIL):
                            load(ITER, k, False)

                    @block.gpsimd
                    def _(pool):
                        turn0 = [pool.snap(rnd * u) for u in USES]
                        n0 = pool.snap(rnd * NCH)

                        def gather(g, k, peeled):
                            n = SLOTS * g + k
                            pool.wait_ge(s["idx"][k], 16 * (turn0[k] + g) + 16)
                            pool.sem_inc(pool_turn, 1)
                            for q in range(QUADS):
                                if not peeled:
                                    pool.wait_ge(s["sums"], QUADS * (n0 + n) - QUADS * SLOTS + q + 1)
                                    pool.sem_inc(pool_turn, 1)
                                for t in range(q * QT, q * QT + QT):
                                    pool.indirect_dma_start(
                                        slots[:, k, t, 0:width], None, table,
                                        bass.IndirectOffsetOnAxis(ap=idx[:, k, t:t + 1], axis=0),
                                    ).then_inc(s["rows"][k], 16)

                        for k in range(SLOTS):
                            gather(0, k, True)
                        with loop(pool, 1, ITER) as g:
                            for k in range(SLOTS):
                                gather(g, k, False)
                        for k in range(TAIL):
                            gather(ITER, k, False)

                    @block.scalar
                    def _(act):
                        n0 = act.snap(rnd * NCH)

                        def one_hot(g, k, q, free):
                            n = SLOTS * g + k
                            b = (QUADS * k + q) % SB
                            if free is None or free >= SB:
                                act.wait_ge(s["sums"], QUADS * (n0 + n) + q - SB + 1)
                            for t in range(QT):
                                col = n * CT + q * QT + t
                                nc.scalar.activation(onehot[:, b, t, :], lanes[:, :], ACT.Abs,
                                                     bias=negrel[:, bass.ds(col, 1)]).then_inc(s["wz0"], 1)
                            act.wait_ge(s["wz0"], CT * (n0 + n) + q * QT + QT)
                            nc.scalar.activation(onehot[:, b, :, :], onehot[:, b, :, :], ACT.Relu,
                                                 bias=one_c[:, 0:1], scale=-1.0).then_inc(s["onehot"], 1)

                        def weigh(n):
                            act.wait_ge(s["arg"], n + 1)
                            act.wait_ge(s["old_arg"], n + 1)
                            nc.scalar.activation(wrow[:, :], wexp[:, :], ACT.Exp).then_inc(s["weights"], 1)

                        def chunk(g, k, nth=None, more=True):
                            n = SLOTS * g + k
                            g1, k1 = (g, k + 1) if k + 1 < SLOTS else (g + 1, 0)
                            free = (lambda i: None) if nth is None else (lambda i: nth * QUADS + i)
                            one_hot(g, k, 3, free(3))
                            if more:
                                one_hot(g1, k1, 0, free(4))
                                if gat:
                                    weigh(n0 + n + 1)
                                one_hot(g1, k1, 1, free(5))
                                one_hot(g1, k1, 2, free(6))

                        for q in range(3):
                            one_hot(0, 0, q, q)
                        if gat:
                            weigh(n0)
                        for k in range(SLOTS):
                            chunk(0, k, nth=k)
                        with loop(act, 1, ITER) as g:
                            for k in range(SLOTS):
                                chunk(g, k)
                        for k in range(TAIL):
                            chunk(ITER, k, more=(k + 1 < TAIL))

                    @block.tensor
                    def _(pe):
                        T = nc.tensor
                        n0 = pe.snap(rnd * NCH)

                        def quad(g, k, q, nth, between=None):
                            n = SLOTS * g + k
                            qn = QUADS * (n0 + n) + q
                            b = (QUADS * k + q) % SB
                            pe.wait_ge(s["onehot"], qn + 1)
                            if gat:
                                pe.wait_ge(s["scaled"], qn + 1)
                            else:
                                pe.wait_ge(s["rows"][k], 16 * CT * g + 16 * CT)
                            if nth is None or nth * QUADS + q >= 2:
                                pe.wait_ge(s["added"], qn - 1)
                            for w in range(2):
                                if w and between:
                                    between()
                                for t in range(QT):
                                    last = T.matmul(pair[q % 2][:, w, 0:cols_in],
                                                    onehot[:, b, t, w * P:w * P + P],
                                                    slots[:, k, q * QT + t, 0:cols_in],
                                                    start=(t == 0), stop=(t == QT - 1))
                            last.then_inc(s["sums"], 1)

                        def el_rows(n):
                            pe.wait_ge(s["el_cols"], n + 1)
                            pe.sem_inc(pe_turn, 1)
                            T.transpose(ps_x[0:ROWS, 0:P], el_cols[:, :], ident[:, :]).then_inc(s["el_rows"], 1)

                        def tile_ends(n):
                            pe.wait_ge(s["tile_last"], n + 1)
                            pe.wait_ge(s["tile_first"], n + 1)
                            pe.sem_inc(pe_turn, 1)
                            T.matmul(ps_c[0:HEADS, 0:2 * CT], head_mask[:, :],
                                     ends[:, :, :].rearrange("p a t -> p (a t)"),
                                     start=True, stop=True).then_inc(s["tile_ends"], 1)

                        def carry_rows(n):
                            pe.wait_ge(s["carry_fwd"], n + 1)
                            pe.wait_ge(s["carry_bwd"], n + 1)
                            T.matmul(ps_c[0:ROWS, 64:64 + 2 * CT], head_rows[:, :],
                                     carry[:, :].rearrange("p (a t) -> p a t", a=2)[:, :, 0:CT],
                                     start=True, stop=True).then_inc(s["carry_rows"], 1)

                        def w_cols(n):
                            pe.wait_ge(s["weights"], n + 1)
                            pe.sem_inc(pe_turn, 1)
                            T.transpose(ps_w[:, 0:ROWS], wrow[:, 0:P], ident[0:ROWS, 0:ROWS]).then_inc(s["w_cols"], 1)
                            T.matmul(ps_c[0:1, 128:128 + HEADS], wrow[:, P:P + 1], first_rows[:, :],
                                     start=True, stop=True).then_inc(s["r_row"], 1)

                        def r_cols(k, n):
                            pe.wait_ge(s["rm1"], n + 1)
                            pe.wait_ge(s["onehot"], QUADS * n + 1)
                            T.matmul(ps_d[:, 0:HEADS], onehot[0:1, (QUADS * k) % SB, 0, 0:P], rm1[:, :],
                                     start=True, stop=True).then_inc(s["r_cols"], 1)

                        def chunk(g, k, nth=None, more=True):
                            n = n0 + SLOTS * g + k
                            g1, k1 = (g, k + 1) if k + 1 < SLOTS else (g + 1, 0)
                            more = more and gat
                            quad(g, k, 0, nth)
                            if more:
                                el_rows(n + 1)
                            quad(g, k, 1, nth, (lambda: tile_ends(n + 1)) if more else None)
                            if more:
                                carry_rows(n + 1)
                            quad(g, k, 2, nth)
                            quad(g, k, 3, nth, (lambda: w_cols(n + 1)) if more else None)
                            if more:
                                r_cols(k1, n + 1)

                        if gat:
                            el_rows(n0)
                            tile_ends(n0)
                            carry_rows(n0)
                            w_cols(n0)
                            r_cols(0, n0)
                        for k in range(SLOTS):
                            chunk(0, k, nth=k)
                        with loop(pe, 1, ITER) as g:
                            for k in range(SLOTS):
                                chunk(g, k)
                        for k in range(TAIL):
                            chunk(ITER, k, more=(k + 1 < TAIL))

                    @block.vector
                    def _(dve):
                        V = nc.vector
                        turn0 = [dve.snap(rnd * u) for u in USES]
                        n0 = dve.snap(rnd * NCH)

                        def add(g, k, q, first):
                            qn = QUADS * (n0 + SLOTS * g + k) + q
                            base = dve.value_load(base_row[0:1, bass.ds(QUADS * (SLOTS * g + k) + q, 1)],
                                                  min_val=0, max_val=NT)
                            dve.wait_ge(s["sums"], qn + 1)
                            if not (first and k == 0 and q == 0):
                                dve.wait_ge(s["added"], qn)
                            if gat and q == 0:
                                dve.wait_ge(s["rescaled"], n0 + SLOTS * g + k + 1)
                            to = accf[:, bass.ds(base * AW, 2 * AW)].rearrange("p (w c) -> p w c", w=2)[:, :, 0:cols_in]
                            V.tensor_tensor(to, to, pair[q % 2][:, :, 0:cols_in], ALU.add).then_inc(s["added"], 1)

                        def scans(k, left, right, out_f, out_b, done_f, done_b):
                            V.tensor_tensor_scan(out_f[:, :], pen[:, k, 0:P], ps_x[0:ROWS, 0:P], left,
                                                 ALU.add, ALU.max).then_inc(s[done_f], 1)
                            V.tensor_tensor_scan(out_b[:, P - 1::-1], pen[:, k, P:0:-1], ps_x[0:ROWS, P - 1::-1], right,
                                                 ALU.add, ALU.max).then_inc(s[done_b], 1)

                        def pack_el(g, k, n):
                            dve.wait_ge(s["rows"][k], 16 * CT * g + 16 * CT)
                            V.tensor_copy(el_cols[:, :].rearrange("p (h t) -> p h t", h=HEADS),
                                          slots[:, k, :, AW:AW + HEADS].rearrange("p t h -> p h t")
                                          ).then_inc(s["el_cols"], 1)

                        def local_maxima(g, k, n):
                            dve.wait_ge(s["el_rows"], n + 1)
                            dve.wait_ge(s["tables"][k], 48 * (turn0[k] + g) + 48)
                            scans(k, NEG, NEG, scan_f, scan_b, "fwd_local", "bwd_local")
                            dve.wait_ge(s["fwd_local"], n + 1)
                            V.tensor_scalar(ends[:, 0, :], tile_mask[:, :], scan_f[:, P - 1:P], None,
                                            ALU.mult).then_inc(s["tile_last"], 1)
                            dve.wait_ge(s["bwd_local"], n + 1)
                            V.tensor_scalar(ends[:, 1, :], tile_mask[:, :], scan_b[:, 0:1], None,
                                            ALU.mult).then_inc(s["tile_first"], 1)

                        def carries(k, n, peeled=False):
                            dve.wait_ge(s["tile_ends"], n + 1)
                            if not peeled:
                                dve.wait_ge(s["carry_fwd"], n)
                            V.tensor_copy(carry[:, 0:1], carry[:, CT:CT + 1]).then_inc(s["carry_old"], 1)
                            V.tensor_tensor_scan(carry[:, 2 * CT:CT:-1], chain_pen[:, k, 2 * CT - 1:CT - 1:-1],
                                                 ps_c[0:HEADS, 2 * CT - 1:CT - 1:-1], NEG,
                                                 ALU.add, ALU.max).then_inc(s["carry_bwd"], 1)
                            dve.wait_ge(s["carry_old"], n + 1)
                            V.tensor_tensor_scan(carry[:, 1:CT + 1], chain_pen[:, k, 0:CT], ps_c[0:HEADS, 0:CT],
                                                 carry[:, 0:1], ALU.add, ALU.max).then_inc(s["carry_fwd"], 1)

                        def exponents(k, n):
                            dve.wait_ge(s["carry_rows"], n + 1)
                            for side, done in ((0, "in_left"), (1, "in_right")):
                                V.tensor_tensor_reduce(out=scrap[:, side, :], in0=ps_c[0:ROWS, 64 + side * CT:64 + side * CT + CT],
                                                       in1=tile_mask[:, :], scale=1.0, scalar=0.0, op0=ALU.mult,
                                                       op1=ALU.add, accum_out=edge_in[:, side:side + 1]).then_inc(s[done], 1)
                            V.tensor_tensor(logit[:, 0, :], er[:, k, :], ps_x[0:ROWS, 0:P], ALU.add).then_inc(s["e"], 1)
                            dve.wait_ge(s["in_left"], n + 1)
                            dve.wait_ge(s["in_right"], n + 1)
                            scans(k, edge_in[:, 0:1], edge_in[:, 1:2], scan_f, scan_b, "fwd", "bwd")
                            V.tensor_tensor(old[:, 0:1], edge_in[:, 0:1], er[:, k, 0:1], ALU.add).then_inc(s["old_e"], 1)
                            dve.wait_ge(s["fwd"], n + 1)
                            dve.wait_ge(s["bwd"], n + 1)
                            V.tensor_tensor(scan_f[:, :], scan_f[:, :], scan_b[:, :], ALU.max).then_inc(s["seg_max"], 1)
                            dve.wait_ge(s["old_e"], n + 1)
                            V.scalar_tensor_tensor(out=old[:, 1:2], in0=old[:, 0:1], scalar=SLOPE, in1=old[:, 0:1],
                                                   op0=ALU.mult, op1=ALU.max).then_inc(s["old_leaky"], 1)
                            dve.wait_ge(s["seg_max"], n + 1)
                            V.tensor_tensor(logit[:, 1, :], scan_f[:, :], er[:, k, :], ALU.add).then_inc(s["e_max"], 1)
                            dve.wait_ge(s["e"], n + 1)
                            dve.wait_ge(s["e_max"], n + 1)
                            V.scalar_tensor_tensor(out=logit[:, :, :], in0=logit[:, :, :], scalar=SLOPE, in1=logit[:, :, :],
                                                   op0=ALU.mult, op1=ALU.max).then_inc(s["leaky"], 1)
                            dve.wait_ge(s["leaky"], n + 1)
                            V.tensor_tensor(wexp[:, 0:P], logit[:, 0, :], logit[:, 1, :], ALU.subtract).then_inc(s["arg"], 1)
                            dve.wait_ge(s["old_leaky"], n + 1)
                            V.tensor_scalar(wexp[:, P:P + 1], old[:, 1:2], logit[:, 1, 0:1], 0.0,
                                            ALU.subtract, ALU.min).then_inc(s["old_arg"], 1)

                        def scale(k, q, n):
                            dve.wait_ge(s["w_cols"], n + 1)
                            v = slots[:, k, q * QT:(q + 1) * QT, 0:AW].rearrange("p t (h d) -> p t h d", h=HEADS)
                            w = ps_w[:, 0:ROWS].rearrange("p (h t) -> p t h", h=HEADS)[:, q * QT:(q + 1) * QT, :]
                            V.tensor_tensor(v, v, w.unsqueeze(3).broadcast_to([P, QT, HEADS, HD + 1]),
                                            ALU.mult).then_inc(s["scaled"], 1)

                        def r_minus_1(n):
                            dve.wait_ge(s["r_row"], n + 1)
                            V.tensor_scalar(rm1[:, :], ps_c[0:1, 128:128 + HEADS], 1.0, None,
                                            ALU.subtract).then_inc(s["rm1"], 1)

                        def rescale_acc(g, k, n, peeled=False):
                            base = dve.value_load(base_row[0:1, bass.ds(QUADS * (SLOTS * g + k), 1)],
                                                  min_val=0, max_val=NT)
                            dve.wait_ge(s["r_cols"], n + 1)
                            V.tensor_scalar(rescale[:, :], ps_d[:, 0:HEADS], 1.0, None, ALU.add).then_inc(s["rescale"], 1)
                            dve.wait_ge(s["rescale"], n + 1)
                            if not peeled:
                                dve.wait_ge(s["added"], QUADS * n)
                            v = accf[:, bass.ds(base * AW, AW)].rearrange("p (h d) -> p h d", h=HEADS)
                            V.tensor_tensor(v, v, rescale[:, :].unsqueeze(2).broadcast_to([P, HEADS, HD + 1]),
                                            ALU.mult).then_inc(s["rescaled"], 1)

                        def chunk(g, k, more=True, first=False):
                            n = n0 + SLOTS * g + k
                            g1, k1 = (g, k + 1) if k + 1 < SLOTS else (g + 1, 0)
                            more = more and gat
                            if more:
                                pack_el(g1, k1, n + 1)
                            add(g, k, 0, first)
                            if more:
                                local_maxima(g1, k1, n + 1)
                                carries(k1, n + 1)
                            add(g, k, 1, first)
                            if more:
                                exponents(k1, n + 1)
                            add(g, k, 2, first)
                            if more:
                                scale(k1, 0, n + 1)
                                r_minus_1(n + 1)
                                scale(k1, 1, n + 1)
                            add(g, k, 3, first)
                            if more:
                                scale(k1, 2, n + 1)
                                scale(k1, 3, n + 1)
                                rescale_acc(g1, k1, n + 1)

                        if gat:
                            pack_el(0, 0, n0)
                            local_maxima(0, 0, n0)
                            carries(0, n0, peeled=True)
                            exponents(0, n0)
                            for q in range(QUADS):
                                scale(0, q, n0)
                            r_minus_1(n0)
                            rescale_acc(0, 0, n0, peeled=True)
                        for k in range(SLOTS):
                            chunk(0, k, first=True)
                        with loop(dve, 1, ITER) as g:
                            for k in range(SLOTS):
                                chunk(g, k)
                        for k in range(TAIL):
                            chunk(ITER, k, more=(k + 1 < TAIL))

                with nc.Block() as block:
                    @block.vector
                    def _(dve):
                        V = nc.vector
                        b0_ = s["base"]
                        row_f = in_a[0:1, 0, 0:2, :].rearrange("p t d -> p (t d)")[:, 0:NCH * QUADS]
                        V.tensor_scalar(lanes[:, :], lanes[:, :], float(WIN), None, ALU.add)
                        V.tensor_copy(row_f, base_row[:, :]).then_inc(b0_, 1)
                        dve.wait_ge(b0_, 3 * rnd + 1)
                        V.tensor_scalar(row_f, row_f, 2.0, float(NT), ALU.add, ALU.min).then_inc(b0_, 1)
                        dve.wait_ge(b0_, 3 * rnd + 2)
                        V.tensor_copy(base_row[:, :], row_f).then_inc(b0_, 1)

                    @block.gpsimd
                    def _(pool):
                        pool.memset(carry[:, :], NEG)
                        pool.inc_swdge_sem(s["rows"], [16 * CT * u for u in USES], mode="sub")

            clear_stage_sems()
            s_back = sem(f"{name}_back")
            with nc.Block() as block:
                @block.gpsimd
                def _(pool):
                    pool.iota(lane_i, [[1, WIN]], base=0, channel_multiplier=0).then_inc(s_back, 1)
                    pool.wait_ge(s_back, 1)
                    pool.tensor_copy(lanes[:, :], lane_i)

                @block.sync
                def _(sp):
                    sp.dma_start(base_row[:, :], base_tab.rearrange("c q -> (c q)").unsqueeze(0)).then_inc(s_back_d, 16)
                    sp.wait_ge(s_back_d, 16 * back_count[0])

        s_back_d = sem("s_back_d")
        back_count = [1]

        aggregate("sage", h0_tab, False)

        s_deg = sem("s_deg")
        s_cum = sem("s_cum")
        pos_f = tmp_a[:, 0, 0:NT]
        tot_f = tmp_b[:, 0, 0:NT]
        cum_f = tmp_b[:, 1, 0:NT]
        zer_f = tmp_a[:, 1, 0:NT]
        with nc.Block() as block:
            @block.vector
            def _(dve):
                V = nc.vector
                n = [0]

                def then(ins):
                    n[0] += 1
                    ins.then_inc(s_deg, 1)
                    dve.wait_ge(s_deg, n[0])

                V.memset(zer_f, 0.0)
                then(V.tensor_copy(deg[:, :], accf.rearrange("p (t c) -> p t c", c=AW)[:, 0:NT, D]))
                then(V.tensor_scalar(deg_inv[:, :], deg[:, :], 1.0, None, ALU.max))
                then(V.reciprocal(deg_inv[:, :], deg_inv[:, :]))
                dve.wait_ge(s_cum, 2)
                then(V.tensor_copy(tot_f, ps_w[:, 0:NT]))
                then(V.tensor_tensor_scan(cum_f, zer_f, tot_f, 0.0, ALU.add, ALU.add))
                then(V.tensor_tensor(cum_f, cum_f, tot_f, ALU.subtract))
                then(V.tensor_tensor(pos_f, cum_f, ps_x[:, 0:NT], ALU.add))
                then(V.tensor_scalar(tot_f, deg[:, :], 0.0, float(NOWHERE), ALU.is_equal, ALU.mult))
                then(V.tensor_tensor(pos_f, pos_f, tot_f, ALU.max))
                then(V.tensor_copy(seg_pos[:, :], pos_f))

            @block.tensor
            def _(pe):
                pe.wait_ge(s_deg, 1)
                nc.tensor.matmul(ps_x[:, 0:NT], before[:, :], deg[:, :], start=True, stop=True).then_inc(s_cum, 1)
                nc.tensor.matmul(ps_w[:, 0:NT], ones[:, :], deg[:, :], start=True, stop=True).then_inc(s_cum, 1)

        s_in = [sem(f"s_in{i}") for i in range(2)]
        s_mean = sem("s_mean")
        s_tr = sem("s_tr")
        s_cp = sem("s_cp")
        s_mm = sem("s_mm")
        s_biased = sem("s_biased")
        s_x1 = sem("s_x1")
        s_st = sem("s_st")
        s_ag = sem("s_ag")
        s_mv = sem("s_mv")
        s_x1o = [sem(f"s_x1o{i}") for i in range(2)]

        def tile_of(v, g, j):
            return v * 0 + g * GROUP + j

        with nc.Block() as block:
            @block.sync
            def _(sp):
                def load(g, half, last=False, peeled=False):
                    if not peeled:
                        sp.wait_ge(s_x1o[half], 16 * g)
                    half_load(sp, x, in_a, g, half, s_in[half], last)
                    half_load(sp, h0_tab, in_b, g, half, s_in[half], False)

                def store(g, half):
                    sp.wait_ge(s_x1, g * GROUP + half * HALF + HALF)
                    sp.wait_ge(s_st, g * GROUP + half * HALF + HALF)
                    sp.dma_start(store_rows(x1_tab, g, half), in_a[:, half, :, :]).then_inc(s_x1o[half], 16)

                load(0, 0, peeled=True)
                load(0, 1, peeled=True)
                with loop(sp, 0, NG - 2) as g:
                    for half in range(2):
                        store(g, half)
                        load(g + 1, half)
                store(NG - 2, 0)
                load(NG - 1, 0)
                store(NG - 2, 1)
                load(NG - 1, 1, last=True)
                store(NG - 1, 0)
                store(NG - 1, 1)
                sp.wait_ge(s_x1o[0], 16 * NG)
                sp.wait_ge(s_x1o[1], 16 * NG)

            @block.vector
            def _(dve):
                V = nc.vector

                def mean(g, j, first):
                    if not (first and j < 2):
                        dve.wait_ge(s_tr, g * GROUP + j - 1)
                    V.tensor_scalar(tmp_b[:, j % 2, :], acc_cols(g * GROUP + j, 0, D), deg_inv[:, bass.ds(g * GROUP + j, 1)], None, ALU.mult).then_inc(s_mean, 1)

                def finish(g, j):
                    t = g * GROUP + j
                    v = in_a[:, j // HALF, j % HALF, :]
                    dve.wait_ge(s_mm, t + 1)
                    V.tensor_tensor(v, v, ps_w[:, 0:D] if j % 2 else ps_d[:, 0:D], ALU.add).then_inc(s_x1, 1)
                    dve.wait_ge(s_x1, t + 1)
                    V.bn_stats(stats[:, j, :], v).then_inc(s_st, 1)

                def aggregate_stats(g):
                    dve.wait_ge(s_st, g * GROUP + GROUP)
                    dve.sem_inc(dve_turn, 1)
                    for j in range(GROUP):
                        V.bn_aggr(mvg[:, j, :], stats[:, j, :]).then_inc(s_ag, 1)
                    dve.wait_ge(s_ag, g * GROUP + GROUP)
                    V.tensor_copy(mv[:, bass.ds(g * GROUP, GROUP), :], mvg[:, :, :]).then_inc(s_mv, 1)

                mean(0, 0, True)
                mean(0, 1, True)

                def group(g, first, last=False):
                    for j in range(GROUP):
                        if j == 0 or j == HALF:
                            dve.wait_ge(s_biased, 2 * g + j // HALF + 1)
                        if not (last and j >= GROUP - 2):
                            mean(*((g, j + 2) if j + 2 < GROUP else (g + 1, j + 2 - GROUP)), False)
                        finish(g, j)
                    aggregate_stats(g)
                    dve.wait_ge(s_mv, g + 1)

                group(0, True)
                with loop(dve, 1, NG - 1) as g:
                    group(g, False)
                group(NG - 1, False, last=True)

            @block.tensor
            def _(pe):
                T = nc.tensor

                def transposes(g, j, first, last):
                    t = g * GROUP + j
                    if j == 0 or j == HALF:
                        pe.wait_ge(s_in[j // HALF], 32 * g + 32 + (16 if last and j else 0))
                    pe.wait_ge(s_mean, t + 1)
                    if not (first and j < 2):
                        pe.wait_ge(s_cp, t - 1)
                    to = pair[j % 2][:, 0, :]
                    for c in range(2):
                        T.transpose(to[:, c * P:c * P + P], tmp_b[:, j % 2, c * P:c * P + P], ident[:, :])
                    for c in range(2):
                        last_ = T.transpose(to[:, (2 + c) * P:(3 + c) * P],
                                            in_b[:, j // HALF, j % HALF, c * P:c * P + P], ident[:, :])
                    last_.then_inc(s_tr, 1)

                def products(g, j, first):
                    t = g * GROUP + j
                    pe.wait_ge(s_cp, t + 1)
                    if not (first and j < 2):
                        pe.wait_ge(s_x1, t - 1)
                    to = ps_w if j % 2 else ps_d
                    for c in range(4):
                        last = T.matmul(to[:, 0:D], lhs[:, j % 2, c * P:c * P + P],
                                        (wnT if c < 2 else wsT)[:, c % 2, :], start=(c == 0), stop=(c == 3))
                    last.then_inc(s_mm, 1)

                def group(g, first, last=False):
                    for j in range(GROUP):
                        nxt = (g, j + 1) if j + 1 < GROUP else (g + 1, 0)
                        if not (last and j == GROUP - 1):
                            transposes(*nxt, first and j + 1 < GROUP, last)
                        products(g, j, first)

                transposes(0, 0, True, False)
                group(0, True)
                with loop(pe, 1, NG - 1) as g:
                    group(g, False)
                group(NG - 1, False, last=True)

            @block.gpsimd
            def _(pool):
                def add_bias(g, half, count):
                    pool.wait_ge(s_in[half], count)
                    v = in_a[:, half, :, :]
                    pool.tensor_tensor(v, v, bias[0][:, :].unsqueeze(1).broadcast_to([P, HALF, D]),
                                       ALU.add).then_inc(s_biased, 1)

                with loop(pool, 0, NG - 1) as g:
                    for half in range(2):
                        add_bias(g, half, 32 * g + 32)
                add_bias(NG - 1, 0, 32 * NG)
                add_bias(NG - 1, 1, 32 * NG + 16)

            @block.scalar
            def _(act):
                def copies(g, first):
                    for j in range(GROUP):
                        t = g * GROUP + j
                        act.wait_ge(s_tr, t + 1)
                        if not (first and j < 2):
                            act.wait_ge(s_mm, t - 1)
                        nc.scalar.activation(lhs[:, j % 2, :], pair[j % 2][:, 0, :], ACT.Copy).then_inc(s_cp, 1)

                copies(0, True)
                with loop(act, 1, NG) as g:
                    copies(g, False)

        s_sq = sem("s_sq")
        with nc.Block() as block:
            @block.scalar
            def _(act):
                nc.scalar.activation(rstd[:, :], mv[:, :, 1], ACT.Sqrt, bias=eps_c[:, 0:1]).then_inc(s_sq, 1)

            @block.vector
            def _(dve):
                dve.wait_ge(s_sq, 1)
                nc.vector.reciprocal(rstd[:, :], rstd[:, :]).then_inc(s_sq, 1)
                dve.wait_ge(s_sq, 2)
                nc.vector.scalar_tensor_tensor(out=nbias[:, :], in0=mv[:, :, 0], scalar=-1.0, in1=rstd[:, :],
                                               op0=ALU.mult, op1=ALU.mult)
                nc.vector.memset(z_out, 1.0)

        def gat_output(dve, act, s, b, g, j, first, to):
            pass

        def node_stage(name, norm, layer, final):
            s = {n: stage_sem(f"node_{n}") for n in
                 ("h", "tr", "cp", "mm", "z", "zel", "zer", "den", "rec", "div", "res", "bias", "neg", "exp",
                  "elu", "pos")}
            s["scat"] = sem(f"{name}_scat")
            s_load = [stage_sem(f"node_load{i}") for i in range(2)]
            s_hout = [stage_sem(f"node_hout{i}") for i in range(2)]
            s_zout = [stage_sem(f"node_zout{i}") for i in range(2)]
            z_w = None if final else wz[layer]
            ahead = 3

            def next_tile(g, j, n=1):
                return (g, j + n) if j + n < GROUP else (g + 1, j + n - GROUP)

            def last_tile(g, j):
                return (g, j - 1) if j else (g - 1, GROUP - 1)

            def lhs_copy(eng, g, j, first):
                t = g * GROUP + j
                eng.wait_ge(s["tr"], t + 1)
                if not (first and j < 2):
                    eng.wait_ge(s["mm"], t - 1)
                to, of = lhs[:, j % 2, 0:D], pair[j % 2][:, 0, 0:D]
                (nc.vector.tensor_copy(to, of) if norm else
                 nc.scalar.activation(to, of, ACT.Copy)).then_inc(s["cp"], 1)

            if not norm:
                with nc.Block() as block:
                    @block.vector
                    def _(dve):
                        sums = accf.rearrange("p (t h d) -> p t h d", h=HEADS, d=HD + 1)[:, 0:NT, :, HD]
                        inv = w_inv[:, :].rearrange("p (t h) -> p t h", h=HEADS)
                        nc.vector.tensor_scalar(inv, sums, 1e-30, None, ALU.max).then_inc(s["den"], 1)
                        dve.wait_ge(s["den"], 1)
                        nc.vector.reciprocal(w_inv[:, :], w_inv[:, :])

            with nc.Block() as block:
                @block.sync
                def _(sp):
                    def load(g, half):
                        half_load(sp, x1_tab if norm else hin_tab, in_a, g, half, s_load[half], False)
                        if final:
                            half_load(sp, x1_tab, in_b, g, half, s_load[half], False)

                    def store(g, half, last=False):
                        sp.wait_ge(s["h"], g * GROUP + half * HALF + HALF)
                        v = accf[:, bass.ds((g * 2 + half) * HALF * AW, HALF * AW)]
                        v = v.rearrange("p (t c) -> p t c", c=AW)[:, :, 0:D]
                        if not final:
                            sp.dma_start(store_rows(hin_tab, g, half), in_b[:, half, :, :]).then_inc(s_hout[half], 16)
                            sp.wait_ge(s["zel"], g * GROUP + half * HALF + HALF)
                            sp.wait_ge(s["z"], g * GROUP + half * HALF + HALF)
                            sp.dma_start(store_rows(z_tab, g, half), z_out[:, half, :, :]).then_inc(s_zout[half], 16)
                        elif not last:
                            sp.dma_start(store_rows(out, g, half), v).then_inc(s_hout[half], 16)
                        else:
                            full, n = (NT - HALF) * P, (HALF - 1) * P
                            sp.dma_start(out[full:full + n, :].rearrange("(t p) d -> p t d", p=P),
                                         v[:, 0:HALF - 1, :]).then_inc(s_hout[half], 16)
                            sp.dma_start(out[full + n:NODES, :], v[0:LAST_ROWS, HALF - 1, :]).then_inc(s_hout[half], 16)

                    load(0, 0)
                    load(0, 1)
                    with loop(sp, 0, NG - 1) as g:
                        for half in range(2):
                            store(g, half)
                            load(g + 1, half)
                    store(NG - 1, 0)
                    store(NG - 1, 1, last=True)
                    sp.wait_ge(s_hout[0], 16 * NG)
                    sp.wait_ge(s_hout[1], 16 * NG + (16 if final else 0))
                    if not final:
                        sp.wait_ge(s_zout[0], 16 * NG)
                        sp.wait_ge(s_zout[1], 16 * NG)

                @block.scalar
                def _(act):
                    def tile(g, j, first):
                        t = g * GROUP + j
                        if norm:
                            if not first and j % HALF == 0:
                                act.wait_ge(s_hout[j // HALF], 16 * g)
                            if j % HALF == 0:
                                act.wait_ge(s_load[j // HALF], 16 * (g + 1))
                            nc.scalar.activation(in_b[:, j // HALF, j % HALF, :],
                                                 in_a[:, j // HALF, j % HALF, :], ACT.Relu, bias=nbias[:, bass.ds(t, 1)],
                                                 scale=rstd[:, bass.ds(t, 1)]).then_inc(s["h"], 1)
                        else:
                            act.wait_ge(s["neg"], t + 1)
                            nc.scalar.activation(tmp_b[:, j % 2, :], tmp_b[:, j % 2, :], ACT.Exp).then_inc(s["exp"], 1)

                    def z_copy(g, j, first):
                        t = g * GROUP + j
                        act.wait_ge(s["mm"], t + 1)
                        if not first:
                            act.wait_ge(s_zout[j // HALF], 16 * g)
                        zp = ps_w if j % 2 else ps_d
                        to = z_out[:, j // HALF, j % HALF, 0:AW].rearrange("p (h d) -> p h d", h=HEADS)[:, :, 0:HD]
                        nc.scalar.activation(to, zp[:, 0:D].rearrange("p (h d) -> p h d", h=HEADS),
                                             ACT.Copy).then_inc(s["z"], 1)

                    def group(g, first, last=False, second=False):
                        for j in range(GROUP):
                            if not (last and j >= GROUP - ahead):
                                tile(*((g, j + ahead) if j + ahead < GROUP else (g + 1, j + ahead - GROUP)),
                                     first and j + ahead < GROUP)
                            if not final:
                                if not norm and not (last and j == GROUP - 1):
                                    lhs_copy(act, *next_tile(g, j), first and j + 1 < GROUP)
                                if not (first and j == 0):
                                    z_copy(*last_tile(g, j), first or (second and j == 0))

                    for j in range(ahead):
                        tile(0, j, True)
                    if not norm and not final:
                        lhs_copy(act, 0, 0, True)
                    group(0, True)
                    group(1, False, second=True)
                    with loop(act, 2, NG - 1) as g:
                        group(g, False)
                    group(NG - 1, False, last=True)
                    if not final:
                        z_copy(NG - 1, GROUP - 1, False)

                @block.vector
                def _(dve):
                    V = nc.vector

                    def activated(g, j, first):
                        t = g * GROUP + j
                        v = acc_cols(t, 0, AW).rearrange("p (h d) -> p h d", h=HEADS)
                        a = tmp_a[:, j % 2, :]
                        if not (first and j < 2):
                            dve.wait_ge(s["h"], t - 1)
                        V.tensor_tensor(a.rearrange("p (h d) -> p h d", h=HEADS), v[:, :, 0:HD],
                                        w_inv[:, bass.ds(t * HEADS, HEADS)].unsqueeze(2)
                                        .broadcast_to([P, HEADS, HD]),
                                        ALU.mult).then_inc(s["div"], 1)
                        if j == 0 or j == HALF:
                            dve.wait_ge(s["bias"], 2 * g + j // HALF + 1)
                        dve.wait_ge(s["div"], t + 1)
                        V.tensor_tensor(a, a, in_a[:, j // HALF, j % HALF, :], ALU.add).then_inc(s["res"], 1)
                        dve.wait_ge(s["res"], t + 1)
                        V.tensor_scalar(tmp_b[:, j % 2, :], a, 0.0, None, ALU.min).then_inc(s["neg"], 1)

                    def elu(g, j, first):
                        t = g * GROUP + j
                        dve.wait_ge(s["exp"], t + 1)
                        if not final and not first and j % HALF == 0:
                            dve.wait_ge(s_hout[j // HALF], 16 * g)
                        to = acc_cols(t, 0, D) if final else in_b[:, j // HALF, j % HALF, :]
                        e = V.scalar_tensor_tensor(out=tmp_a[:, j % 2, :] if final else to, in0=tmp_b[:, j % 2, :],
                                                   scalar=-1.0, in1=tmp_a[:, j % 2, :], op0=ALU.add, op1=ALU.max)
                        if final:
                            e.then_inc(s["elu"], 1)
                            dve.wait_ge(s["elu"], t + 1)
                            V.tensor_tensor(to, tmp_a[:, j % 2, :], in_b[:, j // HALF, j % HALF, :],
                                            ALU.add).then_inc(s["h"], 1)
                        else:
                            e.then_inc(s["h"], 1)

                    def tails(g, j, first):
                        t = g * GROUP + j
                        dve.wait_ge(s["mm"], t + 1)
                        dve.wait_ge(s["z"], t + 1)
                        if not first:
                            dve.wait_ge(s_zout[j // HALF], 16 * g)
                            if j == 0:
                                dve.wait_ge(s["scat"], 16 * GROUP * g)
                        zp = ps_w if j % 2 else ps_d
                        V.tensor_copy(z_out[:, j // HALF, j % HALF, AW:ROW], zp[:, D:D + 2 * HEADS]).then_inc(s["zel"], 1)
                        V.tensor_copy(er_stage[:, j, :], zp[:, D + HEADS:D + 2 * HEADS]).then_inc(s["zer"], 1)
                        if j == GROUP - 1:
                            V.tensor_copy(pos_stage[:, :], seg_pos[:, bass.ds(g * GROUP, GROUP)]).then_inc(s["pos"], 1)

                    def group(g, first, last=False, second=False):
                        for j in range(GROUP):
                            if not norm:
                                if not (last and j >= GROUP - ahead):
                                    activated(*next_tile(g, j, ahead), first and j + ahead < GROUP)
                                if not (last and j >= GROUP - ahead + 1):
                                    elu(*next_tile(g, j, ahead - 1), first and j + ahead - 1 < GROUP)
                            if not final:
                                if norm and not (last and j == GROUP - 1):
                                    lhs_copy(dve, *next_tile(g, j), first and j + 1 < GROUP)
                                if not (first and j == 0):
                                    tails(*last_tile(g, j), first or (second and j == 0))

                    if norm:
                        lhs_copy(dve, 0, 0, True)
                    else:
                        for j in range(ahead):
                            activated(0, j, True)
                            if j:
                                elu(0, j - 1, True)
                    group(0, True)
                    group(1, False, second=True)
                    with loop(dve, 2, NG - 1) as g:
                        group(g, False)
                    group(NG - 1, False, last=True)
                    if not final:
                        tails(NG - 1, GROUP - 1, False)

                def add_bias(pool, g, half):
                    pool.wait_ge(s_load[half], (32 if final else 16) * (g + 1))
                    v = in_a[:, half, :, :]
                    pool.tensor_tensor(v, v, bias[2 if final else layer][:, :].unsqueeze(1)
                                       .broadcast_to([P, HALF, D]), ALU.add).then_inc(s["bias"], 1)

                if final:
                    @block.gpsimd
                    def _(pool):
                        with loop(pool, 0, NG) as g:
                            for half in range(2):
                                add_bias(pool, g, half)

                if not final:
                    @block.tensor
                    def _(pe):
                        T = nc.tensor

                        def transposes(g, j, first):
                            t = g * GROUP + j
                            pe.wait_ge(s["h"], t + 1)
                            if not (first and j < 2):
                                pe.wait_ge(s["cp"], t - 1)
                            for c in range(2):
                                last = T.transpose(pair[j % 2][:, 0, c * P:c * P + P],
                                                   in_b[:, j // HALF, j % HALF, c * P:c * P + P], ident[:, :])
                            last.then_inc(s["tr"], 1)

                        def products(g, j, first):
                            t = g * GROUP + j
                            pe.wait_ge(s["cp"], t + 1)
                            if not (first and j < 2):
                                pe.wait_ge(s["zer"], t - 1)
                            zp = ps_w if j % 2 else ps_d
                            for c in range(2):
                                last = T.matmul(zp[:, 0:D + 2 * HEADS], lhs[:, j % 2, c * P:c * P + P], z_w[:, c, :],
                                                start=(c == 0), stop=(c == 1))
                            last.then_inc(s["mm"], 1)

                        def group(g, first, last=False):
                            for j in range(GROUP):
                                if not (last and j == GROUP - 1):
                                    transposes(*next_tile(g, j), first and j + 1 < GROUP)
                                products(g, j, first)

                        transposes(0, 0, True)
                        group(0, True)
                        with loop(pe, 1, NG - 1) as g:
                            group(g, False)
                        group(NG - 1, False, last=True)

                    @block.gpsimd
                    def _(pool):
                        def scatter(g):
                            pool.wait_ge(s["pos"], g + 1)
                            pool.wait_ge(s["zer"], g * GROUP + GROUP)
                            pool.sem_inc(pool_turn, 1)
                            for j in range(GROUP):
                                pool.indirect_dma_start(
                                    er_start, bass.IndirectOffsetOnAxis(ap=pos_stage[:, j:j + 1], axis=0),
                                    er_stage[:, j, :], None, bounds_check=EPAD - 1,
                                    oob_is_err=False).then_inc(s["scat"], 16)

                        if not norm:
                            add_bias(pool, 0, 0)
                            add_bias(pool, 0, 1)
                        with loop(pool, 0, NG - 1) as g:
                            if not norm:
                                add_bias(pool, g + 1, 0)
                            scatter(g)
                            if not norm:
                                add_bias(pool, g + 1, 1)
                        scatter(NG - 1)
                        pool.wait_ge(s["scat"], 16 * NT)

            clear_stage_sems()

        val = flat[0:NCH, 0:CE * HEADS]
        same = flat[0:NCH, CE * HEADS:CE * HEADS + CE]
        filled = [flat[0:NCH, CE * HEADS + CE:CE * HEADS + 2 * CE], hot[0:NCH, 0:CE]]

        def spread_er(name):
            s_l = sem(f"{name}_load")
            s_g = sem(f"{name}_first")
            s_f = sem(f"{name}_filled")
            s_o = [sem(f"{name}_out{i}") for i in range(2)]
            with nc.Block() as block:
                @block.sync
                def _(sp):
                    sp.dma_start(val, er_start.rearrange("(c e) h -> c (e h)", e=CE)).then_inc(s_l, 16)
                    sp.dma_start(same, same_tab).then_inc(s_l, 16)
                    for h in range(HEADS):
                        sp.wait_ge(s_f, h + 1)
                        sp.dma_start(er_rows[:, h, :], filled[h % 2]).then_inc(s_o[h % 2], 16)
                    for i in range(2):
                        sp.wait_ge(s_o[i], 16 * HEADS // 2)

                @block.gpsimd
                def _(pool):
                    pool.indirect_dma_start(er_init[:, :], None, z_tab,
                                            bass.IndirectOffsetOnAxis(ap=first_dst[:, 0:1], axis=0)).then_inc(s_g, 16)
                    pool.memset(accf, 0.0)

                @block.vector
                def _(dve):
                    dve.wait_ge(s_l, 32)
                    dve.wait_ge(s_g, 16)
                    for h in range(HEADS):
                        if h >= 2:
                            dve.wait_ge(s_o[h % 2], 16)
                        nc.vector.tensor_tensor_scan(filled[h % 2], same, val[:, h:CE * HEADS:HEADS],
                                                     er_init[:, AW + HEADS + h:AW + HEADS + h + 1],
                                                     ALU.mult, ALU.add).then_inc(s_f, 1)

        back_count[0] = 2
        node_stage("norm", True, 0, False)
        spread_er("fill0")
        aggregate("gat0", z_tab, True)
        s_ones = sem("s_ones")
        with nc.Block() as block:
            @block.vector
            def _(dve):
                nc.vector.memset(z_out, 1.0).then_inc(s_ones, 1)

        back_count[0] = 3
        node_stage("mid", False, 1, False)
        spread_er("fill1")
        aggregate("gat1", z_tab, True)
        node_stage("last", False, 1, True)


_INS = ["x", "src", "dst", "L0_gnn_W_neigh", "L0_gnn_W_self", "L0_gnn_b_self",
        "L1_gnn_W0", "L1_gnn_al0", "L1_gnn_ar0", "L1_gnn_b0",
        "L1_gnn_W1", "L1_gnn_al1", "L1_gnn_ar1", "L1_gnn_b1"]


def kernel(**inputs):
    import numpy as np
    import concourse.bacc as bacc
    from concourse.bass_utils import run_bass_kernel_spmd

    nc = bacc.Bacc("TRN2", target_bir_lowering=False, num_devices=1)
    arrays, args = {}, []
    for name in _INS:
        a = np.ascontiguousarray(inputs[name])
        arrays[f"in_{name}"] = a
        args.append(nc.dram_tensor(f"in_{name}", a.shape, mybir.dt.from_np(a.dtype), kind="ExternalInput").ap())
    args.append(nc.dram_tensor("out", (NODES, D), F32, kind="ExternalOutput").ap())
    gnn_kernel(nc, *args)
    r = run_bass_kernel_spmd(nc, [arrays], core_ids=[0])
    return r.results[0]["out"]
```

```python
from contextlib import ExitStack

import concourse.bass as bass
from concourse import mybir

F32 = mybir.dt.float32
I32 = mybir.dt.int32
ACT = mybir.ActivationFunctionType
ALU = mybir.AluOpType
AX = mybir.AxisListType

P = 128
NODES, D, EDGES = 12500, 256, 200000
HEADS, HD = 4, 64
NT = -(-NODES // P)
NPAD = NT * P
LAST_ROWS = NODES - (NT - 1) * P
CT = 16
CE = CT * P
SLOTS = 3
NCH = -(-EDGES // CE)
ITER = NCH // SLOTS
TAIL = NCH % SLOTS
USES = [ITER + (k < TAIL) for k in range(SLOTS)]
EPAD = NCH * CE
QUADS, QT = 4, 4
QE = QT * P
ROWS = HEADS * CT
WIN = 2 * P
AW = HEADS * (HD + 1)
ROW = AW + 2 * HEADS
ACC_TILES = NT + 2
GROUP, HALF = 14, 7
NG = NT // GROUP
SB = 3
SLOPE = 0.2
LN_EPS = 1e-5
NEG = -1e30
PAD_NODE = NPAD - 1
NOWHERE = EPAD

assert TAIL and NCH == NT and NT == NG * GROUP and NCH == EDGES // CE + 1 <= P and EDGES % QE and PAD_NODE >= NODES


def gnn_kernel(nc, x, src, dst, w_neigh, w_self, b_self,
               w0, al0, ar0, b0, w1, al1, ar1, b1, out):
    ctx = ExitStack()
    with ctx:
        def sb(name, shape, dt=F32):
            return ctx.enter_context(nc.sbuf_tensor(name, shape, dt))

        def pb(name, shape):
            return ctx.enter_context(nc.psum_tensor(name, shape, F32))

        def sem(name):
            return ctx.enter_context(nc.semaphore(name))

        shared = {}

        def stage_sem(name):
            if name not in shared:
                shared[name] = sem(name)
            return shared[name]

        def clear_stage_sems():
            with nc.Block() as block:
                @block.sync
                def _(sp):
                    for handle in shared.values():
                        sp.sem_clear(handle)

        def dram(name, shape, dt=F32):
            return nc.dram_tensor(name, shape, dt, kind="Internal").ap()

        h0_tab = dram("h0_tab", (NPAD, D))
        z_tab = dram("z_tab", (NPAD, ROW))
        x1_tab = dram("x1_tab", (NPAD, D))
        hin_tab = dram("hin_tab", (NPAD, D))
        er_start = dram("er_start", (EPAD, HEADS))
        er_rows = dram("er_rows", (NCH, HEADS, CE))
        pen_rows = dram("pen_rows", (NCH, HEADS, CT, P + 2))
        same_tab = dram("same_tab", (NCH, CE))
        chain_tab = dram("chain_tab", (NCH, 2 * CT))
        base_tab = dram("base_tab", (NCH, QUADS), I32)

        acc = sb("acc", [P, ACC_TILES * AW])
        slots = sb("slots", [P, SLOTS, CT, ROW])
        onehot = sb("onehot", [P, SB, QT, WIN])
        src_t = sb("src_t", [P, NCH * CT], I32)
        negrel = sb("negrel", [P, NCH * CT])
        idx = sb("idx", [P, SLOTS, CT], I32)
        base_row = sb("base_row", [1, NCH * QUADS], I32)
        rounds_i = sb("rounds_i", [1, 1], I32)
        first_dst = sb("first_dst", [NCH, 1], I32)
        seg_pos = sb("seg_pos", [P, NT], I32)
        ident = sb("ident", [P, P])
        ones = sb("ones", [P, P])
        before = sb("before", [P, P])
        lanes = sb("lanes", [P, WIN])
        tile_mask = sb("tile_mask", [ROWS, CT])
        head_mask = sb("head_mask", [ROWS, HEADS])
        head_rows = sb("head_rows", [HEADS, ROWS])
        first_rows = sb("first_rows", [ROWS, HEADS])
        one_c = sb("one_c", [P, 1])
        eps_c = sb("eps_c", [P, 1])
        wsT = sb("wsT", [P, 2, D])
        wnT = sb("wnT", [P, 2, D])
        wz = [sb(f"wz{i}", [P, 2, D + 2 * HEADS]) for i in range(2)]
        attn = [sb(f"attn{i}", [P, 2, 2 * HEADS]) for i in range(2)]
        bias = [sb(f"bias{i}", [P, D]) for i in range(3)]
        soft = sb("soft", [P, 2 * SLOTS * D + D + 256])
        soft_at = [0]

        def soft_buf(rows, n):
            v = soft[0:rows, soft_at[0]:soft_at[0] + n]
            soft_at[0] += n
            return v

        pen = soft_buf(ROWS, SLOTS * (P + 2)).rearrange("p (s c) -> p s c", s=SLOTS)
        er = soft_buf(ROWS, SLOTS * P).rearrange("p (s c) -> p s c", s=SLOTS)
        chain_pen = sb("chain_pen", [HEADS, SLOTS, 2 * CT])
        el_cols = soft_buf(P, ROWS)
        scan_f = soft_buf(ROWS, P)
        scan_b = soft_buf(ROWS, P)
        ends = sb("ends", [ROWS, 2, CT])
        carry = sb("carry", [HEADS, 2 * CT + 4])
        scrap = sb("scrap", [ROWS, 2, CT])
        edge_in = sb("edge_in", [ROWS, 2])
        logit = soft_buf(ROWS, 2 * P).rearrange("p (s c) -> p s c", s=2)
        old = sb("old", [ROWS, 2])
        wexp = soft_buf(ROWS, P + 1)
        wrow = soft_buf(ROWS, P + 1)
        rm1 = sb("rm1", [1, HEADS])
        rescale = sb("rescale", [P, HEADS])
        mv = sb("mv", [P, NT, 2])
        stats = sb("stats", [P, GROUP, 6])
        mvg = sb("mvg", [P, GROUP, 2])
        rstd = sb("rstd", [P, NT])
        nbias = sb("nbias", [P, NT])
        deg_inv = sb("deg_inv", [P, NT])
        deg = sb("deg", [P, NT])
        w_inv = soft_buf(P, NT * HEADS)
        er_stage = sb("er_stage", [P, GROUP, HEADS])
        pos_stage = sb("pos_stage", [P, GROUP], I32)
        er_init = sb("er_init", [NCH, ROW])

        self_x = soft[:, 0:SLOTS * D].rearrange("p (s d) -> p s d", s=SLOTS)
        self_h = soft[:, SLOTS * D:2 * SLOTS * D].rearrange("p (s d) -> p s d", s=SLOTS)
        self_hT = soft[:, 2 * SLOTS * D:2 * SLOTS * D + D]

        flat = slots[:, :, :, :].rearrange("p a b c -> p (a b c)")
        H = HALF * D
        in_a = flat[:, 0:2 * H].rearrange("p (s t d) -> p s t d", s=2, t=HALF)
        in_b = flat[:, 2 * H:4 * H].rearrange("p (s t d) -> p s t d", s=2, t=HALF)
        z_out = flat[:, 4 * H:4 * H + 2 * HALF * ROW].rearrange("p (s t d) -> p s t d", s=2, t=HALF)
        hot = onehot[:, :, :, :].rearrange("p a b c -> p (a b c)")
        lhs = hot[:, 0:1024].rearrange("p (s c) -> p s c", s=2)
        tmp_a = hot[:, 1024:1536].rearrange("p (s c) -> p s c", s=2)
        tmp_b = hot[:, 1536:2048].rearrange("p (s c) -> p s c", s=2)
        accf = acc[:, :]

        def loop(eng, start, end):
            return nc.Fori(start, end, engines=bass.OrderedEngineSet([eng.engine]), hint_back_edge=True)

        def acc_cols(tile, lo, n):
            return accf[:, bass.ds(tile * AW + lo, n)]

        pair = [pb(f"pair{i}", [P, 2, 512]) for i in range(2)]
        ps_x = pb("ps_x", [P, 512])
        ps_w = pb("ps_w", [P, 512])
        ps_c = pb("ps_c", [P, 512])
        ps_d = pb("ps_d", [P, 512])

        pool_turn = sem("pool_turn")
        dve_turn = sem("dve_turn")
        pe_turn = sem("pe_turn")
        sp_turn = sem("sp_turn")

        cols = [0]

        def edge_buf(n, dt=F32):
            v = accf[0:NCH, cols[0]:cols[0] + n]
            cols[0] += n
            return v if dt is F32 else v.bitcast(dt)

        d_i = edge_buf(CE + 2, I32)
        s_i = edge_buf(CE, I32)
        d_f = edge_buf(CE + 2)
        s_f = edge_buf(CE)
        start_f = edge_buf(CE + 1)
        pen_f = edge_buf(CE + 1)
        same_f = edge_buf(CE)
        ch_f = edge_buf(2 * CT)
        b_first = edge_buf(QUADS, I32)
        b_last = edge_buf(QUADS, I32)
        span_i = edge_buf(QUADS, I32)
        span_f = edge_buf(QUADS)
        span_m = edge_buf(1)
        d_last = edge_buf(QUADS, I32)
        whole, rest = EDGES // CE, EDGES % CE
        s_pad = sem("s_pad")
        s_eload = sem("s_eload")
        s_ev = sem("s_ev")
        s_estore = sem("s_estore")
        zero_view = accf[:, 16384:16384 + EPAD * HEADS // P]

        s_masks = sem("s_masks")
        s_wload = sem("s_wload")
        s_wzero = sem("s_wzero")
        raw = [in_a[:, i, :, :].rearrange("p t d -> p (t d)")[:, 0:2 * D]
               .rearrange("p (c d) -> p c d", c=2) for i in range(2)]
        wT = in_b[:, 0, :, :].rearrange("p t d -> p (t d)")[:, 0:2 * D].rearrange("p (c d) -> p c d", c=2)
        lane_i = in_b[:, 1, 0, :].bitcast(I32)
        with nc.Block() as block:
            @block.gpsimd
            def _(pool):
                pool.memset(ident[:, :], 0.0)
                pool.memset(before[:, :], 1.0)
                pool.memset(ones[:, :], 1.0)
                pool.memset(one_c[:, :], 1.0)
                pool.memset(eps_c[:, :], LN_EPS)
                pool.iota(lane_i, [[1, WIN]], base=0, channel_multiplier=0).then_inc(s_masks, 1)
                pool.wait_ge(s_masks, 1)
                pool.affine_select(out=ident[:, :], in_=ident[:, :], compare_op=ALU.not_equal, fill=1.0,
                                   base=0, pattern=[[-1, P]], channel_multiplier=1)
                pool.affine_select(out=before[:, :], in_=before[:, :], compare_op=ALU.is_gt, fill=0.0,
                                   base=0, pattern=[[1, P]], channel_multiplier=-1)
                pool.tensor_copy(lanes[:, :], lane_i)

            @block.vector
            def _(dve):
                nc.vector.memset(attn[0][:, :, :], 0.0).then_inc(s_wzero, 1)
                nc.vector.memset(attn[1][:, :, :], 0.0).then_inc(s_wzero, 1)
                nc.vector.memset(d_i, PAD_NODE).then_inc(s_pad, 1)
                nc.vector.memset(d_last, PAD_NODE).then_inc(s_pad, 1)
                nc.vector.memset(s_i, 0).then_inc(s_pad, 1)
                nc.vector.memset(zero_view, 0.0).then_inc(s_pad, 1)
                dve.wait_ge(s_pad, 1)
                nc.vector.memset(d_i[0:1, 0:1], -1).then_inc(s_pad, 1)

            @block.sync
            def _(sp):
                n = 0
                for w, to in ((w_self, raw[0]), (w_neigh, raw[1]),
                              (w0, wz[0][:, :, 0:D]), (w1, wz[1][:, :, 0:D])):
                    sp.dma_start(to, w.rearrange("(c p) d -> p c d", p=P)).then_inc(s_wload, 16)
                    n += 16
                for i, b in enumerate((b_self, b0, b1)):
                    sp.dma_start(bias[i][:, :], b.unsqueeze(0).broadcast_to([P, D])).then_inc(s_wload, 16)
                    n += 16
                sp.wait_ge(s_wzero, 2)
                with nc.allow_non_contiguous_dma(reason="columns of the attention vectors, once"):
                    for i, pairs in enumerate(((al0, ar0), (al1, ar1))):
                        for j, a in enumerate(pairs):
                            for h in range(HEADS):
                                lo = (h % 2) * HD
                                c = j * HEADS + h
                                sp.dma_start(attn[i][lo:lo + HD, h // 2, c:c + 1],
                                             a[h, :].unsqueeze(1)).then_inc(s_wload, 16)
                                n += 16
                sp.wait_ge(s_pad, 5)
                rows = bass.AP(tensor=dst.tensor, offset=CE - 1, ap=[[CE, whole - 1], [1, CE + 2]])
                sp.dma_start(d_i[1:whole, :], rows).then_inc(s_eload, 16)
                sp.dma_start(d_i[0:1, 1:CE + 2], dst[0:CE + 1].unsqueeze(0)).then_inc(s_eload, 16)
                sp.dma_start(d_i[whole:whole + 1, 0:rest + 1],
                             dst[whole * CE - 1:EDGES].unsqueeze(0)).then_inc(s_eload, 16)
                sp.dma_start(s_i[0:whole, :], src[0:whole * CE].rearrange("(c e) -> c e", e=CE)).then_inc(s_eload, 16)
                sp.dma_start(s_i[whole:whole + 1, 0:rest], src[whole * CE:EDGES].unsqueeze(0)).then_inc(s_eload, 16)
                sp.dma_start(er_start.rearrange("(p e) h -> p (e h)", p=P), zero_view).then_inc(s_eload, 16)
                with nc.allow_non_contiguous_dma(reason="an edge per quad, once"):
                    sp.dma_start(d_last[0:whole, :], bass.AP(tensor=dst.tensor, offset=QE - 1,
                                                             ap=[[CE, whole], [QE, QUADS]])).then_inc(s_eload, 16)
                    sp.dma_start(d_last[whole:whole + 1, 0:rest // QE],
                                 bass.AP(tensor=dst.tensor, offset=whole * CE + QE - 1,
                                         ap=[[CE, 1], [QE, rest // QE]])).then_inc(s_eload, 16)
                sp.dma_start(d_last[whole:whole + 1, rest // QE:rest // QE + 1],
                             dst[EDGES - 1:EDGES].unsqueeze(0)).then_inc(s_eload, 16)
                sp.wait_ge(s_eload, 144)
                sp.wait_ge(s_wload, n)

        s_mk = sem("s_mk")
        s_wt = sem("s_wt")
        s_wc = sem("s_wc")
        s_wv = sem("s_wv")
        jobs = [("T", raw[0], wsT), ("T", raw[1], wnT), ("Z", wz[0], 0), ("Z", wz[1], 1)]
        with nc.Block() as block:
            @block.vector
            def _(dve):
                sq = ident[0:ROWS, 0:ROWS]
                nc.vector.tensor_reduce(out=tile_mask[:, :], in_=sq.rearrange("p (h t) -> p t h", h=HEADS),
                                        axis=AX.X, op=ALU.add)
                nc.vector.tensor_reduce(out=head_mask[:, :], in_=sq.rearrange("p (h t) -> p h t", h=HEADS),
                                        axis=AX.X, op=ALU.add)
                nc.vector.tensor_copy(head_rows[:, :].rearrange("p (h t) -> p h t", h=HEADS),
                                      ident[0:HEADS, 0:HEADS].unsqueeze(2).broadcast_to([HEADS, HEADS, CT]))
                nc.vector.tensor_copy(first_rows[:, :],
                                      sq.rearrange("p (h t) -> p h t", h=HEADS)[:, :, 0])
                for n, (kind, _, to) in enumerate(jobs):
                    dve.wait_ge(s_wt, n + 1)
                    if n >= 3:
                        dve.wait_ge(s_wv, n - 2)
                    view = (to if kind == "T" else wT)[:, :, :]
                    nc.vector.tensor_copy(view.rearrange("p c d -> p (c d)"), ps_x[:, :]).then_inc(s_wc, 1)
                    if kind == "Z":
                        dve.wait_ge(s_wv, to + 1)
                        nc.vector.tensor_copy(wz[to][:, :, D:D + 2 * HEADS],
                                              ps_w[:, 0:16].rearrange("p (c a) -> p c a", c=2)).then_inc(s_mk, 1)

            @block.tensor
            def _(pe):
                for n, (kind, w, to) in enumerate(jobs):
                    if n:
                        pe.wait_ge(s_wc, n)
                    for a in range(2):
                        for b in range(2):
                            last = nc.tensor.transpose(ps_x[:, b * D + a * P:b * D + a * P + P],
                                                       w[:, a, b * P:b * P + P], ident[:, :])
                    last.then_inc(s_wt, 1)
                    if kind == "Z":
                        pe.wait_ge(s_wc, n + 1)
                        if to:
                            pe.wait_ge(s_mk, to)
                        for a in range(2):
                            for b in range(2):
                                last = nc.tensor.matmul(ps_w[:, a * 8:a * 8 + 8], wT[:, b, a * P:a * P + P],
                                                        attn[to][:, b, :], start=(b == 0), stop=(b == 1))
                        last.then_inc(s_wv, 1)

        with nc.Block() as block:
            @block.vector
            def _(dve):
                V = nc.vector
                step = [0]

                def then(ins):
                    step[0] += 1
                    ins.then_inc(s_ev, 1)
                    dve.wait_ge(s_ev, step[0])

                V.tensor_copy(s_f, s_i)
                V.tensor_single_scalar(b_first, d_i[:, 1:1 + CE:QE], 7, op=ALU.logical_shift_right)
                V.tensor_single_scalar(b_last, d_last, 7, op=ALU.logical_shift_right)
                V.tensor_copy(first_dst[:, :], d_i[:, 1:2])
                then(V.tensor_copy(d_f, d_i))
                then(V.tensor_tensor(start_f, d_f[:, 0:CE + 1], d_f[:, 1:CE + 2], ALU.not_equal))
                V.tensor_scalar(pen_f, start_f, NEG, None, ALU.mult)
                V.tensor_scalar(same_f, start_f[:, 0:CE], -1.0, 1.0, ALU.mult, ALU.add)
                V.tensor_tensor(ch_f[:, 0:CT], d_f[:, P:CE + 1:P], d_f[:, 0:CE:P], ALU.not_equal)
                then(V.tensor_tensor(ch_f[:, CT:2 * CT], d_f[:, 1:CE + 1:P], d_f[:, P + 1:CE + 2:P], ALU.not_equal))
                V.tensor_scalar(ch_f, ch_f, NEG, None, ALU.mult)
                then(V.tensor_tensor(span_i, b_last, b_first, ALU.subtract))
                then(V.tensor_copy(span_f, span_i))
                V.tensor_reduce(out=span_m, in_=span_f, axis=AX.X, op=ALU.max)

        s_e2 = sem("s_e2")
        s_eT = sem("s_eT")
        s_sT = sem("s_sT")
        s_dT = sem("s_dT")
        s_sp = sem("s_sp")
        with nc.Block() as block:
            @block.sync
            def _(sp):
                pv = pen_f[:, 0:CE].rearrange("c (t p) -> c t p", p=P)
                n = 0
                for h in range(HEADS):
                    sp.dma_start(pen_rows[:, h, :, 0:P], pv).then_inc(s_estore, 16)
                    with nc.allow_non_contiguous_dma(reason="a column per tile, once"):
                        for col in (P, P + 1):
                            sp.dma_start(pen_rows[:, h, :, col:col + 1],
                                         pen_f[:, P:CE + 1:P].unsqueeze(2)).then_inc(s_estore, 16)
                    n += 48
                sp.dma_start(same_tab, same_f).then_inc(s_estore, 16)
                sp.dma_start(chain_tab, ch_f).then_inc(s_estore, 16)
                sp.dma_start(base_tab, b_first).then_inc(s_estore, 16)
                sp.wait_ge(s_estore, n + 48)
                row = base_tab.rearrange("c q -> (c q)").unsqueeze(0)
                sp.dma_start(base_row[:, :], row).then_inc(s_e2, 16)
                sp.dma_start(in_a[:, 0, 0:2, :].rearrange("p t d -> p (t d)")[:, 0:NCH * QUADS].bitcast(I32),
                             row.broadcast_to([P, NCH * QUADS])).then_inc(s_e2, 16)
                sp.wait_ge(s_e2, 32)

            @block.tensor
            def _(pe):
                banks = [pair[0], pair[1]]
                for j in range(2 * CT):
                    t = j // 2
                    buf = (s_f, d_f)[j % 2]
                    lo = t * P + (j % 2)
                    if j >= 2:
                        pe.wait_ge((s_sT, s_dT)[j % 2], j // 2)
                    nc.tensor.transpose(banks[j % 2][:, 0, 0:NCH], buf[:, lo:lo + P],
                                        ident[0:NCH, 0:NCH]).then_inc(s_eT, 1)
                nc.tensor.transpose(ps_x[0:1, 0:NCH], span_m, ident[0:NCH, 0:NCH]).then_inc(s_eT, 1)

            @block.vector
            def _(dve):
                V = nc.vector
                for j in range(2 * CT):
                    dve.wait_ge(s_eT, j + 1)
                    to, done = ((src_t, s_sT), (negrel, s_dT))[j % 2]
                    V.tensor_copy(to[:, :].rearrange("p (c t) -> p c t", t=CT)[:, :, j // 2],
                                  pair[j % 2][:, 0, 0:NCH]).then_inc(done, 1)
                dve.wait_ge(s_eT, 2 * CT + 1)
                V.tensor_reduce(out=old[0:1, 0:1], in_=ps_x[0:1, 0:NCH], axis=AX.X, op=ALU.max).then_inc(s_sp, 1)
                dve.wait_ge(s_sp, 1)
                V.tensor_copy(rounds_i[:, :], old[0:1, 0:1]).then_inc(s_sp, 1)
                dve.wait_ge(s_sp, 2)
                V.tensor_single_scalar(rounds_i[:, :], rounds_i[:, :], 1, op=ALU.logical_shift_right).then_inc(s_sp, 1)
                dve.wait_ge(s_sp, 3)
                V.tensor_copy(old[0:1, 0:1], rounds_i[:, :]).then_inc(s_sp, 1)
                dve.wait_ge(s_sp, 4)
                V.tensor_scalar(rounds_i[:, :], old[0:1, 0:1], 1.0, None, ALU.add).then_inc(s_sp, 1)
                base_b = in_a[:, 0, 0:2, :].rearrange("p t d -> p (t d)")[:, 0:NCH * QUADS]
                base_f = in_a[:, 1, 0:2, :].rearrange("p t d -> p (t d)")[:, 0:NCH * QUADS]
                dve.wait_ge(s_e2, 32)
                V.tensor_copy(base_f, base_b.bitcast(I32)).then_inc(s_sp, 1)
                dve.wait_ge(s_sp, 6)
                V.tensor_scalar(base_f, base_f, float(P), None, ALU.mult).then_inc(s_sp, 1)
                dve.wait_ge(s_sp, 7)
                dve.wait_ge(s_dT, CT)
                rel = negrel[:, :].rearrange("p (q t) -> p q t", t=QT)
                V.tensor_tensor(rel, base_f.unsqueeze(2).broadcast_to([P, NCH * QUADS, QT]), rel,
                                ALU.subtract).then_inc(s_sp, 1)

        def half_load(sp, tab, buf, g, half, done, rows_limit):
            if rows_limit:
                full = (NT - HALF) * P
                n = (HALF - 1) * P
                sp.dma_start(buf[:, half, 0:HALF - 1, :],
                             tab[full:full + n, :].rearrange("(t p) d -> p t d", p=P)).then_inc(done, 16)
                sp.dma_start(buf[0:LAST_ROWS, half, HALF - 1, :], tab[full + n:NODES, :]).then_inc(done, 16)
            else:
                v = tab[bass.ds((g * 2 + half) * HALF * P, HALF * P), :]
                sp.dma_start(buf[:, half, :, :], v.rearrange("(t p) d -> p t d", p=P)).then_inc(done, 16)

        def store_rows(tab, g, half):
            return tab[bass.ds((g * 2 + half) * HALF * P, HALF * P), :].rearrange("(t p) d -> p t d", p=P)

        s_x = [sem(f"s_xload{i}") for i in range(2)]
        s_xz = sem("s_xz")
        s_h0 = [sem(f"s_h0out{i}") for i in range(2)]
        s_bn = sem("s_bn")
        s_agg = sem("s_agg")
        s_std = sem("s_std")
        s_rs = sem("s_rs")
        s_relu = sem("s_relu")
        with nc.Block() as block:
            @block.gpsimd
            def _(pool):
                pool.memset(in_a[:, :, :, :], 0.0).then_inc(s_xz, 1)
                pool.memset(accf, 0.0)

            @block.sync
            def _(sp):
                sp.wait_ge(s_xz, 1)

                def load(g, half, last=False):
                    half_load(sp, x, in_a, g, half, s_x[half], last)

                def store(g, half):
                    sp.wait_ge(s_relu, g * GROUP + half * HALF + HALF)
                    sp.dma_start(store_rows(h0_tab, g, half), in_b[:, half, :, :]).then_inc(s_h0[half], 16)

                load(0, 0)
                load(0, 1)
                with loop(sp, 0, NG - 2) as g:
                    for half in range(2):
                        store(g, half)
                        load(g + 1, half)
                store(NG - 2, 0)
                load(NG - 1, 0)
                store(NG - 2, 1)
                load(NG - 1, 1, last=True)
                store(NG - 1, 0)
                store(NG - 1, 1)
                sp.wait_ge(s_h0[0], 16 * NG)
                sp.wait_ge(s_h0[1], 16 * NG)

            @block.vector
            def _(dve):
                V = nc.vector

                def half_stats(g, half, last=False):
                    t0 = half * HALF
                    dve.wait_ge(s_x[half], 16 * g + 16 + (16 if last else 0))
                    for j in range(HALF):
                        V.bn_stats(stats[:, t0 + j, :], in_a[:, half, j, :]).then_inc(s_bn, 1)
                    dve.wait_ge(s_bn, g * GROUP + t0 + HALF)
                    dve.sem_inc(dve_turn, 1)
                    for j in range(HALF):
                        V.bn_aggr(mvg[:, t0 + j, :], stats[:, t0 + j, :]).then_inc(s_agg, 1)
                    dve.wait_ge(s_std, g * 2 + half + 1)
                    V.reciprocal(rstd[:, t0:t0 + HALF], rstd[:, t0:t0 + HALF]).then_inc(s_rs, 1)
                    dve.wait_ge(s_rs, g * 4 + half * 2 + 1)
                    V.scalar_tensor_tensor(out=nbias[:, t0:t0 + HALF], in0=mvg[:, t0:t0 + HALF, 0], scalar=-1.0,
                                           in1=rstd[:, t0:t0 + HALF], op0=ALU.mult, op1=ALU.mult).then_inc(s_rs, 1)

                half_stats(0, 0)
                half_stats(0, 1)
                with loop(dve, 1, NG - 1) as g:
                    for half in range(2):
                        half_stats(g, half)
                half_stats(NG - 1, 0)
                half_stats(NG - 1, 1, last=True)

            @block.scalar
            def _(act):
                def half_relu(g, half, wait_store):
                    t0 = half * HALF
                    act.wait_ge(s_agg, g * GROUP + t0 + HALF)
                    nc.scalar.activation(rstd[:, t0:t0 + HALF], mvg[:, t0:t0 + HALF, 1], ACT.Sqrt,
                                         bias=eps_c[:, 0:1]).then_inc(s_std, 1)
                    act.wait_ge(s_rs, g * 4 + half * 2 + 2)
                    if wait_store:
                        act.wait_ge(s_h0[half], 16 * g)
                    for j in range(HALF):
                        nc.scalar.activation(in_b[:, half, j, :], in_a[:, half, j, :], ACT.Relu,
                                             bias=nbias[:, t0 + j:t0 + j + 1],
                                             scale=rstd[:, t0 + j:t0 + j + 1]).then_inc(s_relu, 1)

                for half in range(2):
                    half_relu(0, half, False)
                with loop(act, 1, NG) as g:
                    for half in range(2):
                        half_relu(g, half, True)

        rounds = nc.values_load(rounds_i[0:1, 0:1], min_val=1, max_val=NT)

        def aggregate(name, table, gat):
            width = ROW if gat else D
            cols_in = AW if gat else D + 1
            s = {}

            def sm(n, count=None):
                s[n] = (stage_sem(f"agg_{n}") if count is None else
                        [stage_sem(f"agg_{n}{i}") for i in range(count)])

            for n in ("onehot", "sums", "added", "wz0", "base"):
                sm(n)
            sm("idx", SLOTS)
            s["rows"] = [sem(f"{name}_rows{i}") for i in range(SLOTS)]
            if gat:
                sm("tables", SLOTS)
                for n in ("el_cols", "el_rows", "fwd_local", "bwd_local", "tile_last", "tile_first", "tile_ends",
                          "carry_old", "carry_fwd", "carry_bwd", "carry_rows", "in_left", "in_right",
                          "fwd", "bwd", "seg_max", "e", "e_max", "leaky", "old_e", "old_leaky", "old_arg",
                          "arg", "weights", "w_cols", "r_row", "rm1", "r_cols", "rescale", "rescaled",
                          "scaled"):
                    sm(n)
            else:
                sm("self_in", SLOTS)
                sm("self_stored", SLOTS)
                for n in ("self_tr", "self_cp", "self_mm", "self_bias", "self_sum"):
                    sm(n)

            with nc.Block() as block:
                @block.vector
                def _(dve):
                    if not gat:
                        nc.vector.memset(slots[:, :, :, D:D + 1], 1.0)

                @block.gpsimd
                def _(pool):
                    pool.memset(carry[:, :], NEG)

            with nc.Fori(0, rounds) as rnd:
                with nc.Block() as block:
                    @block.sync
                    def _(sp):
                        n0 = sp.snap(rnd * NCH)
                        turn0 = [sp.snap(rnd * u) for u in USES]

                        def self_store(g, k):
                            n = SLOTS * g + k
                            sp.wait_ge(s["self_sum"], n0 + n + 1)
                            sp.dma_start(x1_tab[bass.ds(n * P, P), :], self_x[:, k, :]).then_inc(s["self_stored"][k], 16)

                        def self_load(g, k, peeled, last):
                            n = SLOTS * g + k
                            if not peeled:
                                self_store(g - 1, k)
                                sp.wait_ge(s["self_stored"][k], 16 * (turn0[k] + g))
                            if last:
                                sp.dma_start(self_x[0:LAST_ROWS, k, :], x[NODES - LAST_ROWS:NODES, :]).then_inc(s["self_in"][k], 16)
                            else:
                                sp.dma_start(self_x[:, k, :], x[bass.ds(n * P, P), :]).then_inc(s["self_in"][k], 16)
                            sp.dma_start(self_h[:, k, :], h0_tab[bass.ds(n * P, P), :]).then_inc(s["self_in"][k], 16)

                        def load(g, k, peeled, last=False):
                            n = SLOTS * g + k
                            if not peeled:
                                sp.wait_ge(s["sums"], QUADS * (n0 + n) - QUADS * SLOTS + 1)
                            sp.dma_start(idx[:, k, :], src_t[:, bass.ds(n * CT, CT)]).then_inc(s["idx"][k], 16)
                            if gat:
                                if not peeled:
                                    sp.wait_ge(s["weights"], n0 + n - (SLOTS - 1))
                                sp.dma_start(pen[:, k, :], pen_rows[bass.ds(n, 1), :, :, :]
                                             .rearrange("c h t p -> (c h t) p")).then_inc(s["tables"][k], 16)
                                sp.dma_start(er[:, k, :], er_rows[bass.ds(n, 1), :, :]
                                             .rearrange("c h (t p) -> (c h t) p", p=P)).then_inc(s["tables"][k], 16)
                                sp.dma_start(chain_pen[:, k, :], chain_tab[bass.ds(n, 1), :]
                                             .broadcast_to([HEADS, 2 * CT])).then_inc(s["tables"][k], 16)
                            else:
                                self_load(g, k, peeled, last)

                        for k in range(SLOTS):
                            load(0, k, True)
                        with loop(sp, 1, ITER) as g:
                            for k in range(SLOTS):
                                load(g, k, False)
                        for k in range(TAIL):
                            load(ITER, k, False, last=(k + 1 == TAIL))
                        if not gat:
                            for n in range(NCH - SLOTS, NCH):
                                self_store(n // SLOTS, n % SLOTS)
                            for k in range(SLOTS):
                                sp.wait_ge(s["self_stored"][k], 16 * (turn0[k] + USES[k]))
                            sp.sem_inc(sp_turn, 1)

                    @block.gpsimd
                    def _(pool):
                        turn0 = [pool.snap(rnd * u) for u in USES]
                        n0 = pool.snap(rnd * NCH)

                        def gather(g, k, peeled):
                            n = SLOTS * g + k
                            pool.wait_ge(s["idx"][k], 16 * (turn0[k] + g) + 16)
                            pool.sem_inc(pool_turn, 1)
                            for q in range(QUADS):
                                if not peeled:
                                    pool.wait_ge(s["sums"], QUADS * (n0 + n) - QUADS * SLOTS + q + 1)
                                    pool.sem_inc(pool_turn, 1)
                                for t in range(q * QT, q * QT + QT):
                                    pool.indirect_dma_start(
                                        slots[:, k, t, 0:width], None, table,
                                        bass.IndirectOffsetOnAxis(ap=idx[:, k, t:t + 1], axis=0),
                                    ).then_inc(s["rows"][k], 16)

                        for k in range(SLOTS):
                            gather(0, k, True)
                        with loop(pool, 1, ITER) as g:
                            for k in range(SLOTS):
                                gather(g, k, False)
                        for k in range(TAIL):
                            gather(ITER, k, False)

                    @block.scalar
                    def _(act):
                        n0 = act.snap(rnd * NCH)

                        def one_hot(g, k, q, free):
                            n = SLOTS * g + k
                            b = (QUADS * k + q) % SB
                            if free is None or free >= SB:
                                act.wait_ge(s["sums"], QUADS * (n0 + n) + q - SB + 1)
                            for t in range(QT):
                                col = n * CT + q * QT + t
                                nc.scalar.activation(onehot[:, b, t, :], lanes[:, :], ACT.Abs,
                                                     bias=negrel[:, bass.ds(col, 1)]).then_inc(s["wz0"], 1)
                            act.wait_ge(s["wz0"], CT * (n0 + n) + q * QT + QT)
                            nc.scalar.activation(onehot[:, b, :, :], onehot[:, b, :, :], ACT.Relu,
                                                 bias=one_c[:, 0:1], scale=-1.0).then_inc(s["onehot"], 1)

                        def weigh(n):
                            act.wait_ge(s["arg"], n + 1)
                            act.wait_ge(s["old_arg"], n + 1)
                            nc.scalar.activation(wrow[:, :], wexp[:, :], ACT.Exp).then_inc(s["weights"], 1)

                        def self_copy(n, first):
                            act.wait_ge(s["self_tr"], n + 1)
                            if not first:
                                act.wait_ge(s["self_mm"], n)
                            nc.scalar.activation(self_hT, ps_x[:, 0:D], ACT.Copy).then_inc(s["self_cp"], 1)

                        def chunk(g, k, nth=None, more=True):
                            n = SLOTS * g + k
                            g1, k1 = (g, k + 1) if k + 1 < SLOTS else (g + 1, 0)
                            free = (lambda i: None) if nth is None else (lambda i: nth * QUADS + i)
                            one_hot(g, k, 3, free(3))
                            if not gat:
                                self_copy(n0 + n, nth == 0)
                            if more:
                                one_hot(g1, k1, 0, free(4))
                                if gat:
                                    weigh(n0 + n + 1)
                                one_hot(g1, k1, 1, free(5))
                                one_hot(g1, k1, 2, free(6))

                        for q in range(3):
                            one_hot(0, 0, q, q)
                        if gat:
                            weigh(n0)
                        for k in range(SLOTS):
                            chunk(0, k, nth=k)
                        with loop(act, 1, ITER) as g:
                            for k in range(SLOTS):
                                chunk(g, k)
                        for k in range(TAIL):
                            chunk(ITER, k, more=(k + 1 < TAIL))

                    @block.tensor
                    def _(pe):
                        T = nc.tensor
                        n0 = pe.snap(rnd * NCH)
                        turn0 = [pe.snap(rnd * u) for u in USES]

                        def quad(g, k, q, nth, between=None):
                            n = SLOTS * g + k
                            qn = QUADS * (n0 + n) + q
                            b = (QUADS * k + q) % SB
                            pe.wait_ge(s["onehot"], qn + 1)
                            if gat:
                                pe.wait_ge(s["scaled"], qn + 1)
                            else:
                                pe.wait_ge(s["rows"][k], 16 * CT * g + 16 * CT)
                            if nth is None or nth * QUADS + q >= 2:
                                pe.wait_ge(s["added"], qn - 1)
                            for w in range(2):
                                if w and between:
                                    between()
                                for t in range(QT):
                                    last = T.matmul(pair[q % 2][:, w, 0:cols_in],
                                                    onehot[:, b, t, w * P:w * P + P],
                                                    slots[:, k, q * QT + t, 0:cols_in],
                                                    start=(t == 0), stop=(t == QT - 1))
                            last.then_inc(s["sums"], 1)

                        def self_transposes(g, k, n, first):
                            pe.wait_ge(s["self_in"][k], 32 * (turn0[k] + g) + 32)
                            if not first:
                                pe.wait_ge(s["self_cp"], n)
                            pe.sem_inc(pe_turn, 1)
                            for c in range(2):
                                last = T.transpose(ps_x[:, c * P:c * P + P], self_h[:, k, c * P:c * P + P],
                                                   ident[:, :])
                            last.then_inc(s["self_tr"], 1)

                        def self_products(n, first):
                            pe.wait_ge(s["self_cp"], n + 1)
                            if not first:
                                pe.wait_ge(s["self_sum"], n)
                            for c in range(2):
                                last = T.matmul(ps_w[:, 0:D], self_hT[:, c * P:c * P + P], wsT[:, c, :],
                                                start=(c == 0), stop=(c == 1))
                            last.then_inc(s["self_mm"], 1)

                        def el_rows(n):
                            pe.wait_ge(s["el_cols"], n + 1)
                            pe.sem_inc(pe_turn, 1)
                            T.transpose(ps_x[0:ROWS, 0:P], el_cols[:, :], ident[:, :]).then_inc(s["el_rows"], 1)

                        def tile_ends(n):
                            pe.wait_ge(s["tile_last"], n + 1)
                            pe.wait_ge(s["tile_first"], n + 1)
                            pe.sem_inc(pe_turn, 1)
                            T.matmul(ps_c[0:HEADS, 0:2 * CT], head_mask[:, :],
                                     ends[:, :, :].rearrange("p a t -> p (a t)"),
                                     start=True, stop=True).then_inc(s["tile_ends"], 1)

                        def carry_rows(n):
                            pe.wait_ge(s["carry_fwd"], n + 1)
                            pe.wait_ge(s["carry_bwd"], n + 1)
                            T.matmul(ps_c[0:ROWS, 64:64 + 2 * CT], head_rows[:, :],
                                     carry[:, :].rearrange("p (a t) -> p a t", a=2)[:, :, 0:CT],
                                     start=True, stop=True).then_inc(s["carry_rows"], 1)

                        def w_cols(n):
                            pe.wait_ge(s["weights"], n + 1)
                            pe.sem_inc(pe_turn, 1)
                            T.transpose(ps_w[:, 0:ROWS], wrow[:, 0:P], ident[0:ROWS, 0:ROWS]).then_inc(s["w_cols"], 1)
                            T.matmul(ps_c[0:1, 128:128 + HEADS], wrow[:, P:P + 1], first_rows[:, :],
                                     start=True, stop=True).then_inc(s["r_row"], 1)

                        def r_cols(k, n):
                            pe.wait_ge(s["rm1"], n + 1)
                            pe.wait_ge(s["onehot"], QUADS * n + 1)
                            T.matmul(ps_d[:, 0:HEADS], onehot[0:1, (QUADS * k) % SB, 0, 0:P], rm1[:, :],
                                     start=True, stop=True).then_inc(s["r_cols"], 1)

                        def chunk(g, k, nth=None, more=True):
                            n = n0 + SLOTS * g + k
                            g1, k1 = (g, k + 1) if k + 1 < SLOTS else (g + 1, 0)
                            more = more and gat
                            quad(g, k, 0, nth)
                            if not gat:
                                self_transposes(g, k, n, nth == 0)
                            if more:
                                el_rows(n + 1)
                            quad(g, k, 1, nth, (lambda: tile_ends(n + 1)) if more else None)
                            if more:
                                carry_rows(n + 1)
                            quad(g, k, 2, nth)
                            if not gat:
                                self_products(n, nth == 0)
                            quad(g, k, 3, nth, (lambda: w_cols(n + 1)) if more else None)
                            if more:
                                r_cols(k1, n + 1)

                        if gat:
                            el_rows(n0)
                            tile_ends(n0)
                            carry_rows(n0)
                            w_cols(n0)
                            r_cols(0, n0)
                        for k in range(SLOTS):
                            chunk(0, k, nth=k)
                        with loop(pe, 1, ITER) as g:
                            for k in range(SLOTS):
                                chunk(g, k)
                        for k in range(TAIL):
                            chunk(ITER, k, more=(k + 1 < TAIL))

                    @block.vector
                    def _(dve):
                        V = nc.vector
                        turn0 = [dve.snap(rnd * u) for u in USES]
                        n0 = dve.snap(rnd * NCH)

                        def add(g, k, q, first):
                            qn = QUADS * (n0 + SLOTS * g + k) + q
                            base = dve.value_load(base_row[0:1, bass.ds(QUADS * (SLOTS * g + k) + q, 1)],
                                                  min_val=0, max_val=NT)
                            dve.wait_ge(s["sums"], qn + 1)
                            if not (first and k == 0 and q == 0):
                                dve.wait_ge(s["added"], qn)
                            if gat and q == 0:
                                dve.wait_ge(s["rescaled"], n0 + SLOTS * g + k + 1)
                            to = accf[:, bass.ds(base * AW, 2 * AW)].rearrange("p (w c) -> p w c", w=2)[:, :, 0:cols_in]
                            V.tensor_tensor(to, to, pair[q % 2][:, :, 0:cols_in], ALU.add).then_inc(s["added"], 1)

                        def self_bias(g, k, n):
                            dve.wait_ge(s["self_in"][k], 32 * (turn0[k] + g) + 32)
                            V.tensor_tensor(self_x[:, k, :], self_x[:, k, :], bias[0][:, :],
                                            ALU.add).then_inc(s["self_bias"], 1)

                        def self_sum(k, n):
                            dve.wait_ge(s["self_bias"], n + 1)
                            dve.wait_ge(s["self_mm"], n + 1)
                            V.tensor_tensor(self_x[:, k, :], self_x[:, k, :], ps_w[:, 0:D],
                                            ALU.add).then_inc(s["self_sum"], 1)

                        def scans(k, left, right, out_f, out_b, done_f, done_b):
                            V.tensor_tensor_scan(out_f[:, :], pen[:, k, 0:P], ps_x[0:ROWS, 0:P], left,
                                                 ALU.add, ALU.max).then_inc(s[done_f], 1)
                            V.tensor_tensor_scan(out_b[:, P - 1::-1], pen[:, k, P:0:-1], ps_x[0:ROWS, P - 1::-1], right,
                                                 ALU.add, ALU.max).then_inc(s[done_b], 1)

                        def pack_el(g, k, n):
                            dve.wait_ge(s["rows"][k], 16 * CT * g + 16 * CT)
                            V.tensor_copy(el_cols[:, :].rearrange("p (h t) -> p h t", h=HEADS),
                                          slots[:, k, :, AW:AW + HEADS].rearrange("p t h -> p h t")
                                          ).then_inc(s["el_cols"], 1)

                        def local_maxima(g, k, n):
                            dve.wait_ge(s["el_rows"], n + 1)
                            dve.wait_ge(s["tables"][k], 48 * (turn0[k] + g) + 48)
                            scans(k, NEG, NEG, scan_f, scan_b, "fwd_local", "bwd_local")
                            dve.wait_ge(s["fwd_local"], n + 1)
                            V.tensor_scalar(ends[:, 0, :], tile_mask[:, :], scan_f[:, P - 1:P], None,
                                            ALU.mult).then_inc(s["tile_last"], 1)
                            dve.wait_ge(s["bwd_local"], n + 1)
                            V.tensor_scalar(ends[:, 1, :], tile_mask[:, :], scan_b[:, 0:1], None,
                                            ALU.mult).then_inc(s["tile_first"], 1)

                        def carries(k, n, peeled=False):
                            dve.wait_ge(s["tile_ends"], n + 1)
                            if not peeled:
                                dve.wait_ge(s["carry_fwd"], n)
                            V.tensor_copy(carry[:, 0:1], carry[:, CT:CT + 1]).then_inc(s["carry_old"], 1)
                            V.tensor_tensor_scan(carry[:, 2 * CT:CT:-1], chain_pen[:, k, 2 * CT - 1:CT - 1:-1],
                                                 ps_c[0:HEADS, 2 * CT - 1:CT - 1:-1], NEG,
                                                 ALU.add, ALU.max).then_inc(s["carry_bwd"], 1)
                            dve.wait_ge(s["carry_old"], n + 1)
                            V.tensor_tensor_scan(carry[:, 1:CT + 1], chain_pen[:, k, 0:CT], ps_c[0:HEADS, 0:CT],
                                                 carry[:, 0:1], ALU.add, ALU.max).then_inc(s["carry_fwd"], 1)

                        def exponents(k, n):
                            dve.wait_ge(s["carry_rows"], n + 1)
                            for side, done in ((0, "in_left"), (1, "in_right")):
                                V.tensor_tensor_reduce(out=scrap[:, side, :], in0=ps_c[0:ROWS, 64 + side * CT:64 + side * CT + CT],
                                                       in1=tile_mask[:, :], scale=1.0, scalar=0.0, op0=ALU.mult,
                                                       op1=ALU.add, accum_out=edge_in[:, side:side + 1]).then_inc(s[done], 1)
                            V.tensor_tensor(logit[:, 0, :], er[:, k, :], ps_x[0:ROWS, 0:P], ALU.add).then_inc(s["e"], 1)
                            dve.wait_ge(s["in_left"], n + 1)
                            dve.wait_ge(s["in_right"], n + 1)
                            scans(k, edge_in[:, 0:1], edge_in[:, 1:2], scan_f, scan_b, "fwd", "bwd")
                            V.tensor_tensor(old[:, 0:1], edge_in[:, 0:1], er[:, k, 0:1], ALU.add).then_inc(s["old_e"], 1)
                            dve.wait_ge(s["fwd"], n + 1)
                            dve.wait_ge(s["bwd"], n + 1)
                            V.tensor_tensor(scan_f[:, :], scan_f[:, :], scan_b[:, :], ALU.max).then_inc(s["seg_max"], 1)
                            dve.wait_ge(s["old_e"], n + 1)
                            V.scalar_tensor_tensor(out=old[:, 1:2], in0=old[:, 0:1], scalar=SLOPE, in1=old[:, 0:1],
                                                   op0=ALU.mult, op1=ALU.max).then_inc(s["old_leaky"], 1)
                            dve.wait_ge(s["seg_max"], n + 1)
                            V.tensor_tensor(logit[:, 1, :], scan_f[:, :], er[:, k, :], ALU.add).then_inc(s["e_max"], 1)
                            dve.wait_ge(s["e"], n + 1)
                            dve.wait_ge(s["e_max"], n + 1)
                            V.scalar_tensor_tensor(out=logit[:, :, :], in0=logit[:, :, :], scalar=SLOPE, in1=logit[:, :, :],
                                                   op0=ALU.mult, op1=ALU.max).then_inc(s["leaky"], 1)
                            dve.wait_ge(s["leaky"], n + 1)
                            V.tensor_tensor(wexp[:, 0:P], logit[:, 0, :], logit[:, 1, :], ALU.subtract).then_inc(s["arg"], 1)
                            dve.wait_ge(s["old_leaky"], n + 1)
                            V.tensor_scalar(wexp[:, P:P + 1], old[:, 1:2], logit[:, 1, 0:1], 0.0,
                                            ALU.subtract, ALU.min).then_inc(s["old_arg"], 1)

                        def scale(k, q, n):
                            dve.wait_ge(s["w_cols"], n + 1)
                            v = slots[:, k, q * QT:(q + 1) * QT, 0:AW].rearrange("p t (h d) -> p t h d", h=HEADS)
                            w = ps_w[:, 0:ROWS].rearrange("p (h t) -> p t h", h=HEADS)[:, q * QT:(q + 1) * QT, :]
                            V.tensor_tensor(v, v, w.unsqueeze(3).broadcast_to([P, QT, HEADS, HD + 1]),
                                            ALU.mult).then_inc(s["scaled"], 1)

                        def r_minus_1(n):
                            dve.wait_ge(s["r_row"], n + 1)
                            V.tensor_scalar(rm1[:, :], ps_c[0:1, 128:128 + HEADS], 1.0, None,
                                            ALU.subtract).then_inc(s["rm1"], 1)

                        def rescale_acc(g, k, n, peeled=False):
                            base = dve.value_load(base_row[0:1, bass.ds(QUADS * (SLOTS * g + k), 1)],
                                                  min_val=0, max_val=NT)
                            dve.wait_ge(s["r_cols"], n + 1)
                            V.tensor_scalar(rescale[:, :], ps_d[:, 0:HEADS], 1.0, None, ALU.add).then_inc(s["rescale"], 1)
                            dve.wait_ge(s["rescale"], n + 1)
                            if not peeled:
                                dve.wait_ge(s["added"], QUADS * n)
                            v = accf[:, bass.ds(base * AW, AW)].rearrange("p (h d) -> p h d", h=HEADS)
                            V.tensor_tensor(v, v, rescale[:, :].unsqueeze(2).broadcast_to([P, HEADS, HD + 1]),
                                            ALU.mult).then_inc(s["rescaled"], 1)

                        def chunk(g, k, more=True, first=False):
                            n = n0 + SLOTS * g + k
                            g1, k1 = (g, k + 1) if k + 1 < SLOTS else (g + 1, 0)
                            more = more and gat
                            if more:
                                pack_el(g1, k1, n + 1)
                            add(g, k, 0, first)
                            if more:
                                local_maxima(g1, k1, n + 1)
                                carries(k1, n + 1)
                            add(g, k, 1, first)
                            if more:
                                exponents(k1, n + 1)
                            if not gat:
                                self_bias(g, k, n)
                            add(g, k, 2, first)
                            if not gat:
                                self_sum(k, n)
                            if more:
                                scale(k1, 0, n + 1)
                                r_minus_1(n + 1)
                                scale(k1, 1, n + 1)
                            add(g, k, 3, first)
                            if more:
                                scale(k1, 2, n + 1)
                                scale(k1, 3, n + 1)
                                rescale_acc(g1, k1, n + 1)

                        if gat:
                            pack_el(0, 0, n0)
                            local_maxima(0, 0, n0)
                            carries(0, n0, peeled=True)
                            exponents(0, n0)
                            for q in range(QUADS):
                                scale(0, q, n0)
                            r_minus_1(n0)
                            rescale_acc(0, 0, n0, peeled=True)
                        for k in range(SLOTS):
                            chunk(0, k, first=True)
                        with loop(dve, 1, ITER) as g:
                            for k in range(SLOTS):
                                chunk(g, k)
                        for k in range(TAIL):
                            chunk(ITER, k, more=(k + 1 < TAIL))

                with nc.Block() as block:
                    @block.vector
                    def _(dve):
                        V = nc.vector
                        b0_ = s["base"]
                        row_f = in_a[0:1, 0, 0:2, :].rearrange("p t d -> p (t d)")[:, 0:NCH * QUADS]
                        V.tensor_scalar(lanes[:, :], lanes[:, :], float(WIN), None, ALU.add)
                        V.tensor_copy(row_f, base_row[:, :]).then_inc(b0_, 1)
                        dve.wait_ge(b0_, 3 * rnd + 1)
                        V.tensor_scalar(row_f, row_f, 2.0, float(NT), ALU.add, ALU.min).then_inc(b0_, 1)
                        dve.wait_ge(b0_, 3 * rnd + 2)
                        V.tensor_copy(base_row[:, :], row_f).then_inc(b0_, 1)

                    @block.gpsimd
                    def _(pool):
                        pool.memset(carry[:, :], NEG)
                        pool.inc_swdge_sem(s["rows"], [16 * CT * u for u in USES], mode="sub")

            clear_stage_sems()
            s_back = sem(f"{name}_back")
            with nc.Block() as block:
                @block.gpsimd
                def _(pool):
                    pool.iota(lane_i, [[1, WIN]], base=0, channel_multiplier=0).then_inc(s_back, 1)
                    pool.wait_ge(s_back, 1)
                    pool.tensor_copy(lanes[:, :], lane_i)

                @block.sync
                def _(sp):
                    sp.dma_start(base_row[:, :], base_tab.rearrange("c q -> (c q)").unsqueeze(0)).then_inc(s_back_d, 16)
                    sp.wait_ge(s_back_d, 16 * back_count[0])

        s_back_d = sem("s_back_d")
        back_count = [1]

        aggregate("sage", h0_tab, False)

        s_deg = sem("s_deg")
        s_cum = sem("s_cum")
        pos_f = tmp_a[:, 0, 0:NT]
        tot_f = tmp_b[:, 0, 0:NT]
        cum_f = tmp_b[:, 1, 0:NT]
        zer_f = tmp_a[:, 1, 0:NT]
        with nc.Block() as block:
            @block.vector
            def _(dve):
                V = nc.vector
                n = [0]

                def then(ins):
                    n[0] += 1
                    ins.then_inc(s_deg, 1)
                    dve.wait_ge(s_deg, n[0])

                V.memset(zer_f, 0.0)
                then(V.tensor_copy(deg[:, :], accf.rearrange("p (t c) -> p t c", c=AW)[:, 0:NT, D]))
                then(V.tensor_scalar(deg_inv[:, :], deg[:, :], 1.0, None, ALU.max))
                then(V.reciprocal(deg_inv[:, :], deg_inv[:, :]))
                dve.wait_ge(s_cum, 2)
                then(V.tensor_copy(tot_f, ps_w[:, 0:NT]))
                then(V.tensor_tensor_scan(cum_f, zer_f, tot_f, 0.0, ALU.add, ALU.add))
                then(V.tensor_tensor(cum_f, cum_f, tot_f, ALU.subtract))
                then(V.tensor_tensor(pos_f, cum_f, ps_x[:, 0:NT], ALU.add))
                then(V.tensor_scalar(tot_f, deg[:, :], 0.0, float(NOWHERE), ALU.is_equal, ALU.mult))
                then(V.tensor_tensor(pos_f, pos_f, tot_f, ALU.max))
                then(V.tensor_copy(seg_pos[:, :], pos_f))

            @block.tensor
            def _(pe):
                pe.wait_ge(s_deg, 1)
                nc.tensor.matmul(ps_x[:, 0:NT], before[:, :], deg[:, :], start=True, stop=True).then_inc(s_cum, 1)
                nc.tensor.matmul(ps_w[:, 0:NT], ones[:, :], deg[:, :], start=True, stop=True).then_inc(s_cum, 1)

        s_in = [sem(f"s_in{i}") for i in range(2)]
        s_mean = sem("s_mean")
        s_tr = sem("s_tr")
        s_cp = sem("s_cp")
        s_mm = sem("s_mm")
        s_x1 = sem("s_x1")
        s_st = sem("s_st")
        s_ag = sem("s_ag")
        s_mv = sem("s_mv")
        s_x1o = [sem(f"s_x1o{i}") for i in range(2)]

        with nc.Block() as block:
            @block.sync
            def _(sp):
                def load(g, half, peeled=False):
                    if not peeled:
                        sp.wait_ge(s_x1o[half], 16 * g)
                    half_load(sp, x1_tab, in_a, g, half, s_in[half], False)

                def store(g, half):
                    sp.wait_ge(s_x1, g * GROUP + half * HALF + HALF)
                    sp.wait_ge(s_st, g * GROUP + half * HALF + HALF)
                    sp.dma_start(store_rows(x1_tab, g, half), in_a[:, half, :, :]).then_inc(s_x1o[half], 16)

                load(0, 0, peeled=True)
                load(0, 1, peeled=True)
                with loop(sp, 0, NG - 1) as g:
                    for half in range(2):
                        store(g, half)
                        load(g + 1, half)
                store(NG - 1, 0)
                store(NG - 1, 1)
                sp.wait_ge(s_x1o[0], 16 * NG)
                sp.wait_ge(s_x1o[1], 16 * NG)

            @block.vector
            def _(dve):
                V = nc.vector

                def mean(g, j, first):
                    if not (first and j < 2):
                        dve.wait_ge(s_tr, g * GROUP + j - 1)
                    V.tensor_scalar(tmp_b[:, j % 2, :], acc_cols(g * GROUP + j, 0, D), deg_inv[:, bass.ds(g * GROUP + j, 1)], None, ALU.mult).then_inc(s_mean, 1)

                def finish(g, j):
                    t = g * GROUP + j
                    v = in_a[:, j // HALF, j % HALF, :]
                    dve.wait_ge(s_mm, t + 1)
                    V.tensor_tensor(v, v, ps_w[:, 0:D] if j % 2 else ps_d[:, 0:D], ALU.add).then_inc(s_x1, 1)
                    dve.wait_ge(s_x1, t + 1)
                    V.bn_stats(stats[:, j, :], v).then_inc(s_st, 1)

                def aggregate_stats(g):
                    dve.wait_ge(s_st, g * GROUP + GROUP)
                    dve.sem_inc(dve_turn, 1)
                    for j in range(GROUP):
                        V.bn_aggr(mvg[:, j, :], stats[:, j, :]).then_inc(s_ag, 1)
                    dve.wait_ge(s_ag, g * GROUP + GROUP)
                    V.tensor_copy(mv[:, bass.ds(g * GROUP, GROUP), :], mvg[:, :, :]).then_inc(s_mv, 1)

                mean(0, 0, True)
                mean(0, 1, True)

                def group(g, first, last=False):
                    for j in range(GROUP):
                        if j == 0 or j == HALF:
                            dve.wait_ge(s_in[j // HALF], 16 * g + 16)
                        if not (last and j >= GROUP - 2):
                            mean(*((g, j + 2) if j + 2 < GROUP else (g + 1, j + 2 - GROUP)), False)
                        finish(g, j)
                    aggregate_stats(g)
                    dve.wait_ge(s_mv, g + 1)

                group(0, True)
                with loop(dve, 1, NG - 1) as g:
                    group(g, False)
                group(NG - 1, False, last=True)

            @block.tensor
            def _(pe):
                T = nc.tensor

                def transposes(g, j, first):
                    t = g * GROUP + j
                    pe.wait_ge(s_mean, t + 1)
                    if not (first and j < 2):
                        pe.wait_ge(s_cp, t - 1)
                    to = pair[j % 2][:, 0, :]
                    for c in range(2):
                        last = T.transpose(to[:, c * P:c * P + P], tmp_b[:, j % 2, c * P:c * P + P], ident[:, :])
                    last.then_inc(s_tr, 1)

                def products(g, j, first):
                    t = g * GROUP + j
                    pe.wait_ge(s_cp, t + 1)
                    if not (first and j < 2):
                        pe.wait_ge(s_x1, t - 1)
                    to = ps_w if j % 2 else ps_d
                    for c in range(2):
                        last = T.matmul(to[:, 0:D], lhs[:, j % 2, c * P:c * P + P], wnT[:, c, :],
                                        start=(c == 0), stop=(c == 1))
                    last.then_inc(s_mm, 1)

                def group(g, first, last=False):
                    for j in range(GROUP):
                        nxt = (g, j + 1) if j + 1 < GROUP else (g + 1, 0)
                        if not (last and j == GROUP - 1):
                            transposes(*nxt, first and j + 1 < GROUP)
                        products(g, j, first)

                transposes(0, 0, True)
                group(0, True)
                with loop(pe, 1, NG - 1) as g:
                    group(g, False)
                group(NG - 1, False, last=True)

            @block.scalar
            def _(act):
                def copies(g, first):
                    for j in range(GROUP):
                        t = g * GROUP + j
                        act.wait_ge(s_tr, t + 1)
                        if not (first and j < 2):
                            act.wait_ge(s_mm, t - 1)
                        nc.scalar.activation(lhs[:, j % 2, 0:D], pair[j % 2][:, 0, 0:D], ACT.Copy).then_inc(s_cp, 1)

                copies(0, True)
                with loop(act, 1, NG) as g:
                    copies(g, False)

        s_sq = sem("s_sq")
        with nc.Block() as block:
            @block.scalar
            def _(act):
                nc.scalar.activation(rstd[:, :], mv[:, :, 1], ACT.Sqrt, bias=eps_c[:, 0:1]).then_inc(s_sq, 1)

            @block.vector
            def _(dve):
                dve.wait_ge(s_sq, 1)
                nc.vector.reciprocal(rstd[:, :], rstd[:, :]).then_inc(s_sq, 1)
                dve.wait_ge(s_sq, 2)
                nc.vector.scalar_tensor_tensor(out=nbias[:, :], in0=mv[:, :, 0], scalar=-1.0, in1=rstd[:, :],
                                               op0=ALU.mult, op1=ALU.mult)
                nc.vector.memset(z_out, 1.0)

        def node_stage(name, norm, layer, final):
            s = {n: stage_sem(f"node_{n}") for n in
                 ("h", "tr", "cp", "mm", "z", "zel", "zer", "den", "rec", "div", "res", "bias", "neg", "exp",
                  "elu", "pos")}
            s["scat"] = [sem(f"{name}_scat{i}") for i in range(2)]
            s_load = [stage_sem(f"node_load{i}") for i in range(2)]
            s_x1l = [stage_sem(f"node_x1load{i}") for i in range(2)]
            s_hout = [stage_sem(f"node_hout{i}") for i in range(2)]
            s_zout = [stage_sem(f"node_zout{i}") for i in range(2)]
            z_w = None if final else wz[layer]
            ahead = 3
            elu_ahead = ahead - 2 if final else ahead - 1
            depth = HALF if final else 2
            a_buf = flat[:, 4 * H:5 * H].rearrange("p (s c) -> p s c", s=HALF) if final else tmp_a
            e_buf = flat[:, 5 * H:6 * H].rearrange("p (s c) -> p s c", s=HALF) if final else tmp_b

            def next_tile(g, j, n=1):
                return (g, j + n) if j + n < GROUP else (g + 1, j + n - GROUP)

            def last_tile(g, j):
                return (g, j - 1) if j else (g - 1, GROUP - 1)

            def lhs_copy(eng, g, j, first):
                t = g * GROUP + j
                eng.wait_ge(s["tr"], t + 1)
                if not (first and j < 2):
                    eng.wait_ge(s["mm"], t - 1)
                to, of = lhs[:, j % 2, 0:D], pair[j % 2][:, 0, 0:D]
                (nc.vector.tensor_copy(to, of) if norm else
                 nc.scalar.activation(to, of, ACT.Copy)).then_inc(s["cp"], 1)

            if not norm:
                with nc.Block() as block:
                    @block.vector
                    def _(dve):
                        sums = accf.rearrange("p (t h d) -> p t h d", h=HEADS, d=HD + 1)[:, 0:NT, :, HD]
                        inv = w_inv[:, :].rearrange("p (t h) -> p t h", h=HEADS)
                        nc.vector.tensor_scalar(inv, sums, 1e-30, None, ALU.max).then_inc(s["den"], 1)
                        dve.wait_ge(s["den"], 1)
                        nc.vector.reciprocal(w_inv[:, :], w_inv[:, :])

            with nc.Block() as block:
                @block.sync
                def _(sp):
                    def load(g, half):
                        half_load(sp, x1_tab if norm else hin_tab, in_a, g, half, s_load[half], False)

                    def load_x1(g, half):
                        if final:
                            half_load(sp, x1_tab, in_b, g, half, s_x1l[half], False)

                    def store(g, half, last=False):
                        if not last:
                            sp.wait_ge(s["h"] if norm else s["res"], g * GROUP + half * HALF + HALF)
                            load(g + 1, half)
                        sp.wait_ge(s["h"], g * GROUP + half * HALF + HALF)
                        v = accf[:, bass.ds((g * 2 + half) * HALF * AW, HALF * AW)]
                        v = v.rearrange("p (t c) -> p t c", c=AW)[:, :, 0:D]
                        if not final:
                            sp.dma_start(store_rows(hin_tab, g, half), in_b[:, half, :, :]).then_inc(s_hout[half], 16)
                            sp.wait_ge(s["zel"], g * GROUP + half * HALF + HALF)
                            sp.wait_ge(s["z"], g * GROUP + half * HALF + HALF)
                            sp.dma_start(store_rows(z_tab, g, half), z_out[:, half, :, :]).then_inc(s_zout[half], 16)
                        elif not last:
                            sp.dma_start(store_rows(out, g, half), v).then_inc(s_hout[half], 16)
                            load_x1(g + 1, half)
                        elif half == 0:
                            sp.dma_start(store_rows(out, g, half), v).then_inc(s_hout[half], 16)
                        else:
                            full, n = (NT - HALF) * P, (HALF - 1) * P
                            sp.dma_start(out[full:full + n, :].rearrange("(t p) d -> p t d", p=P),
                                         v[:, 0:HALF - 1, :]).then_inc(s_hout[half], 16)
                            sp.dma_start(out[full + n:NODES, :], v[0:LAST_ROWS, HALF - 1, :]).then_inc(s_hout[half], 16)

                    for half in range(2):
                        load(0, half)
                        load_x1(0, half)
                    with loop(sp, 0, NG - 1) as g:
                        for half in range(2):
                            store(g, half)
                    store(NG - 1, 0, last=True)
                    store(NG - 1, 1, last=True)
                    sp.wait_ge(s_hout[0], 16 * NG)
                    sp.wait_ge(s_hout[1], 16 * NG + (16 if final else 0))
                    if not final:
                        sp.wait_ge(s_zout[0], 16 * NG)
                        sp.wait_ge(s_zout[1], 16 * NG)

                @block.scalar
                def _(act):
                    def tile(g, j, first):
                        t = g * GROUP + j
                        if norm:
                            if not first and j % HALF == 0:
                                act.wait_ge(s_hout[j // HALF], 16 * g)
                            if j % HALF == 0:
                                act.wait_ge(s_load[j // HALF], 16 * (g + 1))
                            nc.scalar.activation(in_b[:, j // HALF, j % HALF, :],
                                                 in_a[:, j // HALF, j % HALF, :], ACT.Relu, bias=nbias[:, bass.ds(t, 1)],
                                                 scale=rstd[:, bass.ds(t, 1)]).then_inc(s["h"], 1)
                        elif final:
                            act.wait_ge(s["res"], t + 1)
                            nc.scalar.activation(e_buf[:, j % depth, :], a_buf[:, j % depth, :], ACT.Relu,
                                                 scale=-1.0).then_inc(s["neg"], 1)
                            act.wait_ge(s["neg"], t + 1)
                            nc.scalar.activation(e_buf[:, j % depth, :], e_buf[:, j % depth, :], ACT.Exp,
                                                 scale=-1.0).then_inc(s["exp"], 1)
                        else:
                            act.wait_ge(s["neg"], t + 1)
                            nc.scalar.activation(e_buf[:, j % 2, :], e_buf[:, j % 2, :], ACT.Exp).then_inc(s["exp"], 1)

                    def z_copy(g, j, first):
                        t = g * GROUP + j
                        act.wait_ge(s["mm"], t + 1)
                        if not first:
                            act.wait_ge(s_zout[j // HALF], 16 * g)
                        zp = ps_w if j % 2 else ps_d
                        to = z_out[:, j // HALF, j % HALF, 0:AW].rearrange("p (h d) -> p h d", h=HEADS)[:, :, 0:HD]
                        nc.scalar.activation(to, zp[:, 0:D].rearrange("p (h d) -> p h d", h=HEADS),
                                             ACT.Copy).then_inc(s["z"], 1)

                    def group(g, first, last=False, second=False):
                        for j in range(GROUP):
                            if not final:
                                if not norm and not (last and j == GROUP - 1):
                                    lhs_copy(act, *next_tile(g, j), first and j + 1 < GROUP)
                                if not (first and j == 0):
                                    z_copy(*last_tile(g, j), first or (second and j == 0))
                            if not (last and j >= GROUP - ahead):
                                tile(*next_tile(g, j, ahead), first and j + ahead < GROUP)

                    for j in range(ahead):
                        tile(0, j, True)
                    if not norm and not final:
                        lhs_copy(act, 0, 0, True)
                    group(0, True)
                    group(1, False, second=True)
                    with loop(act, 2, NG - 1) as g:
                        group(g, False)
                    group(NG - 1, False, last=True)
                    if not final:
                        z_copy(NG - 1, GROUP - 1, False)

                @block.vector
                def _(dve):
                    V = nc.vector

                    def divided(g, j, first):
                        t = g * GROUP + j
                        v = acc_cols(t, 0, AW).rearrange("p (h d) -> p h d", h=HEADS)
                        if not (first and j < depth):
                            dve.wait_ge(s["elu"] if final else s["h"], t - depth + 1)
                        V.tensor_tensor(a_buf[:, j % depth, :].rearrange("p (h d) -> p h d", h=HEADS), v[:, :, 0:HD],
                                        w_inv[:, bass.ds(t * HEADS, HEADS)].unsqueeze(2)
                                        .broadcast_to([P, HEADS, HD]),
                                        ALU.mult).then_inc(s["div"], 1)

                    def residual(g, j):
                        t = g * GROUP + j
                        a = a_buf[:, j % depth, :]
                        if j == 0 or j == HALF:
                            dve.wait_ge(s["bias"], 2 * g + j // HALF + 1)
                        dve.wait_ge(s["div"], t + 1)
                        V.tensor_tensor(a, a, in_a[:, j // HALF, j % HALF, :], ALU.add).then_inc(s["res"], 1)

                    def negative(g, j):
                        t = g * GROUP + j
                        dve.wait_ge(s["res"], t + 1)
                        V.tensor_scalar(e_buf[:, j % depth, :], a_buf[:, j % depth, :], 0.0, None,
                                        ALU.min).then_inc(s["neg"], 1)

                    def elu(g, j, first):
                        t = g * GROUP + j
                        dve.wait_ge(s["exp"], t + 1)
                        if not final and not first and j % HALF == 0:
                            dve.wait_ge(s_hout[j // HALF], 16 * g)
                        to = acc_cols(t, 0, D) if final else in_b[:, j // HALF, j % HALF, :]
                        V.scalar_tensor_tensor(out=to, in0=e_buf[:, j % depth, :], scalar=-1.0,
                                               in1=a_buf[:, j % depth, :], op0=ALU.add,
                                               op1=ALU.max).then_inc(s["elu"] if final else s["h"], 1)

                    def with_x1(g, j):
                        t = g * GROUP + j
                        if j % HALF == 0:
                            dve.wait_ge(s_x1l[j // HALF], 16 * (g + 1))
                        dve.wait_ge(s["elu"], t + 1)
                        to = acc_cols(t, 0, D)
                        V.tensor_tensor(to, to, in_b[:, j // HALF, j % HALF, :], ALU.add).then_inc(s["h"], 1)

                    def tails(g, j, first):
                        t = g * GROUP + j
                        dve.wait_ge(s["mm"], t + 1)
                        dve.wait_ge(s["z"], t + 1)
                        if not first:
                            dve.wait_ge(s_zout[j // HALF], 16 * g)
                            if j % HALF == 0:
                                dve.wait_ge(s["scat"][j // HALF], 16 * HALF * g)
                        if j % HALF == 0:
                            V.tensor_copy(pos_stage[:, j:j + HALF],
                                          seg_pos[:, bass.ds(g * GROUP + j, HALF)]).then_inc(s["pos"], 1)
                        zp = ps_w if j % 2 else ps_d
                        V.tensor_copy(z_out[:, j // HALF, j % HALF, AW:ROW], zp[:, D:D + 2 * HEADS]).then_inc(s["zel"], 1)
                        V.tensor_copy(er_stage[:, j, :], zp[:, D + HEADS:D + 2 * HEADS]).then_inc(s["zer"], 1)

                    def group(g, first, last=False, second=False):
                        for j in range(GROUP):
                            if not norm:
                                if not (last and j >= GROUP - ahead):
                                    divided(*next_tile(g, j, ahead), first and j + ahead < GROUP)
                                if not (last and j >= GROUP - elu_ahead):
                                    elu(*next_tile(g, j, elu_ahead), first and j + elu_ahead < GROUP)
                                if not (last and j >= GROUP - ahead):
                                    residual(*next_tile(g, j, ahead))
                                if final and not (last and j >= GROUP - elu_ahead):
                                    with_x1(*next_tile(g, j, elu_ahead))
                            if not final:
                                if norm and not (last and j == GROUP - 1):
                                    lhs_copy(dve, *next_tile(g, j), first and j + 1 < GROUP)
                                if not (first and j == 0):
                                    tails(*last_tile(g, j), first or (second and j == 0))
                            if not norm and not final and not (last and j >= GROUP - ahead):
                                negative(*next_tile(g, j, ahead))

                    if norm:
                        lhs_copy(dve, 0, 0, True)
                    else:
                        for j in range(ahead):
                            divided(0, j, True)
                            if j and not final:
                                elu(0, j - 1, True)
                            residual(0, j)
                            if not final:
                                negative(0, j)
                        if final:
                            elu(0, 0, True)
                            with_x1(0, 0)
                    group(0, True)
                    group(1, False, second=True)
                    with loop(dve, 2, NG - 1) as g:
                        group(g, False)
                    group(NG - 1, False, last=True)
                    if not final:
                        tails(NG - 1, GROUP - 1, False)

                def add_bias(pool, g, half):
                    pool.wait_ge(s_load[half], 16 * (g + 1))
                    v = in_a[:, half, :, :]
                    pool.tensor_tensor(v, v, bias[2 if final else layer][:, :].unsqueeze(1)
                                       .broadcast_to([P, HALF, D]), ALU.add).then_inc(s["bias"], 1)

                if final:
                    @block.gpsimd
                    def _(pool):
                        with loop(pool, 0, NG) as g:
                            for half in range(2):
                                add_bias(pool, g, half)

                if not final:
                    @block.tensor
                    def _(pe):
                        T = nc.tensor

                        def transposes(g, j, first):
                            t = g * GROUP + j
                            pe.wait_ge(s["h"], t + 1)
                            if not (first and j < 2):
                                pe.wait_ge(s["cp"], t - 1)
                            for c in range(2):
                                last = T.transpose(pair[j % 2][:, 0, c * P:c * P + P],
                                                   in_b[:, j // HALF, j % HALF, c * P:c * P + P], ident[:, :])
                            last.then_inc(s["tr"], 1)

                        def products(g, j, first):
                            t = g * GROUP + j
                            pe.wait_ge(s["cp"], t + 1)
                            if not (first and j < 2):
                                pe.wait_ge(s["zer"], t - 1)
                            zp = ps_w if j % 2 else ps_d
                            for c in range(2):
                                last = T.matmul(zp[:, 0:D + 2 * HEADS], lhs[:, j % 2, c * P:c * P + P], z_w[:, c, :],
                                                start=(c == 0), stop=(c == 1))
                            last.then_inc(s["mm"], 1)

                        def group(g, first, last=False):
                            for j in range(GROUP):
                                if not (last and j == GROUP - 1):
                                    transposes(*next_tile(g, j), first and j + 1 < GROUP)
                                products(g, j, first)

                        transposes(0, 0, True)
                        group(0, True)
                        with loop(pe, 1, NG - 1) as g:
                            group(g, False)
                        group(NG - 1, False, last=True)

                    @block.gpsimd
                    def _(pool):
                        def scatter(g, half):
                            pool.wait_ge(s["pos"], 2 * g + half + 1)
                            pool.wait_ge(s["zer"], g * GROUP + half * HALF + HALF)
                            pool.sem_inc(pool_turn, 1)
                            for j in range(half * HALF, half * HALF + HALF):
                                pool.indirect_dma_start(
                                    er_start, bass.IndirectOffsetOnAxis(ap=pos_stage[:, j:j + 1], axis=0),
                                    er_stage[:, j, :], None, bounds_check=EPAD - 1,
                                    oob_is_err=False).then_inc(s["scat"][half], 16)

                        if not norm:
                            add_bias(pool, 0, 0)
                            add_bias(pool, 0, 1)
                        with loop(pool, 0, NG - 1) as g:
                            for half in range(2):
                                if not norm:
                                    add_bias(pool, g + 1, half)
                                scatter(g, half)
                        for half in range(2):
                            scatter(NG - 1, half)
                        for half in range(2):
                            pool.wait_ge(s["scat"][half], 16 * HALF * NG)

            clear_stage_sems()

        val = flat[0:NCH, 0:CE * HEADS]
        same = flat[0:NCH, CE * HEADS:CE * HEADS + CE]
        filled = [flat[0:NCH, CE * HEADS + CE:CE * HEADS + 2 * CE], hot[0:NCH, 0:CE]]

        def spread_er(name):
            cut = ACC_TILES // 3 * AW
            s_l = sem(f"{name}_load")
            s_g = sem(f"{name}_first")
            s_f = sem(f"{name}_filled")
            s_o = [sem(f"{name}_out{i}") for i in range(2)]
            with nc.Block() as block:
                @block.sync
                def _(sp):
                    sp.dma_start(val, er_start.rearrange("(c e) h -> c (e h)", e=CE)).then_inc(s_l, 16)
                    sp.dma_start(same, same_tab).then_inc(s_l, 16)
                    for h in range(HEADS):
                        sp.wait_ge(s_f, h + 1)
                        sp.dma_start(er_rows[:, h, :], filled[h % 2]).then_inc(s_o[h % 2], 16)
                    for i in range(2):
                        sp.wait_ge(s_o[i], 16 * HEADS // 2)

                @block.gpsimd
                def _(pool):
                    pool.indirect_dma_start(er_init[:, :], None, z_tab,
                                            bass.IndirectOffsetOnAxis(ap=first_dst[:, 0:1], axis=0)).then_inc(s_g, 16)
                    pool.memset(accf[:, cut:], 0.0)

                @block.vector
                def _(dve):
                    nc.vector.memset(accf[:, 0:cut], 0.0)
                    dve.wait_ge(s_l, 32)
                    dve.wait_ge(s_g, 16)
                    for h in range(HEADS):
                        if h >= 2:
                            dve.wait_ge(s_o[h % 2], 16)
                        nc.vector.tensor_tensor_scan(filled[h % 2], same, val[:, h:CE * HEADS:HEADS],
                                                     er_init[:, AW + HEADS + h:AW + HEADS + h + 1],
                                                     ALU.mult, ALU.add).then_inc(s_f, 1)

        back_count[0] = 2
        node_stage("norm", True, 0, False)
        spread_er("fill0")
        aggregate("gat0", z_tab, True)
        s_ones = sem("s_ones")
        with nc.Block() as block:
            @block.vector
            def _(dve):
                nc.vector.memset(z_out, 1.0).then_inc(s_ones, 1)

        back_count[0] = 3
        node_stage("mid", False, 1, False)
        spread_er("fill1")
        aggregate("gat1", z_tab, True)
        node_stage("last", False, 1, True)


_INS = ["x", "src", "dst", "L0_gnn_W_neigh", "L0_gnn_W_self", "L0_gnn_b_self",
        "L1_gnn_W0", "L1_gnn_al0", "L1_gnn_ar0", "L1_gnn_b0",
        "L1_gnn_W1", "L1_gnn_al1", "L1_gnn_ar1", "L1_gnn_b1"]


def kernel(**inputs):
    import numpy as np
    import concourse.bacc as bacc
    from concourse.bass_utils import run_bass_kernel_spmd

    nc = bacc.Bacc("TRN2", target_bir_lowering=False, num_devices=1)
    arrays, args = {}, []
    for name in _INS:
        a = np.ascontiguousarray(inputs[name])
        arrays[f"in_{name}"] = a
        args.append(nc.dram_tensor(f"in_{name}", a.shape, mybir.dt.from_np(a.dtype), kind="ExternalInput").ap())
    args.append(nc.dram_tensor("out", (NODES, D), F32, kind="ExternalOutput").ap())
    gnn_kernel(nc, *args)
    r = run_bass_kernel_spmd(nc, [arrays], core_ids=[0])
    return r.results[0]["out"]
```
